# Optimizing a Trainium2 kernel written in Bass

```python
import numpy as np
import jax
import jax.numpy as jnp

def _softmax(x, axis=-1):
    return jax.nn.softmax(x, axis=axis)

def _gelu(x):
    return jax.nn.gelu(x, approximate=True)

def _silu(x):
    return jax.nn.silu(x)

def _sigmoid(x):
    return jax.nn.sigmoid(x)

def _layernorm(x, axis=-1, eps=1e-05):
    m = jnp.mean(x, axis=axis, keepdims=True)
    v = jnp.var(x, axis=axis, keepdims=True)
    return (x - m) / jnp.sqrt(v + eps)

def _scatter_add(tgt, idx, src, axis=0):
    return tgt.at[idx].add(src)

def _segment_sum(src, seg, n):
    return jax.ops.segment_sum(src, seg, n)
kernel_name = 'mk_vit_tower_d2_tok_img1024_r4_b76f5e'

def setup_inputs(seed: int=0):
    np.random.seed(seed)
    _w = jnp.asarray

    def _rec_inputs():
        import jax
        import jax.numpy as jnp
        _rk = jax.random.key(seed)
        x = -0.00016672 + 0.999947 * jax.random.normal(jax.random.fold_in(_rk, 1), (64, 3, 96, 96), jnp.float32)
        return x
    x = _rec_inputs()

    def _L0_tok_setup():
        import jax, jax.numpy as jnp
        import numpy as np
        B, C, H, W = (64, 3, 96, 96)
        P = 16
        HP, WP = (H // P, W // P)
        N = HP * WP
        F = C * P * P
        D = 256
        key = jax.random.key(seed)
        k1, k2, k3, k4, k5 = jax.random.split(key, 5)
        data = jax.random.normal(k1, (B, C, H, W), dtype=jnp.float32)
        lim = 1.0 / np.sqrt(F)
        W_lin = jax.random.uniform(k2, (D, F), minval=-lim, maxval=lim, dtype=jnp.float32)
        b_lin = jax.random.uniform(k3, (D,), minval=-lim, maxval=lim, dtype=jnp.float32)
        class_token = jax.random.normal(k4, (1, 1, D), dtype=jnp.float32)
        position_embeddings = jax.random.normal(k5, (1, N + 1, D), dtype=jnp.float32)
        return {'data': data, 'W_lin': W_lin, 'b_lin': b_lin, 'class_token': class_token, 'position_embeddings': position_embeddings}
    _L0_tok_all = _L0_tok_setup()
    _L0_tok_in = {k: v for k, v in _L0_tok_all.items() if k in ('W_lin', 'b_lin', 'class_token', 'position_embeddings')}
    del _L0_tok_all

    def _L0_attn_setup():
        import jax, jax.numpy as jnp
        import numpy as np
        B, L, R = (4, 512, 256)
        HID, EXP, K = (64, 2, 3)
        D = HID * EXP
        N = HID
        key = jax.random.key(seed)
        ks = jax.random.split(key, 16)
        g = lambda k, s: jax.random.normal(k, s, dtype=jnp.float32) * 0.02
        inp = {'up_x': jax.random.normal(ks[0], (B, L, R), dtype=jnp.float32), 'W_up': g(ks[1], (R, 2 * D)), 'b_up': g(ks[2], (2 * D,)), 'conv_w': g(ks[3], (D, K)), 'conv_b': g(ks[4], (D,)), 'W_delta': g(ks[5], (D, D)), 'b_delta': g(ks[6], (D,)), 'W_B': g(ks[7], (D, N)), 'b_B': g(ks[8], (N,)), 'W_C': g(ks[9], (D, N)), 'b_C': g(ks[10], (N,)), 'A_log': jnp.log(jnp.broadcast_to(jnp.arange(1, N + 1, dtype=jnp.float32), (D, N))), 'D_skip': jnp.ones((D,), dtype=jnp.float32), 'W_down': g(ks[11], (D, R)), 'b_down': g(ks[12], (R,))}
        return inp
    _L0_attn_all = _L0_attn_setup()
    _L0_attn_in = {k: v for k, v in _L0_attn_all.items() if k in ('W_up', 'b_up', 'conv_w', 'conv_b', 'W_delta', 'b_delta', 'W_B', 'b_B', 'W_C', 'b_C', 'A_log', 'D_skip', 'W_down', 'b_down')}
    del _L0_attn_all

    def _L0_ffn_setup():
        import jax, jax.numpy as jnp
        import numpy as np
        B, S, H = (2, 256, 256)
        E, I, SI = (8, 128, 512)
        TOP_K, N_GROUP, TOPK_GROUP = (2, 2, 1)
        ROUTED_SCALE = 2.5

        def _route(x2d, gate_weight, gate_bias):
            T = x2d.shape[0]
            logits = x2d @ gate_weight.T
            scores = jax.nn.sigmoid(logits)
            sfc = scores + gate_bias[None, :]
            g = sfc.reshape(T, N_GROUP, E // N_GROUP)
            group_scores = jax.lax.top_k(g, 2)[0].sum(-1)
            _, gidx = jax.lax.top_k(group_scores, TOPK_GROUP)
            gmask = jnp.zeros((T, N_GROUP), sfc.dtype).at[jnp.arange(T)[:, None], gidx].set(1.0)
            smask = jnp.repeat(gmask, E // N_GROUP, axis=1)
            masked = jnp.where(smask > 0, sfc, 0.0)
            _, topk_idx = jax.lax.top_k(masked, TOP_K)
            topk_w = jnp.take_along_axis(scores, topk_idx, axis=1)
            topk_w = topk_w / (topk_w.sum(-1, keepdims=True) + 1e-20)
            topk_w = topk_w * ROUTED_SCALE
            return (topk_idx, topk_w)
        key = jax.random.key(seed)
        ks = jax.random.split(key, 7)

        def w(k, shape, sc=0.02):
            return jax.random.normal(k, shape, jnp.float32) * sc
        return {'hidden_states': jax.random.normal(ks[0], (B, S, H), jnp.float32), 'gate_weight': w(ks[1], (E, H)), 'gate_bias': w(ks[2], (E,), 0.01), 'up_weights': w(ks[3], (E, I, H)), 'down_weights': w(ks[4], (E, H, I)), 'shared_up_weight': w(ks[5], (SI, H)), 'shared_down_weight': w(ks[6], (H, SI))}
    _L0_ffn_all = _L0_ffn_setup()
    _L0_ffn_in = {k: v for k, v in _L0_ffn_all.items() if k in ('gate_weight', 'gate_bias', 'up_weights', 'down_weights', 'shared_up_weight', 'shared_down_weight')}
    del _L0_ffn_all

    def _L1_attn_setup():
        import math
        import jax, jax.numpy as jnp
        import numpy as np
        D_MODEL = 256
        N_HEADS = 16
        D_K = D_MODEL // N_HEADS
        D_C = 64
        B, S = (2, 512)
        key = jax.random.key(seed)
        ks = jax.random.split(key, 7)
        sd = lambda fan_in: 1.0 / math.sqrt(fan_in)
        return {'x': jax.random.normal(ks[0], (B, S, D_MODEL), dtype=jnp.float32), 'W_dq': jax.random.uniform(ks[1], (D_MODEL, D_C), minval=-sd(D_MODEL), maxval=sd(D_MODEL), dtype=jnp.float32), 'W_uq': jax.random.uniform(ks[2], (D_C, N_HEADS * D_K), minval=-sd(D_C), maxval=sd(D_C), dtype=jnp.float32), 'W_dkv': jax.random.uniform(ks[3], (D_MODEL, D_C), minval=-sd(D_MODEL), maxval=sd(D_MODEL), dtype=jnp.float32), 'W_uk': jax.random.uniform(ks[4], (D_C, N_HEADS * D_K), minval=-sd(D_C), maxval=sd(D_C), dtype=jnp.float32), 'W_uv': jax.random.uniform(ks[5], (D_C, N_HEADS * D_K), minval=-sd(D_C), maxval=sd(D_C), dtype=jnp.float32), 'W_o': jax.random.uniform(ks[6], (N_HEADS * D_K, D_MODEL), minval=-sd(N_HEADS * D_K), maxval=sd(N_HEADS * D_K), dtype=jnp.float32)}
    _L1_attn_all = _L1_attn_setup()
    _L1_attn_in = {k: v for k, v in _L1_attn_all.items() if k in ('W_dq', 'W_uq', 'W_dkv', 'W_uk', 'W_uv', 'W_o')}
    del _L1_attn_all

    def _L1_ffn_setup():
        import jax, jax.numpy as jnp
        import numpy as np
        B, S, D, H, E = (4, 512, 256, 512, 8)
        key = jax.random.key(seed)
        ks = jax.random.split(key, 8)
        scale = 0.02
        return {'x': jax.random.normal(ks[0], (B, S, D), dtype=jnp.float32), 'Wr': jax.random.normal(ks[1], (D, E), dtype=jnp.float32) * scale, 'br': jnp.zeros((E,), dtype=jnp.float32), 'W1': jax.random.normal(ks[2], (E, D, H), dtype=jnp.float32) * scale, 'b1': jnp.zeros((E, H), dtype=jnp.float32), 'W2': jax.random.normal(ks[3], (E, H, D), dtype=jnp.float32) * scale, 'b2': jnp.zeros((E, D), dtype=jnp.float32)}
    _L1_ffn_all = _L1_ffn_setup()
    _L1_ffn_in = {k: v for k, v in _L1_ffn_all.items() if k in ('Wr', 'br', 'W1', 'b1', 'W2', 'b2')}
    del _L1_ffn_all
    return {'x': x, 'L0_tok_W_lin': _L0_tok_in['W_lin'], 'L0_tok_b_lin': _L0_tok_in['b_lin'], 'L0_tok_class_token': _L0_tok_in['class_token'], 'L0_tok_position_embeddings': _L0_tok_in['position_embeddings'], 'L0_attn_W_up': _L0_attn_in['W_up'], 'L0_attn_b_up': _L0_attn_in['b_up'], 'L0_attn_conv_w': _L0_attn_in['conv_w'], 'L0_attn_conv_b': _L0_attn_in['conv_b'], 'L0_attn_W_delta': _L0_attn_in['W_delta'], 'L0_attn_b_delta': _L0_attn_in['b_delta'], 'L0_attn_W_B': _L0_attn_in['W_B'], 'L0_attn_b_B': _L0_attn_in['b_B'], 'L0_attn_W_C': _L0_attn_in['W_C'], 'L0_attn_b_C': _L0_attn_in['b_C'], 'L0_attn_A_log': _L0_attn_in['A_log'], 'L0_attn_D_skip': _L0_attn_in['D_skip'], 'L0_attn_W_down': _L0_attn_in['W_down'], 'L0_attn_b_down': _L0_attn_in['b_down'], 'L0_ffn_gate_weight': _L0_ffn_in['gate_weight'], 'L0_ffn_gate_bias': _L0_ffn_in['gate_bias'], 'L0_ffn_up_weights': _L0_ffn_in['up_weights'], 'L0_ffn_down_weights': _L0_ffn_in['down_weights'], 'L0_ffn_shared_up_weight': _L0_ffn_in['shared_up_weight'], 'L0_ffn_shared_down_weight': _L0_ffn_in['shared_down_weight'], 'L1_attn_W_dq': _L1_attn_in['W_dq'], 'L1_attn_W_uq': _L1_attn_in['W_uq'], 'L1_attn_W_dkv': _L1_attn_in['W_dkv'], 'L1_attn_W_uk': _L1_attn_in['W_uk'], 'L1_attn_W_uv': _L1_attn_in['W_uv'], 'L1_attn_W_o': _L1_attn_in['W_o'], 'L1_ffn_Wr': _L1_ffn_in['Wr'], 'L1_ffn_br': _L1_ffn_in['br'], 'L1_ffn_W1': _L1_ffn_in['W1'], 'L1_ffn_b1': _L1_ffn_in['b1'], 'L1_ffn_W2': _L1_ffn_in['W2'], 'L1_ffn_b2': _L1_ffn_in['b2']}

def reference(x, L0_tok_W_lin, L0_tok_b_lin, L0_tok_class_token, L0_tok_position_embeddings, L0_attn_W_up, L0_attn_b_up, L0_attn_conv_w, L0_attn_conv_b, L0_attn_W_delta, L0_attn_b_delta, L0_attn_W_B, L0_attn_b_B, L0_attn_W_C, L0_attn_b_C, L0_attn_A_log, L0_attn_D_skip, L0_attn_W_down, L0_attn_b_down, L0_ffn_gate_weight, L0_ffn_gate_bias, L0_ffn_up_weights, L0_ffn_down_weights, L0_ffn_shared_up_weight, L0_ffn_shared_down_weight, L1_attn_W_dq, L1_attn_W_uq, L1_attn_W_dkv, L1_attn_W_uk, L1_attn_W_uv, L1_attn_W_o, L1_ffn_Wr, L1_ffn_br, L1_ffn_W1, L1_ffn_b1, L1_ffn_W2, L1_ffn_b2):
    import jax
    import jax.numpy as jnp

    def _L0_tok_ref(data, W_lin, b_lin, class_token, position_embeddings):
        import jax, jax.numpy as jnp
        import numpy as np
        B, C, H, W = (64, 3, 96, 96)
        P = 16
        HP, WP = (H // P, W // P)
        N = HP * WP
        F = C * P * P
        D = 256
        b = data.shape[0]
        x = data.reshape(b, C, HP, P, WP, P)
        x = x.transpose(0, 2, 4, 1, 3, 5).reshape(b, N, F)
        x = jnp.einsum('bnf,df->bnd', x, W_lin) + b_lin
        cls = jnp.broadcast_to(class_token, (b, 1, D))
        out = jnp.concatenate([cls, x], axis=1) + position_embeddings
        return out

    def _L0_attn_ref(up_x, W_up, b_up, conv_w, conv_b, W_delta, b_delta, W_B, b_B, W_C, b_C, A_log, D_skip, W_down, b_down):
        import jax, jax.numpy as jnp
        import numpy as np
        B, L, R = (4, 512, 256)
        HID, EXP, K = (64, 2, 3)
        D = HID * EXP
        N = HID
        Lq = up_x.shape[1]
        u = up_x @ W_up + b_up
        left, right = jnp.split(u, 2, axis=-1)
        xp = jnp.pad(left, ((0, 0), (K - 1, 0), (0, 0)))
        conv = sum((conv_w[:, k] * xp[:, k:k + Lq, :] for k in range(K))) + conv_b
        x = jax.nn.silu(conv)
        delta = jax.nn.softplus(x @ W_delta + b_delta)
        Bm = x @ W_B + b_B
        Cm = x @ W_C + b_C
        A = -jnp.exp(A_log)
        dA = jnp.exp(delta[..., None] * A)
        dBx = delta[..., None] * Bm[:, :, None, :] * x[..., None]

        def step(h, inputs):
            dA_t, dBx_t, C_t = inputs
            h = dA_t * h + dBx_t
            y_t = jnp.einsum('bdn,bn->bd', h, C_t)
            return (h, y_t)
        h0 = jnp.zeros((up_x.shape[0], D, N), dtype=x.dtype)
        _, ys = jax.lax.scan(step, h0, (jnp.swapaxes(dA, 0, 1), jnp.swapaxes(dBx, 0, 1), jnp.swapaxes(Cm, 0, 1)))
        y = jnp.swapaxes(ys, 0, 1) + D_skip * x
        gated = y * jax.nn.silu(right)
        return gated @ W_down + b_down

    def _L0_ffn_ref(hidden_states, gate_weight, gate_bias, up_weights, down_weights, shared_up_weight, shared_down_weight):
        import jax, jax.numpy as jnp
        import numpy as np
        B, S, H = (2, 256, 256)
        E, I, SI = (8, 128, 512)
        TOP_K, N_GROUP, TOPK_GROUP = (2, 2, 1)
        ROUTED_SCALE = 2.5

        def _route(x2d, gate_weight, gate_bias):
            T = x2d.shape[0]
            logits = x2d @ gate_weight.T
            scores = jax.nn.sigmoid(logits)
            sfc = scores + gate_bias[None, :]
            g = sfc.reshape(T, N_GROUP, E // N_GROUP)
            group_scores = jax.lax.top_k(g, 2)[0].sum(-1)
            _, gidx = jax.lax.top_k(group_scores, TOPK_GROUP)
            gmask = jnp.zeros((T, N_GROUP), sfc.dtype).at[jnp.arange(T)[:, None], gidx].set(1.0)
            smask = jnp.repeat(gmask, E // N_GROUP, axis=1)
            masked = jnp.where(smask > 0, sfc, 0.0)
            _, topk_idx = jax.lax.top_k(masked, TOP_K)
            topk_w = jnp.take_along_axis(scores, topk_idx, axis=1)
            topk_w = topk_w / (topk_w.sum(-1, keepdims=True) + 1e-20)
            topk_w = topk_w * ROUTED_SCALE
            return (topk_idx, topk_w)
        Bv, Sv, Hv = hidden_states.shape
        x = hidden_states.reshape(-1, Hv)
        T = x.shape[0]
        topk_idx, topk_w = _route(x, gate_weight, gate_bias)
        cw = jnp.zeros((T, E), x.dtype).at[jnp.arange(T)[:, None], topk_idx].add(topk_w)
        h = jnp.einsum('th,eih->tei', x, up_weights)
        r = jnp.maximum(h, 0.0)
        r2 = r * r
        routed = jnp.einsum('tei,ehi,te->th', r2, down_weights, cw)
        sh = jnp.maximum(x @ shared_up_weight.T, 0.0)
        shared = sh * sh @ shared_down_weight.T
        return (routed + shared).reshape(Bv, Sv, Hv)

    def _L1_attn_ref(x, W_dq, W_uq, W_dkv, W_uk, W_uv, W_o):
        import math
        import jax, jax.numpy as jnp
        import numpy as np
        D_MODEL = 256
        N_HEADS = 16
        D_K = D_MODEL // N_HEADS
        D_C = 64
        B, S = (2, 512)
        Bx, Sx, _ = x.shape
        c_q = x @ W_dq
        Q = (c_q @ W_uq).reshape(Bx, Sx, N_HEADS, D_K)
        c_kv = x @ W_dkv
        K = (c_kv @ W_uk).reshape(Bx, Sx, N_HEADS, D_K)
        V = (c_kv @ W_uv).reshape(Bx, Sx, N_HEADS, D_K)
        scores = jnp.einsum('bqhd,bkhd->bhqk', Q, K) / math.sqrt(D_K)
        causal = jnp.tril(jnp.ones((Sx, Sx), dtype=bool))
        scores = jnp.where(causal, scores, -jnp.inf)
        attn = jax.nn.softmax(scores, axis=-1)
        out = jnp.einsum('bhqk,bkhd->bqhd', attn, V).reshape(Bx, Sx, N_HEADS * D_K)
        return out @ W_o

    def _L1_ffn_ref(x, Wr, br, W1, b1, W2, b2):
        import jax, jax.numpy as jnp
        import numpy as np
        B, S, D, H, E = (4, 512, 256, 512, 8)
        d = x.shape[-1]
        tokens = x.reshape(-1, d)
        logits = tokens @ Wr + br
        probs = jax.nn.softmax(logits, axis=-1)
        expert = jnp.argmax(probs, axis=-1)
        max_prob = jnp.take_along_axis(probs, expert[:, None], axis=-1)
        h = jax.nn.relu(jnp.einsum('td,edh->teh', tokens, W1) + b1[None])
        y = jnp.einsum('teh,ehd->ted', h, W2) + b2[None]
        out = jnp.take_along_axis(y, expert[:, None, None], axis=1)[:, 0, :]
        return (out * max_prob).reshape(x.shape)
    h = _L0_tok_ref(x, L0_tok_W_lin, L0_tok_b_lin, L0_tok_class_token, L0_tok_position_embeddings)
    h = h + _L0_attn_ref(_layernorm(h, axis=-1), L0_attn_W_up, L0_attn_b_up, L0_attn_conv_w, L0_attn_conv_b, L0_attn_W_delta, L0_attn_b_delta, L0_attn_W_B, L0_attn_b_B, L0_attn_W_C, L0_attn_b_C, L0_attn_A_log, L0_attn_D_skip, L0_attn_W_down, L0_attn_b_down)
    h = h + _L0_ffn_ref(_layernorm(h, axis=-1), L0_ffn_gate_weight, L0_ffn_gate_bias, L0_ffn_up_weights, L0_ffn_down_weights, L0_ffn_shared_up_weight, L0_ffn_shared_down_weight)
    h = h + _L1_attn_ref(_layernorm(h, axis=-1), L1_attn_W_dq, L1_attn_W_uq, L1_attn_W_dkv, L1_attn_W_uk, L1_attn_W_uv, L1_attn_W_o)
    h = h + _L1_ffn_ref(_layernorm(h, axis=-1), L1_ffn_Wr, L1_ffn_br, L1_ffn_W1, L1_ffn_b1, L1_ffn_W2, L1_ffn_b2)
    return h

_drawn_inputs = setup_inputs


def setup_inputs(seed=0):
    import zlib

    import numpy as np

    out = dict(_drawn_inputs(seed))
    spreads = {'L0_attn_D_skip': (1.0, 0.6),
     'L1_ffn_br': (0.0, 0.591),
     'L1_ffn_b1': (0.0, 0.8),
     'L1_ffn_b2': (0.0, 1.446)}
    factors = {'L0_tok_b_lin': 2.853,
     'L0_attn_W_up': 8.0,
     'L0_attn_b_up': 8.0,
     'L0_attn_conv_w': 8.0,
     'L0_attn_conv_b': 8.0,
     'L0_attn_W_delta': 8.0,
     'L0_attn_b_delta': 8.0,
     'L0_attn_W_B': 8.0,
     'L0_attn_b_B': 8.0,
     'L0_attn_W_C': 8.0,
     'L0_attn_b_C': 8.0,
     'L0_attn_A_log': 8.0,
     'L0_attn_W_down': 8.0,
     'L0_attn_b_down': 10.156,
     'L0_ffn_gate_bias': 20.955,
     'L1_attn_W_dq': 8.0,
     'L1_attn_W_uq': 8.0,
     'L1_attn_W_uk': 8.0,
     'L1_ffn_W1': 3.975,
     'L1_ffn_W2': 3.143,
     'L0_ffn_gate_weight': 3.721,
     'L0_ffn_up_weights': 3.394,
     'L0_ffn_down_weights': 3.085,
     'L0_ffn_shared_up_weight': 3.239,
     'L0_ffn_shared_down_weight': 2.905}
    for name, (base, spread) in spreads.items():
        noise = np.random.default_rng([zlib.crc32(name.encode()), seed]).standard_normal(out[name].shape)
        drawn = base * np.exp(spread * noise) if base else spread * noise
        out[name] = jnp.asarray(drawn.astype(out[name].dtype))
    for name, factor in factors.items():
        out[name] = (out[name] * factor).astype(out[name].dtype)
    return out
```

```python
from contextlib import ExitStack

import concourse.bass as bass
from concourse import mybir

P = 128
NI, L = 64, 37
NP = L - 1
T = NI * L
IC = 8
CH = IC * L
NCH = NI // IC
D, HALVES = 256, 2
FK = 6
N = 64
NQ = 4
QI = NI // NQ
QT = QI * L
TT = 19
TP = TT * P
E8 = 8
HEADS, DK = 16, 16
KG = 3
EPS = 1e-5

F32, BF16 = mybir.dt.float32, mybir.dt.bfloat16
ALU = mybir.AluOpType
ACT = mybir.ActivationFunctionType
AX = mybir.AxisListType.X
ds = bass.ds

SMALL = [("pos", 2 * L), ("b_lin", 2), ("cls", 2), ("b_up", 2), ("conv_w", 3), ("conv_b", 1),
         ("b_delta", 1), ("b_bc", 1), ("a_log", N), ("d_skip", 1), ("b_down", 2), ("gate_b", E8),
         ("b_r", E8), ("b1", 32), ("ident", P), ("head_of_row", E8), ("v_mask", KG * P),
         ("causal", L), ("earlier", E8 * E8), ("row32", 32), ("eps", 1)]
AT = {}
_n = 0
for _name, _w in SMALL:
    AT[_name] = (_n, _w)
    _n += _w
NSMALL = _n

DENSE = [("w_up", 512), ("w_delta", 128), ("w_bc", 128), ("w_down", 256), ("gate_w", 16),
         ("w_dqkv", 256), ("w_u", 512), ("w_o", 512), ("w_r", 16)]
WAT = {}
_n = 0
for _name, _w in DENSE:
    WAT[_name] = (_n, _w)
    _n += _w
NDENSE = _n


def bc(ap, axis, n):
    ap = ap.unsqueeze(axis)
    shape = list(ap.shape)
    shape[axis] = n
    return ap.broadcast_to(shape)


def build(nc, small, dense, patches, w_lin, up0, dn0, w1, w2, b2, gates_dram, out):
    with ExitStack() as ctx:
        def sb(name, shape, dt=F32):
            return ctx.enter_context(nc.sbuf_tensor(name, shape, dt))

        def sem(name):
            return ctx.enter_context(nc.semaphore(name))

        hT = sb("hT", [P, HALVES, NI, L])
        hF = hT[:].rearrange("p a i l -> p a (i l)")
        xn = sb("xn", [P, HALVES, TP])
        sm = sb("sm", [P, NSMALL])
        wd = sb("wd", [P, NDENSE])
        b2s = sb("b2s", [E8, D])
        ones = sb("ones", [P, P])
        sq = sb("sq", [P, 2, HALVES, CH])
        rstd = sb("rstd", [P, 2, CH])
        posb = sb("posb", [P, HALVES, L])
        lg = sb("lg", [P, TT, E8])
        sc = sb("sc", [P, TT, E8])
        rt1 = sb("rt1", [P, TT, E8])
        rt2 = sb("rt2", [P, TT, E8])
        pairs = sb("pairs", [P, TT, 2, 6])
        gsum = sb("gsum", [P, TT, 2])
        gsel = sb("gsel", [P, TT, 2])
        red = sb("red", [P, TT])

        gbc = sb("gbc", [P, 2, E8, CH])
        gflat = gbc[:].rearrange("p a e t -> p (a e t)")
        xin = gflat[:, 0:2 * FK * IC * NP].rearrange("p (j k n) -> p j k n", j=2, k=FK)
        sel = gflat[0:96, 0:32 * P // 2].bitcast(BF16).rearrange("p (n m) -> p n m", n=32)

        AREA = 30720
        area = sb("area", [P, AREA])
        a_off = [0]

        def carve(words, dt=F32):
            v = area[:, a_off[0]:a_off[0] + words]
            a_off[0] += words
            assert a_off[0] <= AREA, a_off[0]
            return v if dt == F32 else v.bitcast(dt)

        wl = carve(FK * D).rearrange("p (k d) -> p k d", k=FK)
        leftp = carve(NI * (L + 2)).rearrange("p (i l) -> p i l", i=NI)
        cv = carve(T).rearrange("p (i l) -> p i l", i=NI)
        cvF = cv.rearrange("p i l -> p (i l)")
        x_off = a_off[0]
        xs = carve(T)
        sright = carve(T)
        delta = carve(T)
        dx = carve(T)
        dz = carve(T)
        bcv = carve(T)
        parts = [carve(T // 2, BF16) for _ in range(3)]
        stacks = [carve(T // 2, BF16) for _ in range(4)]
        aneg = sb("aneg", [P, N])
        diag_d = sb("diag_d", [P, P])
        decay = [carve(QT).rearrange("p (i l) -> p i l", i=QI) for _ in range(2)]
        inject = [cvF[:, 0:QT], cvF[:, QT:2 * QT]]
        state = [cvF[:, 2 * QT:3 * QT], cvF[:, 3 * QT:4 * QT]]
        leftF = leftp.rearrange("p i l -> p (i l)")
        read = [leftF[:, 0:QT], leftF[:, QT:2 * QT]]
        bsb = [leftF[:, 2 * QT:3 * QT], leftF[:, 3 * QT:4 * QT]]
        gated = dz

        a_off[0] = 0
        w1s = carve(2 * 4096).rearrange("p (k n) -> p k n", k=2)
        w2s = carve(32 * D).rearrange("p (j n) -> p j n", j=32)
        f_off = a_off[0]
        up0s = carve(2 * 1536).rearrange("p (k n) -> p k n", k=2)
        dn0s = carve(12 * D).rearrange("p (j n) -> p j n", j=12)
        a_off[0] = f_off
        cc = carve(CH)
        qT = carve(2 * CH).rearrange("p (a t) -> p a t", a=2)
        kT = carve(2 * CH).rearrange("p (a t) -> p a t", a=2)
        ckv3 = carve(IC * KG * L).rearrange("p (i r l) -> p i r l", i=IC, r=KG)
        kbd = [carve(4 * 8 * L).rearrange("p (a i h l) -> p a i h l", a=2, i=2, h=8) for _ in range(2)]
        prob = [carve(HEADS * L).rearrange("p (h l) -> p h l", h=HEADS) for _ in range(2)]
        probT = carve(2 * KG * 101).rearrange("p (a c q) -> p a c q", a=2, c=KG)
        vbd = [carve(2 * KG * P).rearrange("p (a c d) -> p a c d", a=2, c=KG) for _ in range(2)]
        oT = carve(2 * CH).rearrange("p (a t) -> p a t", a=2)
        rowm = carve(2 * HEADS).rearrange("p (a h) -> p a h", a=2)
        rows = carve(2 * HEADS).rearrange("p (a h) -> p a h", a=2)
        hid, hid2, hid3 = [carve(3 * CH).rearrange("p (b t) -> p b t", b=3) for _ in range(3)]
        cwT = carve(TP)[0:E8]

        ps = ctx.enter_context(nc.psum_tensor("ps", [P, 8, 512], F32))

        def S(name, part=None):
            o, w = AT[name]
            return sm[:, o:o + w]

        def W(name):
            o, w = WAT[name]
            return wd[:, o:o + w]

        ident = S("ident")
        w_up = W("w_up").rearrange("p (k n) -> p k n", k=2)
        gate_w = W("gate_w").rearrange("p (k n) -> p k n", k=2)
        w_r = W("w_r").rearrange("p (k n) -> p k n", k=2)
        w_dqkv = W("w_dqkv").rearrange("p (k n) -> p k n", k=2)
        w_u = W("w_u")
        w_o = W("w_o").rearrange("p (k n) -> p k n", k=2)

        small_in, dense_in, lin_in = sem("small_in"), sem("dense_in"), sem("lin_in")
        patches_in = [sem("patches_in0"), sem("patches_in1")]
        ffn0_in, ffn1_in = sem("ffn0_in"), sem("ffn1_in")
        consts_set = sem("consts_set")
        pos_ready = sem("pos_ready")
        embedded_ps, embedded = sem("embedded_ps"), sem("embedded")
        LNS = {}
        for ph in ("scan", "moe0", "attn", "moe1"):
            LNS[ph] = {n: sem(f"{ph}_{n}") for n in
                       ("mean", "centered", "squared", "var", "logvar", "rstd", "normed")}
        up_ps, up_left, up_right = sem("up_ps"), sem("up_left"), sem("up_right")
        conv_step, x_ready = sem("conv_step"), sem("x_ready")
        zbc_ps, z_copied, bc_copied = sem("zbc_ps"), sem("z_copied"), sem("bc_copied")
        soft_step, delta_ready, dx_ready = sem("soft_step"), sem("delta_ready"), sem("dx_ready")
        a_exp, a_ready = sem("a_exp"), sem("a_ready")
        split_step, stacks_in = sem("split_step"), sem("stacks_in")
        b_bcast, b_copied, c_bcast = sem("b_bcast"), sem("b_copied"), sem("c_bcast")
        decayed, injected, scanned = sem("decayed"), sem("injected"), sem("scanned")
        read_out, summed = sem("read_out"), sem("summed")
        y_gated = sem("y_gated")
        down_ps, scan_h = sem("down_ps"), sem("scan_h")
        MOE = {}
        for ph in ("moe0", "moe1"):
            MOE[ph] = {n: sem(f"{ph}_{n}") for n in
                       ("logits", "route", "routeT", "cwT", "gates_out", "gates_in0", "gates_in1",
                        "up", "relu", "hid", "down", "h", "gate1", "lg", "exp")}
        moe_out = sem("moe_out")
        cc_ps, cc_copied, ckv_rep = sem("cc_ps"), sem("cc_copied"), sem("ckv_rep")
        qk_ps, q_copied, k_copied = sem("qk_ps"), sem("q_copied"), sem("k_copied")
        k_spread = sem("k_spread")
        scores_ps, masked, maxed, shifted = sem("scores_ps"), sem("masked"), sem("maxed"), sem("shifted")
        exped, rowsum, inverted, scaled = sem("exped"), sem("rowsum"), sem("inverted"), sem("scaled")
        p_turned, p_copied = sem("p_turned"), sem("p_copied")
        v_ps, v_spread = sem("v_ps"), sem("v_spread")
        o_ps, o_copied = sem("o_ps"), sem("o_copied")
        wo_ps, attn_h = sem("wo_ps"), sem("attn_h")

        block = ctx.enter_context(nc.Block())

        def pe_norm(pe, s):
            with pe.Fori(0, NCH // 2) as i:
                for j in range(2):
                    c = i * 2 + j
                    pe.wait_ge(s["centered"], c + 1)
                    for k in range(HALVES):
                        mm = nc.tensor.matmul(ps[:, j, 0:CH], ones[:], hF[:, k, ds(c * CH, CH)],
                                              start=(k == 0), stop=(k == HALVES - 1))
                    mm.then_inc(s["mean"], 1)
                for j in range(2):
                    c = i * 2 + j
                    pe.wait_ge(s["squared"], c + 1)
                    pe.wait_ge(s["logvar"], c + 1)
                    for k in range(HALVES):
                        mm = nc.tensor.matmul(ps[:, 2 + j, 0:CH], ones[:], sq[:, j, k, :],
                                              start=(k == 0), stop=(k == HALVES - 1))
                    mm.then_inc(s["var"], 1)

        def act_norm(act, s):
            nc.scalar.preload_act_table_set("natural_log_exp_and_others")
            act.sem_inc(s["logvar"], 2)
            with act.Fori(0, NCH // 2) as i:
                for j in range(2):
                    c = i * 2 + j
                    act.wait_ge(s["centered"], c + 3)
                    act.wait_ge(s["logvar"], c + 1)
                    nc.scalar.activation(sq[:, j, :, :], xn[:, :, ds(c * CH, CH)],
                                         ACT.Square).then_inc(s["squared"], 1)
                for j in range(2):
                    c = i * 2 + j
                    act.wait_ge(s["var"], c + 1)
                    act.wait_ge(s["normed"], c + 1)
                    nc.scalar.activation(rstd[:, j, :], ps[:, 2 + j, 0:CH], ACT.Ln,
                                         bias=S("eps")).then_inc(s["logvar"], 1)
                for j in range(2):
                    c = i * 2 + j
                    act.wait_ge(s["logvar"], c + 3)
                    nc.scalar.activation(rstd[:, j, :], rstd[:, j, :], ACT.Exp,
                                         scale=-0.5).then_inc(s["rstd"], 1)

        def dve_norm(dve, s):
            dve.sem_inc(s["centered"], 2)
            with dve.Fori(0, NCH // 2) as i:
                for j in range(2):
                    c = i * 2 + j
                    dve.wait_ge(s["mean"], c + 1)
                    nc.vector.tensor_tensor(xn[:, :, ds(c * CH, CH)], hF[:, :, ds(c * CH, CH)],
                                            bc(ps[:, j, 0:CH], 1, HALVES),
                                            ALU.subtract).then_inc(s["centered"], 1)
                for j in range(2):
                    c = i * 2 + j
                    dve.wait_ge(s["rstd"], c + 1)
                    dve.wait_ge(s["centered"], c + 3)
                    nc.vector.tensor_tensor(xn[:, :, ds(c * CH, CH)], xn[:, :, ds(c * CH, CH)],
                                            bc(rstd[:, j, :], 1, HALVES),
                                            ALU.mult).then_inc(s["normed"], 1)

        def pe_logits(pe, s, w):
            for t in range(TT):
                for k in range(HALVES):
                    mm = nc.tensor.matmul(ps[:, 0, t * E8:(t + 1) * E8], xn[:, k, t * P:(t + 1) * P],
                                          w[:, k, :], start=(k == 0), stop=(k == HALVES - 1))
            mm.then_inc(s["logits"], 1)

        def pe_turn_weights(pe, s, n_route, weights):
            pe.wait_ge(s["route"], n_route)
            for t in range(TT):
                mm = nc.tensor.transpose(ps[0:E8, 1 + t // 4, (t % 4) * P:(t % 4 + 1) * P],
                                         weights[:, t, :], ident)
            mm.then_inc(s["routeT"], 1)

        def dve_copy_weights(dve, s):
            dve.wait_ge(s["routeT"], 1)
            for b in range(5):
                n = min(512, TP - b * 512)
                nc.vector.tensor_copy(cwT[:, b * 512:b * 512 + n],
                                      ps[0:E8, 1 + b, 0:n]).then_inc(s["cwT"], 1)

        def dve_select(link, scores, k, out_):
            cmp_ = xs_cmp
            link(nc.vector.tensor_tensor(cmp_, bc(scores, 2, E8), bc(scores, 3, E8), ALU.is_gt))
            link(nc.vector.tensor_tensor(xs_eq, bc(scores, 2, E8), bc(scores, 3, E8), ALU.is_equal))
            earlier = S("earlier").rearrange("p (a b) -> p a b", a=E8)
            link(nc.vector.tensor_tensor(xs_eq, xs_eq, bc(earlier, 1, TT), ALU.mult))
            link(nc.vector.tensor_tensor(cmp_, cmp_, xs_eq, ALU.add))
            link(nc.vector.tensor_reduce(out_, cmp_, AX, ALU.add))
            link(nc.vector.tensor_scalar(out_, out_, float(k) - 0.5, None, ALU.is_lt))

        xs_cmp = gflat[:, 0:TT * 64].rearrange(
            "p (t a b) -> p t a b", t=TT, a=E8)
        xs_eq = gflat[:, TT * 64:TT * 128].rearrange(
            "p (t a b) -> p t a b", t=TT, a=E8)

        def pe_moe(pe, s, nt, up_w, dn_w, bias):
            pe.wait_ge(s["cwT"], 5)
            with pe.Fori(0, NCH // 2) as i:
                for cj in range(2):
                    c = i * 2 + cj
                    cs = ds(c * CH, CH)
                    for j in range(nt + 2):
                        if j < nt:
                            pe.wait_ge(s["relu"], c * nt + j + 2)
                            for k in range(HALVES):
                                mm = nc.tensor.matmul(ps[:, 5 + j % 3, 0:CH],
                                                      up_w[:, k, j * P:(j + 1) * P],
                                                      xn[:, k, cs], start=(k == 0), stop=(k == 1))
                            mm.then_inc(s["up"], 1)
                        if j == 0:
                            pe.wait_ge(s["h"], c + 1)
                            if bias:
                                for m in range(HALVES):
                                    nc.tensor.matmul(ps[:, 1 + 2 * cj + m, 0:CH],
                                                     b2s[:, m * P:(m + 1) * P], cwT[:, cs],
                                                     start=True, stop=False)
                        if j >= 2:
                            jj = j - 2
                            pe.wait_ge(s["hid"], c * nt + jj + 4)
                            for m in range(HALVES):
                                mm = nc.tensor.matmul(ps[:, 1 + 2 * cj + m, 0:CH],
                                                      dn_w[:, jj, m * P:(m + 1) * P],
                                                      hid2[:, jj % 3, :],
                                                      start=(jj == 0 and not bias),
                                                      stop=(jj == nt - 1))
                            if jj == nt - 1:
                                mm.then_inc(s["down"], 1)

        def act_exp(act, s, sign):
            act.wait_ge(s["lg"], 1)
            nc.scalar.activation(sc[:], lg[:], ACT.Exp, scale=sign).then_inc(s["exp"], 1)

        def act_moe(act, s, nt, bias):
            act.sem_inc(s["relu"], 3)
            with act.Fori(0, NCH // 2) as i:
                for cj in range(2):
                    c = i * 2 + cj
                    for j in range(nt):
                        act.wait_ge(s["up"], c * nt + j + 1)
                        act.wait_ge(s["hid"], c * nt + j + 2)
                        nc.scalar.activation(hid[:, j % 3, :], ps[:, 5 + j % 3, 0:CH], ACT.Relu,
                                             bias=(S("b1")[:, j:j + 1] if bias else 0.0)
                                             ).then_inc(s["relu"], 1)

        def dve_moe(dve, s, nt, squares, last):
            dve.sem_inc(s["hid"], 3)
            dve.sem_inc(s["h"], 2)
            with dve.Fori(0, NCH // 2) as i:
                for cj in range(2):
                    c = i * 2 + cj
                    cs = ds(c * CH, CH)
                    dve.wait_ge(s["gates_in0" if cj == 0 else "gates_in1"], i * 16 + 16)
                    for j in range(nt):
                        dve.wait_ge(s["relu"], c * nt + j + 4)
                        a = hid[:, j % 3, :]
                        if squares and j < E8:
                            nc.vector.tensor_tensor(hid3[:, j % 3, :], a, gbc[:, cj, j, :],
                                                    ALU.mult).then_inc(s["gate1"], 1)
                            dve.wait_ge(s["gate1"], c * E8 + j + 1)
                            g = hid3[:, j % 3, :]
                        elif squares:
                            g = a
                        else:
                            g = gbc[:, cj, j // 4, :]
                        nc.vector.tensor_tensor(hid2[:, j % 3, :], a, g, ALU.mult).then_inc(s["hid"], 1)
                    dve.wait_ge(s["down"], c + 1)
                    nc.vector.tensor_tensor(hF[:, :, cs], hF[:, :, cs],
                                            ps[:, 1 + 2 * cj:3 + 2 * cj, 0:CH],
                                            ALU.add).then_inc(s["h"], 1)

        def sp_gates(sp, s, last, n_per):
            sp.wait_ge(s["cwT"], 5)
            sp.dma_start(gates_dram[last], cwT[:, 0:T]).then_inc(s["gates_out"], 16)
            sp.wait_ge(s["gates_out"], 16)
            with sp.Fori(0, NCH // 2) as i:
                for cj in range(2):
                    c = i * 2 + cj
                    sp.wait_ge(s["h"], c + 1)
                    sp.dma_start(gbc[:, cj, :, :],
                                 gates_dram[last][:, ds(c * CH, CH)].partition_broadcast(P)
                                 ).then_inc(s["gates_in0" if cj == 0 else "gates_in1"], 16)

        @block.sync
        def _(sp):
            sp.dma_start(sm[:], small).then_inc(small_in, 16)
            sp.dma_start(wl, w_lin).then_inc(lin_in, 16)
            with sp.Fori(0, NCH // 2) as i:
                for j in range(2):
                    sp.wait_ge(embedded, (i * 2 + j) * 2 + 2)
                    sp.dma_start(xin[:, j, :, :], patches[ds(i * 2 + j, 1), :, :, :].rearrange(
                        "o p k n -> (o p) k n")).then_inc(patches_in[j], 16)
            sp.dma_start(wd[:], dense).then_inc(dense_in, 16)
            sp.dma_start(b2s[:], b2).then_inc(dense_in, 16)
            sp.wait_ge(split_step, 5)
            for g in range(4):
                for k in range(3):
                    sp.dma_start(stacks[g][32 * k:32 * k + 32, :],
                                 parts[k][32 * g:32 * g + 32, :]).then_inc(stacks_in, 16)
            sp.wait_ge(scan_h, NCH + 2)
            sp.dma_start(up0s, up0).then_inc(ffn0_in, 16)
            sp.dma_start(dn0s, dn0).then_inc(ffn0_in, 16)
            sp.dma_start(w1s, w1).then_inc(ffn1_in, 16)
            sp.dma_start(w2s, w2).then_inc(ffn1_in, 16)
            sp_gates(sp, MOE["moe0"], 0, 12)
            sp_gates(sp, MOE["moe1"], 1, 32)

        @block.gpsimd
        def _(pool):
            nc.gpsimd.memset(ones[:], 1.0 / D).then_inc(consts_set, 1)
            nc.gpsimd.memset(xn[:, :, T:TP], 0.0).then_inc(consts_set, 1)
            nc.gpsimd.memset(leftp, 0.0).then_inc(consts_set, 1)
            for j in range(2):
                nc.gpsimd.memset(decay[j], 0.0).then_inc(consts_set, 1)
            pool.wait_ge(small_in, 16)
            pool.wait_ge(embedded, 4 + 2 * NCH)
            nc.gpsimd.tensor_copy(sel, bc(S("row32")[0:96, :], 2, P)).then_inc(consts_set, 1)

            pool.sem_inc(injected, 2)
            pool.wait_ge(dx_ready, 1)
            for q in range(NQ):
                with pool.Fori(0, N // 2) as i:
                    for j in range(2):
                        k = q * N + i * 2 + j
                        pool.wait_ge(b_copied, k + 2)
                        pool.wait_ge(scanned, k + 1)
                        nc.gpsimd.tensor_tensor(inject[j], dx[:, q * QT:(q + 1) * QT], bsb[j],
                                                ALU.mult).then_inc(injected, 1)

            pool.sem_inc(k_spread, 1)
            mask = S("head_of_row")
            with pool.Fori(0, NCH) as c:
                for p in range(4):
                    k = c * 4 + p
                    if p == 0:
                        pool.wait_ge(k_copied, c + 1)
                    pool.wait_ge(scores_ps, k + 1)
                    for a in range(2):
                        for im in range(2):
                            t0 = (2 * p + im) * L
                            mm = nc.gpsimd.tensor_tensor(
                                kbd[p % 2][:, a, im, :, :], bc(kT[:, a, t0:t0 + L], 1, 8),
                                bc(mask, 2, L), ALU.mult)
                    mm.then_inc(k_spread, 1)

            with pool.Fori(0, NCH) as c:
                pool.wait_ge(MOE["moe1"]["h"], c + 3)
                pool.dma_start(out[:, :, ds(c * CH, CH)], hF[:, :, ds(c * CH, CH)]
                               ).then_inc(moe_out, 16)
            pool.wait_ge(moe_out, 16 * NCH)

        @block.tensor
        def _(pe):
            pe.wait_ge(lin_in, 16)
            with pe.Fori(0, NCH // 2) as i:
                for j in range(2):
                    c = i * 2 + j
                    pe.wait_ge(patches_in[j], i * 16 + 16)
                    pe.wait_ge(embedded, c * 2 + 2)
                    for m in range(HALVES):
                        for k in range(FK):
                            mm = nc.tensor.matmul(ps[:, 2 * j + m, 0:IC * NP],
                                                  wl[:, k, m * P:(m + 1) * P], xin[:, j, k, :],
                                                  start=(k == 0), stop=(k == FK - 1))
                    mm.then_inc(embedded_ps, 1)

            pe.wait_ge(embedded, 4 + 2 * NCH)
            pe.wait_ge(consts_set, 5)
            pe.wait_ge(pos_ready, 6)
            pe_norm(pe, LNS["scan"])
            pe.wait_ge(dense_in, 32)
            with pe.Fori(0, NCH // 2) as i:
                for j in range(2):
                    c = i * 2 + j
                    pe.wait_ge(LNS["scan"]["normed"], c + 3)
                    pe.wait_ge(up_right, c + 1)
                    for m in range(2):
                        for k in range(HALVES):
                            mm = nc.tensor.matmul(ps[:, 4 + 2 * m + j, 0:CH],
                                                  w_up[:, k, m * P:(m + 1) * P],
                                                  xn[:, k, ds(c * CH, CH)],
                                                  start=(k == 0), stop=(k == 1))
                    mm.then_inc(up_ps, 1)
            with pe.Fori(0, NCH // 2) as i:
                for j in range(2):
                    c = i * 2 + j
                    pe.wait_ge(x_ready, 1)
                    pe.wait_ge(bc_copied, c + 1)
                    nc.tensor.matmul(ps[:, j, 0:CH], W("w_delta"), xs[:, ds(c * CH, CH)],
                                     start=True, stop=True)
                    nc.tensor.matmul(ps[:, 2 + j, 0:CH], W("w_bc"), xs[:, ds(c * CH, CH)],
                                     start=True, stop=True).then_inc(zbc_ps, 1)

            def spread(q, i, j):
                k = q * N + i * 2 + j
                pe.wait_ge(b_copied, k + 1)
                for h in range(2):
                    mm = nc.tensor.matmul(ps[:, 2 + h, 0:CH], sel[:, ds(i, 1), :].rearrange(
                        "p o m -> p (o m)"), stacks[j][0:96, ds(q * QT + h * CH, CH)], start=True, stop=True)
                mm.then_inc(b_bcast, 1)
                pe.wait_ge(read_out, k + 1)
                for h in range(2):
                    mm = nc.tensor.matmul(ps[:, 4 + 2 * j + h, 0:CH], sel[:, ds(i, 1), :].rearrange(
                        "p o m -> p (o m)"), stacks[2 + j][0:96, ds(q * QT + h * CH, CH)], start=True, stop=True)
                mm.then_inc(c_bcast, 1)

            def sum_state(q, i, j, last=False):
                k = q * N + i * 2 + j
                pe.wait_ge(read_out, k + 3)
                for h in range(2):
                    mm = nc.tensor.matmul(ps[:, h, 0:CH], ident, read[j][:, h * CH:(h + 1) * CH],
                                          start=False, stop=last, skip_group_check=True)
                mm.then_inc(summed, 1)

            pe.wait_ge(stacks_in, 16 * 12)
            pe.wait_ge(a_ready, 2)
            pe.wait_ge(consts_set, 6)
            pe.sem_inc(summed, 2)
            pe.wait_ge(bc_copied, NCH + 2)
            pe.wait_ge(z_copied, NCH)
            with pe.Fori(0, NQ) as q:
                pe.wait_ge(y_gated, q + 1)
                for h in range(2):
                    nc.tensor.matmul(ps[:, h, 0:CH], diag_d[:], xs[:, ds(q * QT + h * CH, CH)],
                                     start=True, stop=False, skip_group_check=True)
                spread(q, 0, 0)
                with pe.Fori(0, N // 2 - 1) as i:
                    spread(q, i, 1)
                    sum_state(q, i, 0)
                    spread(q, i + 1, 0)
                    sum_state(q, i, 1)
                spread(q, N // 2 - 1, 1)
                sum_state(q, N // 2 - 1, 0)
                sum_state(q, N // 2 - 1, 1, last=True)
            pe.wait_ge(y_gated, NQ + 1)
            with pe.Fori(0, NCH // 2) as i:
                for j in range(2):
                    c = i * 2 + j
                    pe.wait_ge(scan_h, c + 1)
                    for m in range(2):
                        mm = nc.tensor.matmul(ps[:, 2 + 2 * j + m, 0:CH],
                                              W("w_down")[:, m * P:(m + 1) * P],
                                              gated[:, ds(c * CH, CH)], start=True, stop=True)
                    mm.then_inc(down_ps, 1)

            pe.wait_ge(scan_h, NCH + 2)
            pe_norm(pe, LNS["moe0"])
            pe.wait_ge(LNS["moe0"]["normed"], NCH + 2)
            pe_logits(pe, MOE["moe0"], gate_w)
            pe_turn_weights(pe, MOE["moe0"], 1, rt1)
            pe.wait_ge(ffn0_in, 32)
            pe_moe(pe, MOE["moe0"], 12, up0s, dn0s, False)

            pe.wait_ge(MOE["moe0"]["h"], NCH + 2)
            pe_norm(pe, LNS["attn"])
            pe.wait_ge(LNS["attn"]["normed"], NCH + 2)
            pe.sem_inc(scores_ps, 2)
            pe.sem_inc(p_turned, 2)
            pe.sem_inc(o_ps, 1)
            pe.sem_inc(wo_ps, 1)
            with pe.Fori(0, NCH) as c:
                pe.wait_ge(attn_h, c + 1)
                for k in range(HALVES):
                    mm = nc.tensor.matmul(ps[:, 6, 0:CH], w_dqkv[:, k, :], xn[:, k, ds(c * CH, CH)],
                                          start=(k == 0), stop=(k == 1))
                mm.then_inc(cc_ps, 1)
                pe.wait_ge(cc_copied, c + 1)
                for m in range(2):
                    mm = nc.tensor.matmul(ps[:, 6 + m, 0:CH], w_u[0:64, m * P:(m + 1) * P],
                                          cc[0:64, :], start=True, stop=True)
                mm.then_inc(qk_ps, 1)
                pe.wait_ge(q_copied, c + 1)
                for m in range(2):
                    mm = nc.tensor.matmul(ps[:, 6 + m, 0:CH], w_u[64:128, m * P:(m + 1) * P],
                                          cc[64:128, :], start=True, stop=True)
                mm.then_inc(qk_ps, 1)

                def scores(p):
                    k = c * 4 + p
                    pe.wait_ge(k_spread, k + 2)
                    pe.wait_ge(masked, k + 1)
                    for im in range(2):
                        t0 = (2 * p + im) * L
                        nq = 64 if im == 0 else L
                        for a in range(2):
                            mm = nc.tensor.matmul(ps[64 * im:64 * im + nq, a, 0:8 * L],
                                                  qT[:, a, t0:t0 + nq],
                                                  kbd[p % 2][:, a, im, :, :].rearrange("p h l -> p (h l)"),
                                                  start=True, stop=True)
                    mm.then_inc(scores_ps, 1)

                scores(0)
                for p in range(4):
                    k = c * 4 + p
                    if p < 3:
                        scores(p + 1)
                    pe.wait_ge(ckv_rep, c + 1)
                    pe.wait_ge(v_spread, k * 2 + 1)
                    for im in range(2):
                        mm = nc.tensor.matmul(ps[0:KG * L, 4, im * D:(im + 1) * D],
                                              ckv3[64:128, 2 * p + im, :, :].rearrange("p r l -> p (r l)"),
                                              w_u[64:128, D:2 * D], start=True, stop=True)
                    mm.then_inc(v_ps, 1)
                    pe.wait_ge(scaled, k + 1)
                    pe.wait_ge(p_copied, k + 1)
                    for a in range(2):
                        for b in range(KG):
                            h0 = 8 * a + min(KG * b, 8 - KG)
                            mm = nc.tensor.transpose(ps[0:KG * L, 2 + a, b * 101:(b + 1) * 101],
                                                     prob[p % 2][0:101, h0:h0 + KG, :].rearrange(
                                                         "p h l -> p (h l)"), ident[0:101, 0:101])
                    mm.then_inc(p_turned, 1)
                    pe.wait_ge(p_copied, k + 2)
                    pe.wait_ge(o_copied, k + 1)
                    for im in range(2):
                        pe.wait_ge(v_spread, k * 2 + im + 2)
                        for a in range(2):
                            for b in range(KG):
                                mm = nc.tensor.matmul(ps[:, 5, (a * 2 + im) * L:(a * 2 + im + 1) * L],
                                                      vbd[im][0:KG * L, a, b, :],
                                                      probT[0:KG * L, a, b, 64 * im:64 * im + L],
                                                      start=(b == 0), stop=(b == KG - 1))
                    mm.then_inc(o_ps, 1)
                pe.wait_ge(o_copied, c * 4 + 5)
                for m in range(2):
                    for k in range(2):
                        mm = nc.tensor.matmul(ps[:, 6 + m, 0:CH], w_o[:, k, m * P:(m + 1) * P],
                                              oT[:, k, :], start=(k == 0), stop=(k == 1))
                mm.then_inc(wo_ps, 1)

            pe.wait_ge(attn_h, NCH + 1)
            pe_norm(pe, LNS["moe1"])
            pe.wait_ge(LNS["moe1"]["normed"], NCH + 2)
            pe_logits(pe, MOE["moe1"], w_r)
            pe_turn_weights(pe, MOE["moe1"], 1, rt1)
            pe.wait_ge(ffn1_in, 32)
            pe_moe(pe, MOE["moe1"], 32, w1s, w2s, True)

        @block.scalar
        def _(act):
            act.wait_ge(small_in, 16)
            act_norm(act, LNS["scan"])
            nc.scalar.preload_act_table(ACT.Silu)
            act.sem_inc(up_right, 2)
            act.wait_ge(consts_set, 3)
            with act.Fori(0, NCH // 2) as i:
                for j in range(2):
                    c = i * 2 + j
                    act.wait_ge(up_ps, c + 1)
                    nc.scalar.activation(leftp[:, ds(c * IC, IC), 2:L + 2],
                                         ps[:, 4 + j, 0:CH].rearrange("p (i l) -> p i l", i=IC),
                                         ACT.Identity, bias=S("b_up")[:, 0:1]).then_inc(up_left, 1)
                    nc.scalar.activation(sright[:, ds(c * CH, CH)], ps[:, 6 + j, 0:CH], ACT.Silu,
                                         bias=S("b_up")[:, 1:2]).then_inc(up_right, 1)
            act.wait_ge(conv_step, 3)
            nc.scalar.activation(xs, cvF, ACT.Silu).then_inc(x_ready, 1)
            nc.scalar.preload_act_table_set("natural_log_exp_and_others")
            nc.scalar.activation(aneg[:], S("a_log"), ACT.Exp).then_inc(a_exp, 1)
            act.sem_inc(bc_copied, 2)
            with act.Fori(0, NCH // 2) as i:
                for j in range(2):
                    c = i * 2 + j
                    act.wait_ge(zbc_ps, c + 1)
                    nc.scalar.activation(dz[:, ds(c * CH, CH)], ps[:, j, 0:CH], ACT.Identity,
                                         bias=S("b_delta")).then_inc(z_copied, 1)
                    nc.scalar.activation(bcv[:, ds(c * CH, CH)], ps[:, 2 + j, 0:CH], ACT.Identity,
                                         bias=S("b_bc")).then_inc(bc_copied, 1)
            act.wait_ge(z_copied, NCH)
            nc.scalar.activation(delta, dz, ACT.Abs).then_inc(soft_step, 1)
            act.wait_ge(soft_step, 1)
            nc.scalar.activation(delta, delta, ACT.Exp, scale=-1.0).then_inc(soft_step, 1)
            act.wait_ge(soft_step, 2)
            nc.scalar.activation(delta, delta, ACT.Ln, bias=1.0).then_inc(soft_step, 1)

            act.sem_inc(b_copied, 1)
            act.wait_ge(delta_ready, 1)
            act.wait_ge(a_ready, 2)
            with act.Fori(0, NQ) as q:
                with act.Fori(0, N // 2) as i:
                    for j in range(2):
                        k = q * N + i * 2 + j
                        act.wait_ge(b_bcast, k + 1)
                        act.wait_ge(injected, k + 1)
                        nc.scalar.activation(bsb[j].rearrange("p (h t) -> p h t", h=2),
                                             ps[:, 2:4, 0:CH], ACT.Copy).then_inc(b_copied, 1)
                        act.wait_ge(scanned, k + 1)
                        nc.scalar.activation(decay[j][:, :, 1:L],
                                             delta.rearrange("p (i l) -> p i l", i=NI)[:, ds(q * QI, QI), 1:L],
                                             ACT.Exp, scale=aneg[:, ds(i + j * 32, 1)]).then_inc(decayed, 1)

            act_norm(act, LNS["moe0"])
            act_exp(act, MOE["moe0"], -1.0)
            act_moe(act, MOE["moe0"], 12, False)

            act_norm(act, LNS["attn"])
            act.sem_inc(p_copied, 1)
            with act.Fori(0, NCH) as c:
                act.wait_ge(cc_ps, c + 1)
                nc.scalar.activation(cc, ps[:, 6, 0:CH], ACT.Copy).then_inc(cc_copied, 1)
                act.wait_ge(qk_ps, c * 2 + 1)
                nc.scalar.activation(qT, ps[:, 6:8, 0:CH], ACT.Copy,
                                     scale=DK ** -0.5).then_inc(q_copied, 1)
                act.wait_ge(qk_ps, c * 2 + 2)
                act.wait_ge(k_spread, c * 4 + 1)
                nc.scalar.activation(kT, ps[:, 6:8, 0:CH], ACT.Copy).then_inc(k_copied, 1)
                act.wait_ge(cc_copied, c + 1)
                nc.scalar.activation(ckv3[64:128], bc(cc[64:128, :].rearrange("p (i l) -> p i l", i=IC), 2, KG),
                                     ACT.Copy).then_inc(ckv_rep, 1)
                for p in range(4):
                    k = c * 4 + p
                    act.wait_ge(shifted, k + 1)
                    nc.scalar.activation(prob[p % 2][0:101], prob[p % 2][0:101], ACT.Exp).then_inc(exped, 1)
                    act.wait_ge(p_turned, k + 3)
                    act.wait_ge(o_ps, k + 1)
                    nc.scalar.activation(probT[0:KG * L].rearrange("p a c q -> p a (c q)"),
                                         ps[0:KG * L, 2:4, 0:KG * 101], ACT.Copy).then_inc(p_copied, 1)

            act_norm(act, LNS["moe1"])
            act_exp(act, MOE["moe1"], 1.0)
            act_moe(act, MOE["moe1"], 32, True)

        @block.vector
        def _(dve):
            linked = [0]
            chain = sem("dve_chain")

            def link(ins):
                linked[0] += 1
                ins.then_inc(chain, 1)
                dve.wait_ge(chain, linked[0])

            dve.wait_ge(small_in, 16)
            for m in range(HALVES):
                pos = S("pos").rearrange("p (a l) -> p a l", a=2)[:, m, :]
                nc.vector.tensor_scalar(posb[:, m, 1:L], pos[:, 1:L], S("b_lin")[:, m:m + 1], None,
                                        ALU.add).then_inc(pos_ready, 1)
                nc.vector.tensor_tensor(posb[:, m, 0:1], pos[:, 0:1], S("cls")[:, m:m + 1],
                                        ALU.add).then_inc(pos_ready, 1)
            dve.wait_ge(pos_ready, 4)
            for m in range(HALVES):
                nc.vector.tensor_copy(hT[:, m, :, 0], posb[:, m, 0:1].broadcast_to([P, NI])
                                      ).then_inc(pos_ready, 1)
            dve.sem_inc(embedded, 4)
            with dve.Fori(0, NCH // 2) as i:
                for j in range(2):
                    c = i * 2 + j
                    dve.wait_ge(embedded_ps, c + 1)
                    for m in range(HALVES):
                        nc.vector.tensor_tensor(hT[:, m, ds(c * IC, IC), 1:L],
                                                ps[:, 2 * j + m, 0:IC * NP].rearrange("p (i l) -> p i l", i=IC),
                                                bc(posb[:, m, 1:L], 1, IC), ALU.add).then_inc(embedded, 1)

            dve.sem_inc(LNS["scan"]["normed"], 2)
            dve_norm(dve, LNS["scan"])
            dve.wait_ge(up_left, NCH)
            w = S("conv_w")
            nc.vector.tensor_scalar(cv, leftp[:, :, 0:L], w[:, 0:1], S("conv_b"), ALU.mult,
                                    ALU.add).then_inc(conv_step, 1)
            for s_ in (1, 2):
                dve.wait_ge(conv_step, s_)
                nc.vector.scalar_tensor_tensor(out=cv, in0=leftp[:, :, s_:L + s_], scalar=w[:, s_:s_ + 1],
                                               in1=cv, op0=ALU.mult, op1=ALU.add).then_inc(conv_step, 1)
            dve.wait_ge(a_exp, 1)
            nc.vector.tensor_scalar(aneg[:], aneg[:], -1.0, None, ALU.mult).then_inc(a_ready, 1)
            nc.vector.tensor_scalar(diag_d[:], ident, S("d_skip"), None, ALU.mult).then_inc(a_ready, 1)
            dve.wait_ge(bc_copied, NCH + 2)
            nc.vector.tensor_copy(parts[0], bcv).then_inc(split_step, 1)
            dve.wait_ge(split_step, 1)
            nc.vector.tensor_tensor(bcv, bcv, parts[0], ALU.subtract).then_inc(split_step, 1)
            dve.wait_ge(split_step, 2)
            nc.vector.tensor_copy(parts[1], bcv).then_inc(split_step, 1)
            dve.wait_ge(split_step, 3)
            nc.vector.tensor_tensor(bcv, bcv, parts[1], ALU.subtract).then_inc(split_step, 1)
            dve.wait_ge(split_step, 4)
            nc.vector.tensor_copy(parts[2], bcv).then_inc(split_step, 1)
            dve.wait_ge(soft_step, 3)
            nc.vector.scalar_tensor_tensor(out=delta, in0=dz, scalar=0.0, in1=delta, op0=ALU.max,
                                           op1=ALU.add).then_inc(delta_ready, 1)
            dve.wait_ge(delta_ready, 1)
            dve.wait_ge(x_ready, 1)
            nc.vector.tensor_tensor(dx, delta, xs, ALU.mult).then_inc(dx_ready, 1)

            dve.sem_inc(scanned, 2)
            dve.sem_inc(read_out, 2)
            dve.sem_inc(y_gated, 1)
            with dve.Fori(0, NQ) as q:
                with dve.Fori(0, N // 2) as i:
                    for j in range(2):
                        k = q * N + i * 2 + j
                        dve.wait_ge(decayed, k + 1)
                        dve.wait_ge(injected, k + 3)
                        dve.wait_ge(read_out, k + 1)
                        nc.vector.tensor_tensor_scan(state[j], decay[j].rearrange("p i l -> p (i l)"),
                                                     inject[j], 0.0, ALU.mult, ALU.add).then_inc(scanned, 1)
                        dve.wait_ge(scanned, k + 3)
                        dve.wait_ge(c_bcast, k + 1)
                        dve.wait_ge(summed, k + 1)
                        nc.vector.tensor_tensor(read[j].rearrange("p (h t) -> p h t", h=2),
                                                state[j].rearrange("p (h t) -> p h t", h=2),
                                                ps[:, 4 + 2 * j:6 + 2 * j, 0:CH],
                                                ALU.mult).then_inc(read_out, 1)
                dve.wait_ge(summed, q * N + N + 2)
                nc.vector.tensor_tensor(
                    gated[:, ds(q * QT, QT)].rearrange("p (h t) -> p h t", h=2), ps[:, 0:2, 0:CH],
                    sright[:, ds(q * QT, QT)].rearrange("p (h t) -> p h t", h=2),
                    ALU.mult).then_inc(y_gated, 1)
            dve.sem_inc(scan_h, 2)
            with dve.Fori(0, NCH // 2) as i:
                for j in range(2):
                    c = i * 2 + j
                    cs = ds(c * CH, CH)
                    dve.wait_ge(down_ps, c + 1)
                    for m in range(2):
                        mm = nc.vector.scalar_tensor_tensor(
                            out=hF[:, m, cs], in0=ps[:, 2 + 2 * j + m, 0:CH],
                            scalar=S("b_down")[:, m:m + 1], in1=hF[:, m, cs], op0=ALU.add, op1=ALU.add)
                    mm.then_inc(scan_h, 1)

            dve.sem_inc(LNS["moe0"]["normed"], 2)
            dve_norm(dve, LNS["moe0"])
            s = MOE["moe0"]
            dve.wait_ge(s["logits"], 1)
            lgp = ps[:, 0, 0:TT * E8].rearrange("p (t e) -> p t e", t=TT)
            nc.vector.tensor_copy(lg[:], lgp).then_inc(s["lg"], 1)
            dve.wait_ge(s["exp"], 1)
            link(nc.vector.tensor_scalar(sc[:], sc[:], 1.0, None, ALU.add))
            link(nc.vector.reciprocal(sc[:], sc[:]))
            link(nc.vector.tensor_tensor(rt2[:], sc[:], bc(S("gate_b"), 1, TT), ALU.add))
            g4 = rt2[:].rearrange("p t (g e) -> p t g e", g=2)
            link(nc.vector.tensor_tensor(pairs[:, :, :, 0:3], g4[:, :, :, 0:3], g4[:, :, :, 1:4], ALU.add))
            link(nc.vector.tensor_tensor(pairs[:, :, :, 3:5], g4[:, :, :, 0:2], g4[:, :, :, 2:4], ALU.add))
            link(nc.vector.tensor_tensor(pairs[:, :, :, 5:6], g4[:, :, :, 0:1], g4[:, :, :, 3:4], ALU.add))
            link(nc.vector.tensor_reduce(gsum[:], pairs[:], AX, ALU.max))
            link(nc.vector.tensor_tensor(gsel[:, :, 0:1], gsum[:, :, 0:1], gsum[:, :, 1:2], ALU.is_ge))
            link(nc.vector.tensor_scalar(gsel[:, :, 1:2], gsel[:, :, 0:1], -1.0, 1.0, ALU.mult, ALU.add))
            link(nc.vector.tensor_tensor(g4, g4, bc(gsel[:], 3, 4), ALU.mult))
            dve_select(link, rt2[:], 2, rt1[:])
            link(nc.vector.tensor_tensor(rt1[:], rt1[:], sc[:], ALU.mult))
            link(nc.vector.tensor_reduce(red[:], rt1[:], AX, ALU.add))
            link(nc.vector.tensor_scalar(red[:], red[:], 1e-20, None, ALU.add))
            link(nc.vector.reciprocal(red[:], red[:]))
            link(nc.vector.tensor_tensor(rt1[:], rt1[:], bc(red[:], 2, E8), ALU.mult))
            nc.vector.tensor_scalar(rt1[:], rt1[:], 2.5, None, ALU.mult).then_inc(s["route"], 1)
            dve_copy_weights(dve, s)
            dve_moe(dve, s, 12, True, False)

            dve.sem_inc(LNS["attn"]["normed"], 2)
            dve_norm(dve, LNS["attn"])
            dve.sem_inc(masked, 1)
            dve.sem_inc(v_spread, 1)
            dve.sem_inc(o_copied, 1)
            dve.sem_inc(attn_h, 1)
            vmask = S("v_mask").rearrange("p (c d) -> p c d", c=KG)
            with dve.Fori(0, NCH) as c:
                def soften(p):
                    k = c * 4 + p
                    pr = prob[p % 2][0:101]
                    dve.wait_ge(scores_ps, k + 3)
                    dve.wait_ge(p_turned, k + 1)
                    nc.vector.tensor_tensor(pr.rearrange("p (a h) l -> p a h l", a=2),
                                            ps[0:101, 0:2, 0:8 * L].rearrange("p a (h l) -> p a h l", h=8),
                                            bc(bc(S("causal")[0:101], 1, 8), 1, 2),
                                            ALU.add).then_inc(masked, 1)
                    dve.wait_ge(masked, k + 2)
                    nc.vector.tensor_reduce(rowm[0:101, p % 2, :], pr, AX, ALU.max).then_inc(maxed, 1)
                    dve.wait_ge(maxed, k + 1)
                    nc.vector.tensor_tensor(pr, pr, bc(rowm[0:101, p % 2, :], 2, L),
                                            ALU.subtract).then_inc(shifted, 1)

                def values(p):
                    k = c * 4 + p
                    dve.wait_ge(v_ps, k + 1)
                    dve.wait_ge(o_ps, k + 1)
                    for im in range(2):
                        nc.vector.tensor_tensor(
                            vbd[im][0:KG * L],
                            bc(ps[0:KG * L, 4, im * D:(im + 1) * D].rearrange("p (a d) -> p a d", a=2), 2, KG),
                            bc(vmask[0:KG * L], 1, 2), ALU.mult).then_inc(v_spread, 1)

                def normalise(p):
                    k = c * 4 + p
                    pr = prob[p % 2][0:101]
                    dve.wait_ge(exped, k + 1)
                    nc.vector.tensor_reduce(rows[0:101, p % 2, :], pr, AX, ALU.add).then_inc(rowsum, 1)
                    dve.wait_ge(rowsum, k + 1)
                    nc.vector.reciprocal(rows[0:101, p % 2, :], rows[0:101, p % 2, :]).then_inc(inverted, 1)
                    dve.wait_ge(inverted, k + 1)
                    nc.vector.tensor_tensor(pr, pr, bc(rows[0:101, p % 2, :], 2, L),
                                            ALU.mult).then_inc(scaled, 1)

                def outputs(p):
                    k = c * 4 + p
                    dve.wait_ge(o_ps, k + 2)
                    if p == 0:
                        dve.wait_ge(wo_ps, c + 1)
                    nc.vector.tensor_copy(oT[:, :, 2 * p * L:(2 * p + 2) * L],
                                          ps[:, 5, 0:4 * L].rearrange("p (a t) -> p a t", a=2)
                                          ).then_inc(o_copied, 1)

                soften(0)
                for p in range(4):
                    values(p)
                    normalise(p)
                    if p < 3:
                        soften(p + 1)
                    outputs(p)
                dve.wait_ge(wo_ps, c + 2)
                nc.vector.tensor_tensor(hF[:, :, ds(c * CH, CH)], hF[:, :, ds(c * CH, CH)],
                                        ps[:, 6:8, 0:CH], ALU.add).then_inc(attn_h, 1)

            dve.sem_inc(LNS["moe1"]["normed"], 2)
            dve_norm(dve, LNS["moe1"])
            s = MOE["moe1"]
            dve.wait_ge(s["logits"], 1)
            link(nc.vector.tensor_tensor(lg[:], lgp, bc(S("b_r"), 1, TT), ALU.add))
            link(nc.vector.tensor_reduce(red[:], lg[:], AX, ALU.max))
            nc.vector.tensor_tensor(lg[:], lg[:], bc(red[:], 2, E8), ALU.subtract).then_inc(s["lg"], 1)
            dve.wait_ge(s["exp"], 1)
            link(nc.vector.tensor_reduce(red[:], sc[:], AX, ALU.add))
            link(nc.vector.reciprocal(red[:], red[:]))
            link(nc.vector.tensor_tensor(sc[:], sc[:], bc(red[:], 2, E8), ALU.mult))
            dve_select(link, sc[:], 1, rt1[:])
            nc.vector.tensor_tensor(rt1[:], rt1[:], sc[:], ALU.mult).then_inc(s["route"], 1)
            dve_copy_weights(dve, s)
            dve_moe(dve, s, 32, False, True)


def kernel(**inputs):
    import numpy as np
    import concourse.bacc as bacc
    from concourse.bass_utils import run_bass_kernel_spmd

    g = {k: np.asarray(v) for k, v in inputs.items()}

    def rows(a, k):
        return np.ascontiguousarray(a.reshape(k, P, -1).transpose(1, 0, 2))

    def cols(v):
        return v.reshape(-1, P).T

    x = g["x"].reshape(NCH, IC, 3, 6, 16, 6, 16).transpose(0, 2, 4, 6, 1, 3, 5)
    x = x.reshape(NCH, FK, P, IC * NP).transpose(0, 2, 1, 3)

    row = np.arange(P)
    eye = np.eye(P, dtype=np.float32)
    head_of_row = (row[:, None] // DK == np.arange(E8)[None]).astype(np.float32)
    v_mask = np.zeros((P, KG, P), np.float32)
    for b in range(KG):
        h0 = min(KG * b, 8 - KG)
        for r in range(KG):
            if h0 + r >= KG * b:
                v_mask[r * L:(r + 1) * L, b, (h0 + r) * DK:(h0 + r + 1) * DK] = 1.0
    causal = np.where(np.arange(L)[None] <= (row % 64)[:, None], 0.0, -1e30).astype(np.float32)
    earlier = np.tile((np.arange(E8)[None] < np.arange(E8)[:, None]).astype(np.float32).reshape(1, -1), (P, 1))
    row32 = (row[:, None] % 32 == np.arange(32)[None]).astype(np.float32)
    pieces = {
        "pos": rows(g["L0_tok_position_embeddings"][0].T, 2).reshape(P, -1),
        "b_lin": cols(g["L0_tok_b_lin"]), "cls": cols(g["L0_tok_class_token"].reshape(-1)),
        "b_up": cols(g["L0_attn_b_up"]), "conv_w": g["L0_attn_conv_w"],
        "conv_b": cols(g["L0_attn_conv_b"]), "b_delta": cols(g["L0_attn_b_delta"]),
        "b_bc": cols(np.concatenate([g["L0_attn_b_B"], g["L0_attn_b_C"]])),
        "a_log": g["L0_attn_A_log"], "d_skip": cols(g["L0_attn_D_skip"]),
        "b_down": cols(g["L0_attn_b_down"]),
        "gate_b": np.broadcast_to(g["L0_ffn_gate_bias"][None], (P, E8)),
        "b_r": np.broadcast_to(g["L1_ffn_br"][None], (P, E8)),
        "b1": cols(g["L1_ffn_b1"].reshape(-1)), "ident": eye, "head_of_row": head_of_row,
        "v_mask": v_mask.reshape(P, -1), "causal": causal, "earlier": earlier, "row32": row32,
        "eps": np.full((P, 1), EPS, np.float32),
    }
    for n, w in SMALL:
        assert pieces[n].shape == (P, w), (n, pieces[n].shape)
    zero = np.zeros((64, D), np.float32)
    dense = {
        "w_up": rows(g["L0_attn_W_up"], 2), "w_delta": g["L0_attn_W_delta"],
        "w_bc": np.concatenate([g["L0_attn_W_B"], g["L0_attn_W_C"]], axis=1),
        "w_down": g["L0_attn_W_down"], "gate_w": rows(g["L0_ffn_gate_weight"].T, 2),
        "w_dqkv": rows(np.concatenate([g["L1_attn_W_dq"], g["L1_attn_W_dkv"]], axis=1), 2),
        "w_u": np.concatenate([np.concatenate([g["L1_attn_W_uq"], zero], axis=1),
                               np.concatenate([g["L1_attn_W_uk"], g["L1_attn_W_uv"]], axis=1)]),
        "w_o": rows(g["L1_attn_W_o"], 2), "w_r": rows(g["L1_ffn_Wr"], 2),
    }
    arrays = {
        "small": np.concatenate([pieces[n] for n, _ in SMALL], axis=1),
        "dense": np.concatenate([dense[n].reshape(P, -1) for n, _ in DENSE], axis=1),
        "patches": x,
        "w_lin": rows(g["L0_tok_W_lin"].T, FK),
        "up0": rows(np.concatenate([g["L0_ffn_up_weights"].reshape(1024, D), g["L0_ffn_shared_up_weight"]]).T, 2),
        "dn0": np.concatenate([g["L0_ffn_down_weights"].transpose(0, 2, 1),
                               g["L0_ffn_shared_down_weight"].T.reshape(4, P, D)]).transpose(1, 0, 2),
        "w1": rows(g["L1_ffn_W1"].transpose(1, 0, 2).reshape(D, -1), 2),
        "w2": g["L1_ffn_W2"].reshape(32, P, D).transpose(1, 0, 2),
        "b2": g["L1_ffn_b2"],
    }
    arrays = {f"in_{k}": np.ascontiguousarray(v) for k, v in arrays.items()}
    nc = bacc.Bacc("TRN2", target_bir_lowering=False, num_devices=1)
    args = [nc.dram_tensor(k, v.shape, F32, kind="ExternalInput").ap() for k, v in arrays.items()]
    gates = nc.dram_tensor("gates", (2, E8, T), F32, kind="Internal").ap()
    res = nc.dram_tensor("out_h", (P, HALVES, T), F32, kind="ExternalOutput").ap()
    build(nc, *args, gates, res)
    got = run_bass_kernel_spmd(nc, [arrays], core_ids=[0]).results[0]["out_h"]
    return np.ascontiguousarray(got.transpose(1, 0, 2).reshape(D, NI, L).transpose(1, 2, 0))
```

```python
from contextlib import ExitStack

import concourse.bass as bass
from concourse import mybir

P = 128
NI, L = 64, 37
NP = L - 1
T = NI * L
IC = 8
CH = IC * L
NCH = NI // IC
D, HALVES = 256, 2
FK = 6
N = 64
NQ = 4
QI = NI // NQ
QT = QI * L
TT = 19
TP = TT * P
E8 = 8
HEADS, DK = 16, 16
KG = 3
QR = 64 + L
O_T = 2 * KG * (KG * DK + KG)
VB = KG * DK + KG
EPS = 1e-5

F32, BF16 = mybir.dt.float32, mybir.dt.bfloat16
ALU = mybir.AluOpType
ACT = mybir.ActivationFunctionType
AX = mybir.AxisListType.X
ds = bass.ds

SMALL = [("pos", 2 * L), ("b_lin", 2), ("cls", 2), ("b_up", 2), ("conv_w", 3), ("conv_b", 1),
         ("b_delta", 1), ("b_bc", 1), ("a_log", N), ("d_skip", 1), ("b_down", 2), ("gate_b", E8),
         ("b_r", E8), ("b1", 32), ("ident", P), ("head_of_row", E8), ("v_mask", VB),
         ("causal", L), ("earlier", E8 * E8), ("row32", 32), ("eps", 1)]
AT = {}
_n = 0
for _name, _w in SMALL:
    AT[_name] = (_n, _w)
    _n += _w
NSMALL = _n

DENSE = [("w_up", 512), ("w_delta", 128), ("w_bc", 128), ("w_down", 256), ("gate_w", 16),
         ("w_dqkv", 256), ("w_u", 512), ("w_o", 512), ("w_r", 16)]
WAT = {}
_n = 0
for _name, _w in DENSE:
    WAT[_name] = (_n, _w)
    _n += _w
NDENSE = _n


def bc(ap, axis, n):
    ap = ap.unsqueeze(axis)
    shape = list(ap.shape)
    shape[axis] = n
    return ap.broadcast_to(shape)


def build(nc, small, dense, patches, w_lin, up0, dn0, w1, w2, b2, gates_dram, out):
    with ExitStack() as ctx:
        def sb(name, shape, dt=F32):
            return ctx.enter_context(nc.sbuf_tensor(name, shape, dt))

        def sem(name):
            return ctx.enter_context(nc.semaphore(name))

        hT = sb("hT", [P, HALVES, NI, L])
        hF = hT[:].rearrange("p a i l -> p a (i l)")
        xn = sb("xn", [P, HALVES, TP])
        sm = sb("sm", [P, NSMALL])
        wd = sb("wd", [P, NDENSE])
        b2s = sb("b2s", [E8, D])
        ones = sb("ones", [P, P])
        sq = sb("sq", [P, 2, HALVES, CH])
        rstd = sb("rstd", [P, 2, CH])
        posb = sb("posb", [P, HALVES, L])
        lg = sb("lg", [P, TT, E8])
        sc = sb("sc", [P, TT, E8])
        rt1 = sb("rt1", [P, TT, E8])
        rt2 = sb("rt2", [P, TT, E8])
        pairs = sb("pairs", [P, TT, 2, 6])
        gsum = sb("gsum", [P, TT, 2])
        gsel = sb("gsel", [P, TT, 2])
        red = sb("red", [P, TT])

        gbc = sb("gbc", [P, 2, E8, CH])
        gflat = gbc[:].rearrange("p a e t -> p (a e t)")
        xin = gflat[:, 0:2 * FK * IC * NP].rearrange("p (j k n) -> p j k n", j=2, k=FK)
        sel = gflat[0:96, 0:32 * P // 2].bitcast(BF16).rearrange("p (n m) -> p n m", n=32)

        AREA = 30720
        area = sb("area", [P, AREA])
        a_off = [0]

        def carve(words, dt=F32):
            v = area[:, a_off[0]:a_off[0] + words]
            a_off[0] += words
            assert a_off[0] <= AREA, a_off[0]
            return v if dt == F32 else v.bitcast(dt)

        wl = carve(FK * D).rearrange("p (k d) -> p k d", k=FK)
        bcv = carve(T)
        parts = [carve(T // 2, BF16) for _ in range(3)]
        leftp = carve(NI * (L + 2)).rearrange("p (i l) -> p i l", i=NI)
        cv = carve(T).rearrange("p (i l) -> p i l", i=NI)
        cvF = cv.rearrange("p i l -> p (i l)")
        x_off = a_off[0]
        xs = carve(T)
        sright = carve(T)
        delta = carve(T)
        dx = carve(T)
        dz = carve(T)
        stacks = [carve(T // 2, BF16) for _ in range(4)]
        aneg = sb("aneg", [P, N])
        diag_d = sb("diag_d", [P, P])
        decay = [carve(QT).rearrange("p (i l) -> p i l", i=QI) for _ in range(2)]
        inject = [cvF[:, 0:QT], cvF[:, QT:2 * QT]]
        state = [cvF[:, 2 * QT:3 * QT], cvF[:, 3 * QT:4 * QT]]
        leftF = leftp.rearrange("p i l -> p (i l)")
        read = [leftF[:, 0:QT], leftF[:, QT:2 * QT]]
        bsb = [leftF[:, 2 * QT:3 * QT], leftF[:, 3 * QT:4 * QT]]
        gated = dz

        a_off[0] = 0
        up0s = carve(2 * 1536).rearrange("p (k n) -> p k n", k=2)
        dn0s = carve(12 * D).rearrange("p (j n) -> p j n", j=12)
        w_off = a_off[0]
        w1s = carve(2 * 4096).rearrange("p (k n) -> p k n", k=2)
        w2s = carve(32 * D).rearrange("p (j n) -> p j n", j=32)
        hid, hid2, hid3 = [carve(3 * CH).rearrange("p (b t) -> p b t", b=3) for _ in range(3)]
        cwT = carve(TP)[0:E8]
        free_off = a_off[0]
        a_off[0] = 0
        cc = carve(CH)
        qT = [carve(2 * CH).rearrange("p (a t) -> p a t", a=2) for _ in range(2)]
        kT = [carve(2 * CH).rearrange("p (a t) -> p a t", a=2) for _ in range(2)]
        prob = [carve(HEADS * L).rearrange("p (h l) -> p h l", h=HEADS) for _ in range(2)]
        oT = [carve(2 * CH).rearrange("p (a t) -> p a t", a=2) for _ in range(2)]
        osb = [carve(D).rearrange("p (a h d) -> p a h d", a=2, h=8) for _ in range(2)]
        assert a_off[0] <= w_off
        a_off[0] = free_off
        probT = carve(2 * KG * QR).rearrange("p (a c q) -> p a c q", a=2, c=KG)
        vm = [carve(4 * KG * VB).rearrange("p (i b d) -> p i b d", i=2, b=2 * KG) for _ in range(2)]
        rowm = carve(2 * HEADS).rearrange("p (j h) -> p j h", j=2)
        rows = carve(2 * KG * KG).rearrange("p (b h) -> p b h", b=2 * KG)
        kbd = [gflat[:, n * 32 * L:(n + 1) * 32 * L].rearrange("p (a i h l) -> p a i h l", a=2, i=2, h=8)
               for n in range(2)]
        ckv3 = [gflat[:, 64 * L + n * CH * KG:64 * L + (n + 1) * CH * KG].rearrange(
            "p (i r l) -> p i r l", i=IC, r=KG) for n in range(2)]

        ps = ctx.enter_context(nc.psum_tensor("ps", [P, 8, 512], F32))

        def S(name, part=None):
            o, w = AT[name]
            return sm[:, o:o + w]

        def W(name):
            o, w = WAT[name]
            return wd[:, o:o + w]

        ident = S("ident")
        w_up = W("w_up").rearrange("p (k n) -> p k n", k=2)
        gate_w = W("gate_w").rearrange("p (k n) -> p k n", k=2)
        w_r = W("w_r").rearrange("p (k n) -> p k n", k=2)
        w_dqkv = W("w_dqkv").rearrange("p (k n) -> p k n", k=2)
        w_u = W("w_u")
        w_o = W("w_o").rearrange("p (k n) -> p k n", k=2)

        small_in, dense_in, lin_in = sem("small_in"), sem("dense_in"), sem("lin_in")
        patches_in = [sem("patches_in0"), sem("patches_in1")]
        ffn0_in, ffn1_in = sem("ffn0_in"), sem("ffn1_in")
        consts_set = sem("consts_set")
        pos_ready = sem("pos_ready")
        embedded_ps, embedded = sem("embedded_ps"), sem("embedded")
        LNS = {}
        for ph in ("scan", "moe0", "attn", "moe1"):
            LNS[ph] = {n: sem(f"{ph}_{n}") for n in
                       ("mean", "centered", "squared", "var", "logvar", "rstd", "normed")}
        up_ps, up_left, up_right = sem("up_ps"), sem("up_left"), sem("up_right")
        conv_step, x_ready = sem("conv_step"), sem("x_ready")
        zbc_ps, z_copied, bc_copied = sem("zbc_ps"), sem("z_copied"), sem("bc_copied")
        soft_step, delta_ready, dx_ready = sem("soft_step"), sem("delta_ready"), sem("dx_ready")
        a_exp, a_ready = sem("a_exp"), sem("a_ready")
        split_step, stacks_in = sem("split_step"), sem("stacks_in")
        b_bcast, b_copied, c_bcast = sem("b_bcast"), sem("b_copied"), sem("c_bcast")
        decayed, injected, scanned = sem("decayed"), sem("injected"), sem("scanned")
        read_out, summed = sem("read_out"), sem("summed")
        y_gated = sem("y_gated")
        down_ps, scan_h = sem("down_ps"), sem("scan_h")
        MOE = {}
        for ph in ("moe0", "moe1"):
            MOE[ph] = {n: sem(f"{ph}_{n}") for n in
                       ("logits", "route", "routeT", "cwT", "gates_out", "gates_in0", "gates_in1",
                        "up", "relu", "hid", "down", "h", "gate1", "lg", "exp")}
        moe_out = sem("moe_out")
        cc_ps, cc_copied, ckv_rep = sem("cc_ps"), sem("cc_copied"), sem("ckv_rep")
        q_ps, k_ps, q_copied, k_copied = sem("q_ps"), sem("k_ps"), sem("q_copied"), sem("k_copied")
        k_spread = sem("k_spread")
        scores_ps, masked, maxed, shifted = sem("scores_ps"), sem("masked"), sem("maxed"), sem("shifted")
        exped, inverted = sem("exped"), sem("inverted")
        p_turned, p_copied = sem("p_turned"), sem("p_copied")
        v_ps, v_spread = sem("v_ps"), sem("v_spread")
        vm_ones = sem("vm_ones")
        o_ps, o_scaled, o_turned, o_copied = sem("o_ps"), sem("o_scaled"), sem("o_turned"), sem("o_copied")
        wo_ps, attn_h = sem("wo_ps"), sem("attn_h")

        def attention(eng, first, step, last):
            first()
            for cj in range(2):
                for p in range(4):
                    step(cj, cj, p, True, True)
            with eng.Fori(1, NCH // 2 - 1) as i:
                for cj in range(2):
                    for p in range(4):
                        step(i * 2 + cj, cj, p, True, True)
            for cj in range(2):
                for p in range(4):
                    step(NCH - 2 + cj, cj, p, False, cj == 0)
            last()

        def ahead(c, cj, p, d):
            return (c, cj, p + d) if p + d < 4 else (c + 1, 1 - cj, p + d - 4)

        block = ctx.enter_context(nc.Block())

        def pe_norm(pe, s):
            with pe.Fori(0, NCH // 2) as i:
                for j in range(2):
                    c = i * 2 + j
                    pe.wait_ge(s["centered"], c + 1)
                    for k in range(HALVES):
                        mm = nc.tensor.matmul(ps[:, j, 0:CH], ones[:], hF[:, k, ds(c * CH, CH)],
                                              start=(k == 0), stop=(k == HALVES - 1))
                    mm.then_inc(s["mean"], 1)
                for j in range(2):
                    c = i * 2 + j
                    pe.wait_ge(s["squared"], c + 1)
                    pe.wait_ge(s["logvar"], c + 1)
                    for k in range(HALVES):
                        mm = nc.tensor.matmul(ps[:, 2 + j, 0:CH], ones[:], sq[:, j, k, :],
                                              start=(k == 0), stop=(k == HALVES - 1))
                    mm.then_inc(s["var"], 1)

        def act_norm(act, s):
            nc.scalar.preload_act_table_set("natural_log_exp_and_others")
            act.sem_inc(s["logvar"], 2)
            with act.Fori(0, NCH // 2) as i:
                for j in range(2):
                    c = i * 2 + j
                    act.wait_ge(s["centered"], c + 3)
                    act.wait_ge(s["logvar"], c + 1)
                    nc.scalar.activation(sq[:, j, :, :], xn[:, :, ds(c * CH, CH)],
                                         ACT.Square).then_inc(s["squared"], 1)
                for j in range(2):
                    c = i * 2 + j
                    act.wait_ge(s["var"], c + 1)
                    act.wait_ge(s["normed"], c + 1)
                    nc.scalar.activation(rstd[:, j, :], ps[:, 2 + j, 0:CH], ACT.Ln,
                                         bias=S("eps")).then_inc(s["logvar"], 1)
                for j in range(2):
                    c = i * 2 + j
                    act.wait_ge(s["logvar"], c + 3)
                    nc.scalar.activation(rstd[:, j, :], rstd[:, j, :], ACT.Exp,
                                         scale=-0.5).then_inc(s["rstd"], 1)

        def dve_norm(dve, s):
            dve.sem_inc(s["centered"], 2)
            with dve.Fori(0, NCH // 2) as i:
                for j in range(2):
                    c = i * 2 + j
                    dve.wait_ge(s["mean"], c + 1)
                    nc.vector.tensor_tensor(xn[:, :, ds(c * CH, CH)], hF[:, :, ds(c * CH, CH)],
                                            bc(ps[:, j, 0:CH], 1, HALVES),
                                            ALU.subtract).then_inc(s["centered"], 1)
                for j in range(2):
                    c = i * 2 + j
                    dve.wait_ge(s["rstd"], c + 1)
                    dve.wait_ge(s["centered"], c + 3)
                    nc.vector.tensor_tensor(xn[:, :, ds(c * CH, CH)], xn[:, :, ds(c * CH, CH)],
                                            bc(rstd[:, j, :], 1, HALVES),
                                            ALU.mult).then_inc(s["normed"], 1)

        def pe_logits(pe, s, w):
            for t in range(TT):
                for k in range(HALVES):
                    mm = nc.tensor.matmul(ps[:, 0, t * E8:(t + 1) * E8], xn[:, k, t * P:(t + 1) * P],
                                          w[:, k, :], start=(k == 0), stop=(k == HALVES - 1))
            mm.then_inc(s["logits"], 1)

        def pe_turn_weights(pe, s, n_route, weights):
            pe.wait_ge(s["route"], n_route)
            for t in range(TT):
                mm = nc.tensor.transpose(ps[0:E8, 1 + t // 4, (t % 4) * P:(t % 4 + 1) * P],
                                         weights[:, t, :], ident)
            mm.then_inc(s["routeT"], 1)

        def dve_copy_weights(dve, s):
            dve.wait_ge(s["routeT"], 1)
            for b in range(5):
                n = min(512, TP - b * 512)
                nc.vector.tensor_copy(cwT[:, b * 512:b * 512 + n],
                                      ps[0:E8, 1 + b, 0:n]).then_inc(s["cwT"], 1)

        def dve_select(link, scores, k, out_):
            cmp_ = xs_cmp
            link(nc.vector.tensor_tensor(cmp_, bc(scores, 2, E8), bc(scores, 3, E8), ALU.is_gt))
            link(nc.vector.tensor_tensor(xs_eq, bc(scores, 2, E8), bc(scores, 3, E8), ALU.is_equal))
            earlier = S("earlier").rearrange("p (a b) -> p a b", a=E8)
            link(nc.vector.tensor_tensor(xs_eq, xs_eq, bc(earlier, 1, TT), ALU.mult))
            link(nc.vector.tensor_tensor(cmp_, cmp_, xs_eq, ALU.add))
            link(nc.vector.tensor_reduce(out_, cmp_, AX, ALU.add))
            link(nc.vector.tensor_scalar(out_, out_, float(k) - 0.5, None, ALU.is_lt))

        xs_cmp = gflat[:, 0:TT * 64].rearrange(
            "p (t a b) -> p t a b", t=TT, a=E8)
        xs_eq = gflat[:, TT * 64:TT * 128].rearrange(
            "p (t a b) -> p t a b", t=TT, a=E8)

        def pe_moe(pe, s, nt, up_w, dn_w, bias):
            pe.wait_ge(s["cwT"], 5)
            with pe.Fori(0, NCH // 2) as i:
                for cj in range(2):
                    c = i * 2 + cj
                    cs = ds(c * CH, CH)
                    for j in range(nt + 2):
                        if j < nt:
                            pe.wait_ge(s["relu"], c * nt + j + 2)
                            for k in range(HALVES):
                                mm = nc.tensor.matmul(ps[:, 5 + j % 3, 0:CH],
                                                      up_w[:, k, j * P:(j + 1) * P],
                                                      xn[:, k, cs], start=(k == 0), stop=(k == 1))
                            mm.then_inc(s["up"], 1)
                        if j == 0:
                            pe.wait_ge(s["h"], c + 1)
                            if bias:
                                for m in range(HALVES):
                                    nc.tensor.matmul(ps[:, 1 + 2 * cj + m, 0:CH],
                                                     b2s[:, m * P:(m + 1) * P], cwT[:, cs],
                                                     start=True, stop=False)
                        if j >= 2:
                            jj = j - 2
                            pe.wait_ge(s["hid"], c * nt + jj + 4)
                            for m in range(HALVES):
                                mm = nc.tensor.matmul(ps[:, 1 + 2 * cj + m, 0:CH],
                                                      dn_w[:, jj, m * P:(m + 1) * P],
                                                      hid2[:, jj % 3, :],
                                                      start=(jj == 0 and not bias),
                                                      stop=(jj == nt - 1))
                            if jj == nt - 1:
                                mm.then_inc(s["down"], 1)

        def act_exp(act, s, sign):
            act.wait_ge(s["lg"], 1)
            nc.scalar.activation(sc[:], lg[:], ACT.Exp, scale=sign).then_inc(s["exp"], 1)

        def act_moe(act, s, nt, bias):
            act.sem_inc(s["relu"], 3)
            with act.Fori(0, NCH // 2) as i:
                for cj in range(2):
                    c = i * 2 + cj
                    for j in range(nt):
                        act.wait_ge(s["up"], c * nt + j + 1)
                        act.wait_ge(s["hid"], c * nt + j + 2)
                        nc.scalar.activation(hid[:, j % 3, :], ps[:, 5 + j % 3, 0:CH], ACT.Relu,
                                             bias=(S("b1")[:, j:j + 1] if bias else 0.0)
                                             ).then_inc(s["relu"], 1)

        def dve_moe(dve, s, nt, squares, last):
            dve.sem_inc(s["hid"], 3)
            dve.sem_inc(s["h"], 2)
            with dve.Fori(0, NCH // 2) as i:
                for cj in range(2):
                    c = i * 2 + cj
                    cs = ds(c * CH, CH)
                    dve.wait_ge(s["gates_in0" if cj == 0 else "gates_in1"], i * 16 + 16)
                    for j in range(nt):
                        dve.wait_ge(s["relu"], c * nt + j + 4)
                        a = hid[:, j % 3, :]
                        if squares and j < E8:
                            nc.vector.tensor_tensor(hid3[:, j % 3, :], a, gbc[:, cj, j, :],
                                                    ALU.mult).then_inc(s["gate1"], 1)
                            dve.wait_ge(s["gate1"], c * E8 + j + 1)
                            g = hid3[:, j % 3, :]
                        elif squares:
                            g = a
                        else:
                            g = gbc[:, cj, j // 4, :]
                        nc.vector.tensor_tensor(hid2[:, j % 3, :], a, g, ALU.mult).then_inc(s["hid"], 1)
                    dve.wait_ge(s["down"], c + 1)
                    nc.vector.tensor_tensor(hF[:, :, cs], hF[:, :, cs],
                                            ps[:, 1 + 2 * cj:3 + 2 * cj, 0:CH],
                                            ALU.add).then_inc(s["h"], 1)

        def sp_gates(sp, s, last, n_per):
            sp.wait_ge(s["cwT"], 5)
            sp.dma_start(gates_dram[last], cwT[:, 0:T]).then_inc(s["gates_out"], 16)
            sp.wait_ge(s["gates_out"], 16)
            with sp.Fori(0, NCH // 2) as i:
                for cj in range(2):
                    c = i * 2 + cj
                    sp.wait_ge(s["h"], c + 1)
                    sp.dma_start(gbc[:, cj, :, :],
                                 gates_dram[last][:, ds(c * CH, CH)].partition_broadcast(P)
                                 ).then_inc(s["gates_in0" if cj == 0 else "gates_in1"], 16)

        @block.sync
        def _(sp):
            sp.dma_start(sm[:], small).then_inc(small_in, 16)
            sp.dma_start(wl, w_lin).then_inc(lin_in, 16)
            with sp.Fori(0, NCH // 2) as i:
                for j in range(2):
                    sp.wait_ge(embedded, (i * 2 + j) * 2 + 2)
                    sp.dma_start(xin[:, j, :, :], patches[ds(i * 2 + j, 1), :, :, :].rearrange(
                        "o p k n -> (o p) k n")).then_inc(patches_in[j], 16)
            sp.dma_start(wd[:], dense).then_inc(dense_in, 16)
            sp.dma_start(b2s[:], b2).then_inc(dense_in, 16)
            sp.wait_ge(split_step, 5)
            for g in range(4):
                for k in range(3):
                    sp.dma_start(stacks[g][32 * k:32 * k + 32, :],
                                 parts[k][32 * g:32 * g + 32, :]).then_inc(stacks_in, 16)
            sp.wait_ge(stacks_in, 16 * 12)
            sp.dma_start(up0s, up0).then_inc(ffn0_in, 16)
            sp.dma_start(dn0s, dn0).then_inc(ffn0_in, 16)
            sp.wait_ge(scan_h, NCH + 2)
            sp.dma_start(w1s, w1).then_inc(ffn1_in, 16)
            sp.dma_start(w2s, w2).then_inc(ffn1_in, 16)
            sp_gates(sp, MOE["moe0"], 0, 12)
            sp_gates(sp, MOE["moe1"], 1, 32)

        @block.gpsimd
        def _(pool):
            nc.gpsimd.memset(ones[:], 1.0 / D).then_inc(consts_set, 1)
            nc.gpsimd.memset(xn[:, :, T:TP], 0.0).then_inc(consts_set, 1)
            nc.gpsimd.memset(leftp, 0.0).then_inc(consts_set, 1)
            for j in range(2):
                nc.gpsimd.memset(decay[j], 0.0).then_inc(consts_set, 1)
            pool.wait_ge(small_in, 16)
            pool.wait_ge(embedded, 4 + 2 * NCH)
            nc.gpsimd.tensor_copy(sel, bc(S("row32")[0:96, :], 2, P)).then_inc(consts_set, 1)

            pool.sem_inc(injected, 2)
            pool.wait_ge(dx_ready, 1)
            for q in range(NQ):
                with pool.Fori(0, N // 2) as i:
                    for j in range(2):
                        k = q * N + i * 2 + j
                        pool.wait_ge(b_copied, k + 2)
                        pool.wait_ge(scanned, k + 1)
                        nc.gpsimd.tensor_tensor(inject[j], dx[:, q * QT:(q + 1) * QT], bsb[j],
                                                ALU.mult).then_inc(injected, 1)

            mask = S("head_of_row")
            pool.wait_ge(MOE["moe0"]["h"], NCH + 2)
            with pool.Fori(0, NCH // 2) as i:
                for cj in range(2):
                    c = i * 2 + cj
                    pool.wait_ge(k_copied, c + 1)
                    for p in range(4):
                        pool.wait_ge(scores_ps, c * 4 + p + 1)
                        for a in range(2):
                            for im in range(2):
                                t0 = (2 * p + im) * L
                                last = nc.gpsimd.tensor_tensor(
                                    kbd[p % 2][:, a, im, :, :], bc(kT[cj][:, a, t0:t0 + L], 1, 8),
                                    bc(mask, 2, L), ALU.mult)
                        last.then_inc(k_spread, 1)

            with pool.Fori(0, NCH) as c:
                pool.wait_ge(MOE["moe1"]["h"], c + 3)
                pool.dma_start(out[:, :, ds(c * CH, CH)], hF[:, :, ds(c * CH, CH)]
                               ).then_inc(moe_out, 16)
            pool.wait_ge(moe_out, 16 * NCH)

        @block.tensor
        def _(pe):
            pe.wait_ge(lin_in, 16)
            with pe.Fori(0, NCH // 2) as i:
                for j in range(2):
                    c = i * 2 + j
                    pe.wait_ge(patches_in[j], i * 16 + 16)
                    pe.wait_ge(embedded, c * 2 + 2)
                    for m in range(HALVES):
                        for k in range(FK):
                            mm = nc.tensor.matmul(ps[:, 2 * j + m, 0:IC * NP],
                                                  wl[:, k, m * P:(m + 1) * P], xin[:, j, k, :],
                                                  start=(k == 0), stop=(k == FK - 1))
                    mm.then_inc(embedded_ps, 1)

            pe.wait_ge(embedded, 4 + 2 * NCH)
            pe.wait_ge(consts_set, 5)
            pe.wait_ge(pos_ready, 6)
            pe_norm(pe, LNS["scan"])
            pe.wait_ge(dense_in, 32)
            with pe.Fori(0, NCH // 2) as i:
                for j in range(2):
                    c = i * 2 + j
                    pe.wait_ge(LNS["scan"]["normed"], c + 3)
                    pe.wait_ge(up_right, c + 1)
                    for m in range(2):
                        for k in range(HALVES):
                            mm = nc.tensor.matmul(ps[:, 4 + 2 * m + j, 0:CH],
                                                  w_up[:, k, m * P:(m + 1) * P],
                                                  xn[:, k, ds(c * CH, CH)],
                                                  start=(k == 0), stop=(k == 1))
                    mm.then_inc(up_ps, 1)
            with pe.Fori(0, NCH // 2) as i:
                for j in range(2):
                    c = i * 2 + j
                    pe.wait_ge(x_ready, 1)
                    pe.wait_ge(bc_copied, c + 1)
                    nc.tensor.matmul(ps[:, j, 0:CH], W("w_delta"), xs[:, ds(c * CH, CH)],
                                     start=True, stop=True)
                    nc.tensor.matmul(ps[:, 2 + j, 0:CH], W("w_bc"), xs[:, ds(c * CH, CH)],
                                     start=True, stop=True).then_inc(zbc_ps, 1)

            def row(stack, q, i, h, bank):
                return nc.tensor.matmul(ps[:, bank, 0:CH],
                                        sel[:, ds(i, 1), :].rearrange("p o m -> p (o m)"),
                                        stacks[stack][0:96, ds(q * QT + h * CH, CH)],
                                        start=True, stop=True)

            def spread_b(q, i, j):
                pe.wait_ge(b_copied, q * N + i * 2 + j + 1)
                for h in range(2):
                    mm = row(j, q, i, h, 2 + h)
                mm.then_inc(b_bcast, 1)

            def spread_c(q, i, j):
                pe.wait_ge(read_out, q * N + i * 2 + j + 1)
                for h in range(2):
                    mm = row(2 + j, q, i, h, 4 + 2 * j + h)
                mm.then_inc(c_bcast, 1)

            def sum_state(q, i, j, last=False):
                k = q * N + i * 2 + j
                pe.wait_ge(read_out, k + 3)
                for h in range(2):
                    mm = nc.tensor.matmul(ps[:, h, 0:CH], ident, read[j][:, h * CH:(h + 1) * CH],
                                          start=False, stop=last, skip_group_check=True)
                mm.then_inc(summed, 1)

            pe.wait_ge(stacks_in, 16 * 12)
            pe.wait_ge(a_ready, 2)
            pe.wait_ge(consts_set, 6)
            pe.sem_inc(summed, 2)
            pe.wait_ge(bc_copied, NCH + 2)
            pe.wait_ge(z_copied, NCH)
            with pe.Fori(0, NQ) as q:
                pe.wait_ge(y_gated, q + 1)
                for h in range(2):
                    nc.tensor.matmul(ps[:, h, 0:CH], diag_d[:], xs[:, ds(q * QT + h * CH, CH)],
                                     start=True, stop=False, skip_group_check=True)
                spread_b(q, 0, 0)
                spread_b(q, 0, 1)
                spread_c(q, 0, 0)
                spread_b(q, 1, 0)
                spread_c(q, 0, 1)
                with pe.Fori(1, N // 2 - 1) as i:
                    spread_b(q, i, 1)
                    spread_c(q, i, 0)
                    sum_state(q, i - 1, 0)
                    spread_b(q, i + 1, 0)
                    spread_c(q, i, 1)
                    sum_state(q, i - 1, 1)
                spread_b(q, N // 2 - 1, 1)
                spread_c(q, N // 2 - 1, 0)
                sum_state(q, N // 2 - 2, 0)
                spread_c(q, N // 2 - 1, 1)
                sum_state(q, N // 2 - 2, 1)
                sum_state(q, N // 2 - 1, 0)
                sum_state(q, N // 2 - 1, 1, last=True)
            pe.wait_ge(y_gated, NQ + 1)
            with pe.Fori(0, NCH // 2) as i:
                for j in range(2):
                    c = i * 2 + j
                    pe.wait_ge(scan_h, c + 1)
                    for m in range(2):
                        mm = nc.tensor.matmul(ps[:, 2 + 2 * j + m, 0:CH],
                                              W("w_down")[:, m * P:(m + 1) * P],
                                              gated[:, ds(c * CH, CH)], start=True, stop=True)
                    mm.then_inc(down_ps, 1)

            pe.wait_ge(scan_h, NCH + 2)
            pe_norm(pe, LNS["moe0"])
            pe.wait_ge(LNS["moe0"]["normed"], NCH + 2)
            pe_logits(pe, MOE["moe0"], gate_w)
            pe_turn_weights(pe, MOE["moe0"], 1, rt1)
            pe.wait_ge(ffn0_in, 32)
            pe_moe(pe, MOE["moe0"], 12, up0s, dn0s, False)

            pe.wait_ge(MOE["moe0"]["h"], NCH + 2)
            pe_norm(pe, LNS["attn"])
            pe.wait_ge(LNS["attn"]["normed"], NCH + 2)
            pe.sem_inc(scores_ps, 2)
            pe.sem_inc(p_turned, 2)
            pe.sem_inc(o_ps, 2)
            pe.sem_inc(o_turned, 2)
            pe.sem_inc(wo_ps, 2)

            def compress(c):
                if isinstance(c, int) and c in (1, 2):
                    pe.wait_ge(k_copied, c)
                elif not isinstance(c, int) or c > 2:
                    pe.wait_ge(attn_h, c - 2)
                for k in range(HALVES):
                    mm = nc.tensor.matmul(ps[:, 6, 0:CH], w_dqkv[:, k, :], xn[:, k, ds(c * CH, CH)],
                                          start=(k == 0), stop=(k == 1))
                mm.then_inc(cc_ps, 1)

            def queries(c):
                pe.wait_ge(cc_copied, c + 1)
                for m in range(2):
                    mm = nc.tensor.matmul(ps[:, 6 + m, 0:CH], w_u[0:64, m * P:(m + 1) * P],
                                          cc[0:64, :], start=True, stop=True)
                mm.then_inc(q_ps, 1)

            def keys(c):
                pe.wait_ge(q_copied, c + 1)
                for m in range(2):
                    mm = nc.tensor.matmul(ps[:, 6 + m, 0:CH], w_u[64:128, m * P:(m + 1) * P],
                                          cc[64:128, :], start=True, stop=True)
                mm.then_inc(k_ps, 1)

            def scores(c, cj, p):
                k = c * 4 + p
                pe.wait_ge(k_spread, k + 1)
                pe.wait_ge(masked, k + 1)
                for im in range(2):
                    t0 = (2 * p + im) * L
                    nq = 64 if im == 0 else L
                    for a in range(2):
                        mm = nc.tensor.matmul(ps[64 * im:64 * im + nq, a, 0:8 * L],
                                              qT[cj][:, a, t0:t0 + nq],
                                              kbd[p % 2][:, a, im, :, :].rearrange("p h l -> p (h l)"),
                                              start=True, stop=True)
                mm.then_inc(scores_ps, 1)

            def values(c, cj, p):
                k = c * 4 + p
                pe.wait_ge(ckv_rep, c + 1)
                pe.wait_ge(v_spread, k + 1)
                for im in range(2):
                    mm = nc.tensor.matmul(ps[0:KG * L, 4, im * D:(im + 1) * D],
                                          ckv3[cj][64:128, 2 * p + im, :, :].rearrange("p r l -> p (r l)"),
                                          w_u[64:128, D:2 * D], start=True, stop=True)
                mm.then_inc(v_ps, 1)

            def project(c, cj):
                pe.wait_ge(o_copied, c * 4 + 5)
                for m in range(2):
                    for k in range(2):
                        mm = nc.tensor.matmul(ps[:, 6 + m, 0:CH], w_o[:, k, m * P:(m + 1) * P],
                                              oT[cj][:, k, :], start=(k == 0), stop=(k == 1))
                mm.then_inc(wo_ps, 1)

            def pe_first():
                compress(0)
                queries(0)
                keys(0)
                compress(1)
                scores(0, 0, 0)
                scores(0, 0, 1)
                values(0, 0, 0)
                pe.wait_ge(vm_ones, 2)

            def pe_step(c, cj, p, more2, more1):
                k = c * 4 + p
                pe.wait_ge(exped, k + 1)
                pe.wait_ge(p_copied, k + 1)
                for a in range(2):
                    for b in range(KG):
                        h0 = 8 * a + min(KG * b, 8 - KG)
                        mm = nc.tensor.transpose(ps[0:KG * L, 2 + a, b * QR:(b + 1) * QR],
                                                 prob[p % 2][0:QR, h0:h0 + KG, :].rearrange(
                                                     "p h l -> p (h l)"), ident[0:QR, 0:QR])
                mm.then_inc(p_turned, 1)
                if more1 or p < 2:
                    scores(*ahead(c, cj, p, 2))
                if more1 and p == 1:
                    keys(c + 1)
                pe.wait_ge(p_copied, k + 2)
                pe.wait_ge(v_spread, k + 2)
                pe.wait_ge(o_copied, k + 1)
                for im in range(2):
                    nq = 64 if im == 0 else L
                    for ab in range(2 * KG):
                        mm = nc.tensor.matmul(ps[64 * im:64 * im + nq, 5, ab * VB:(ab + 1) * VB],
                                              probT[0:KG * L, ab // KG, ab % KG, 64 * im:64 * im + nq],
                                              vm[p % 2][0:KG * L, im, ab, :], start=True, stop=True)
                mm.then_inc(o_ps, 1)
                if more1 or p < 3:
                    values(*ahead(c, cj, p, 1))
                if more1 and p == 0:
                    queries(c + 1)
                if p == 1 and not (isinstance(c, int) and c == 0):
                    if more1:
                        pe.wait_ge(k_copied, c + 2)
                    else:
                        pe.wait_ge(attn_h, c - 1)
                    project(c - 1, 1 - cj)
                pe.wait_ge(o_scaled, k + 1)
                for a in range(2):
                    mm = nc.tensor.transpose(ps[:, 5, O_T + a * QR:O_T + (a + 1) * QR],
                                             osb[p % 2][0:QR, a, :, :].rearrange("p h d -> p (h d)"),
                                             ident[0:QR, 0:QR])
                mm.then_inc(o_turned, 1)
                if more2 and p == 3:
                    compress(c + 2)

            def pe_last():
                pe.wait_ge(attn_h, NCH - 1)
                project(NCH - 1, 1)

            attention(pe, pe_first, pe_step, pe_last)

            pe.wait_ge(attn_h, NCH)
            pe_norm(pe, LNS["moe1"])
            pe.wait_ge(LNS["moe1"]["normed"], NCH + 2)
            pe_logits(pe, MOE["moe1"], w_r)
            pe_turn_weights(pe, MOE["moe1"], 1, rt1)
            pe.wait_ge(ffn1_in, 32)
            pe_moe(pe, MOE["moe1"], 32, w1s, w2s, True)

        @block.scalar
        def _(act):
            act.wait_ge(small_in, 16)
            act_norm(act, LNS["scan"])
            nc.scalar.preload_act_table(ACT.Silu)
            act.sem_inc(up_right, 2)
            act.wait_ge(consts_set, 3)
            with act.Fori(0, NCH // 2) as i:
                for j in range(2):
                    c = i * 2 + j
                    act.wait_ge(up_ps, c + 1)
                    nc.scalar.activation(leftp[:, ds(c * IC, IC), 2:L + 2],
                                         ps[:, 4 + j, 0:CH].rearrange("p (i l) -> p i l", i=IC),
                                         ACT.Identity, bias=S("b_up")[:, 0:1]).then_inc(up_left, 1)
                    nc.scalar.activation(sright[:, ds(c * CH, CH)], ps[:, 6 + j, 0:CH], ACT.Silu,
                                         bias=S("b_up")[:, 1:2]).then_inc(up_right, 1)
            act.wait_ge(conv_step, 3)
            nc.scalar.activation(xs, cvF, ACT.Silu).then_inc(x_ready, 1)
            nc.scalar.preload_act_table_set("natural_log_exp_and_others")
            nc.scalar.activation(aneg[:], S("a_log"), ACT.Exp).then_inc(a_exp, 1)
            act.sem_inc(bc_copied, 2)
            with act.Fori(0, NCH // 2) as i:
                for j in range(2):
                    c = i * 2 + j
                    act.wait_ge(zbc_ps, c + 1)
                    nc.scalar.activation(dz[:, ds(c * CH, CH)], ps[:, j, 0:CH], ACT.Identity,
                                         bias=S("b_delta")).then_inc(z_copied, 1)
                    nc.scalar.activation(bcv[:, ds(c * CH, CH)], ps[:, 2 + j, 0:CH], ACT.Identity,
                                         bias=S("b_bc")).then_inc(bc_copied, 1)
            act.wait_ge(z_copied, NCH)
            nc.scalar.activation(delta, dz, ACT.Abs).then_inc(soft_step, 1)
            act.wait_ge(soft_step, 1)
            nc.scalar.activation(delta, delta, ACT.Exp, scale=-1.0).then_inc(soft_step, 1)
            act.wait_ge(soft_step, 2)
            nc.scalar.activation(delta, delta, ACT.Ln, bias=1.0).then_inc(soft_step, 1)

            act.sem_inc(b_copied, 1)
            act.wait_ge(delta_ready, 1)
            act.wait_ge(a_ready, 2)
            with act.Fori(0, NQ) as q:
                with act.Fori(0, N // 2) as i:
                    for j in range(2):
                        k = q * N + i * 2 + j
                        act.wait_ge(b_bcast, k + 1)
                        act.wait_ge(injected, k + 1)
                        nc.scalar.activation(bsb[j].rearrange("p (h t) -> p h t", h=2),
                                             ps[:, 2:4, 0:CH], ACT.Copy).then_inc(b_copied, 1)
                        act.wait_ge(scanned, k + 1)
                        nc.scalar.activation(decay[j][:, :, 1:L],
                                             delta.rearrange("p (i l) -> p i l", i=NI)[:, ds(q * QI, QI), 1:L],
                                             ACT.Exp, scale=aneg[:, ds(i + j * 32, 1)]).then_inc(decayed, 1)

            act_norm(act, LNS["moe0"])
            act_exp(act, MOE["moe0"], -1.0)
            act_moe(act, MOE["moe0"], 12, False)

            act_norm(act, LNS["attn"])
            act.sem_inc(p_copied, 1)
            act.sem_inc(o_copied, 1)

            def act_compress(c, cj):
                act.wait_ge(cc_ps, c + 1)
                nc.scalar.activation(cc, ps[:, 6, 0:CH], ACT.Copy).then_inc(cc_copied, 1)
                act.wait_ge(cc_copied, c + 1)
                nc.scalar.activation(ckv3[cj][64:128],
                                     bc(cc[64:128, :].rearrange("p (i l) -> p i l", i=IC), 2, KG),
                                     ACT.Copy).then_inc(ckv_rep, 1)

            def act_queries(c, cj):
                act.wait_ge(q_ps, c + 1)
                nc.scalar.activation(qT[cj], ps[:, 6:8, 0:CH], ACT.Copy,
                                     scale=DK ** -0.5).then_inc(q_copied, 1)

            def act_keys(c, cj):
                act.wait_ge(k_ps, c + 1)
                nc.scalar.activation(kT[cj], ps[:, 6:8, 0:CH], ACT.Copy).then_inc(k_copied, 1)

            def act_exp_scores(c, cj, p):
                k = c * 4 + p
                act.wait_ge(shifted, k + 1)
                pr = prob[p % 2][0:QR]
                nc.scalar.activation(pr, pr, ACT.Exp).then_inc(exped, 1)

            def act_first():
                act_compress(0, 0)
                act_queries(0, 0)
                act_keys(0, 0)
                act_compress(1, 1)
                act_exp_scores(0, 0, 0)

            def act_step(c, cj, p, more2, more1):
                k = c * 4 + p
                act.wait_ge(p_turned, k + 3)
                act.wait_ge(o_ps, k + 2)
                nc.scalar.activation(probT[0:KG * L].rearrange("p a c q -> p a (c q)"),
                                     ps[0:KG * L, 2:4, 0:KG * QR], ACT.Copy).then_inc(p_copied, 1)
                if more1 and p == 1:
                    act_keys(c + 1, 1 - cj)
                if more1 or p < 3:
                    act_exp_scores(*ahead(c, cj, p, 1))
                if more1 and p == 0:
                    act_queries(c + 1, 1 - cj)
                act.wait_ge(o_turned, k + 3)
                if p == 0:
                    act.wait_ge(wo_ps, c + 1)
                o = ps[:, 5, O_T:O_T + 2 * QR].rearrange("p (a q) -> p a q", a=2)
                dst = oT[cj].rearrange("p a (i q) -> p a i q", i=IC)
                nc.scalar.activation(dst[:, :, 2 * p, :], o[:, :, 0:L], ACT.Copy)
                nc.scalar.activation(dst[:, :, 2 * p + 1, :], o[:, :, 64:QR],
                                     ACT.Copy).then_inc(o_copied, 1)
                if more2 and p == 3:
                    act_compress(c + 2, cj)

            attention(act, act_first, act_step, lambda: None)

            act_norm(act, LNS["moe1"])
            act_exp(act, MOE["moe1"], 1.0)
            act_moe(act, MOE["moe1"], 32, True)

        @block.vector
        def _(dve):
            linked = [0]
            chain = sem("dve_chain")

            def link(ins):
                linked[0] += 1
                ins.then_inc(chain, 1)
                dve.wait_ge(chain, linked[0])

            dve.wait_ge(small_in, 16)
            for m in range(HALVES):
                pos = S("pos").rearrange("p (a l) -> p a l", a=2)[:, m, :]
                nc.vector.tensor_scalar(posb[:, m, 1:L], pos[:, 1:L], S("b_lin")[:, m:m + 1], None,
                                        ALU.add).then_inc(pos_ready, 1)
                nc.vector.tensor_tensor(posb[:, m, 0:1], pos[:, 0:1], S("cls")[:, m:m + 1],
                                        ALU.add).then_inc(pos_ready, 1)
            dve.wait_ge(pos_ready, 4)
            for m in range(HALVES):
                nc.vector.tensor_copy(hT[:, m, :, 0], posb[:, m, 0:1].broadcast_to([P, NI])
                                      ).then_inc(pos_ready, 1)
            dve.sem_inc(embedded, 4)
            with dve.Fori(0, NCH // 2) as i:
                for j in range(2):
                    c = i * 2 + j
                    dve.wait_ge(embedded_ps, c + 1)
                    for m in range(HALVES):
                        nc.vector.tensor_tensor(hT[:, m, ds(c * IC, IC), 1:L],
                                                ps[:, 2 * j + m, 0:IC * NP].rearrange("p (i l) -> p i l", i=IC),
                                                bc(posb[:, m, 1:L], 1, IC), ALU.add).then_inc(embedded, 1)

            dve.sem_inc(LNS["scan"]["normed"], 2)
            dve_norm(dve, LNS["scan"])
            dve.wait_ge(up_left, NCH)
            w = S("conv_w")
            nc.vector.tensor_scalar(cv, leftp[:, :, 0:L], w[:, 0:1], S("conv_b"), ALU.mult,
                                    ALU.add).then_inc(conv_step, 1)
            for s_ in (1, 2):
                dve.wait_ge(conv_step, s_)
                nc.vector.scalar_tensor_tensor(out=cv, in0=leftp[:, :, s_:L + s_], scalar=w[:, s_:s_ + 1],
                                               in1=cv, op0=ALU.mult, op1=ALU.add).then_inc(conv_step, 1)
            dve.wait_ge(a_exp, 1)
            nc.vector.tensor_scalar(aneg[:], aneg[:], -1.0, None, ALU.mult).then_inc(a_ready, 1)
            nc.vector.tensor_scalar(diag_d[:], ident, S("d_skip"), None, ALU.mult).then_inc(a_ready, 1)
            dve.wait_ge(bc_copied, NCH + 2)
            nc.vector.tensor_copy(parts[0], bcv).then_inc(split_step, 1)
            dve.wait_ge(split_step, 1)
            nc.vector.tensor_tensor(bcv, bcv, parts[0], ALU.subtract).then_inc(split_step, 1)
            dve.wait_ge(split_step, 2)
            nc.vector.tensor_copy(parts[1], bcv).then_inc(split_step, 1)
            dve.wait_ge(split_step, 3)
            nc.vector.tensor_tensor(bcv, bcv, parts[1], ALU.subtract).then_inc(split_step, 1)
            dve.wait_ge(split_step, 4)
            nc.vector.tensor_copy(parts[2], bcv).then_inc(split_step, 1)
            dve.wait_ge(soft_step, 3)
            nc.vector.scalar_tensor_tensor(out=delta, in0=dz, scalar=0.0, in1=delta, op0=ALU.max,
                                           op1=ALU.add).then_inc(delta_ready, 1)
            dve.wait_ge(delta_ready, 1)
            dve.wait_ge(x_ready, 1)
            nc.vector.tensor_tensor(dx, delta, xs, ALU.mult).then_inc(dx_ready, 1)

            dve.sem_inc(scanned, 2)
            dve.sem_inc(read_out, 2)
            dve.sem_inc(y_gated, 1)
            with dve.Fori(0, NQ) as q:
                with dve.Fori(0, N // 2) as i:
                    for j in range(2):
                        k = q * N + i * 2 + j
                        dve.wait_ge(decayed, k + 1)
                        dve.wait_ge(injected, k + 3)
                        dve.wait_ge(read_out, k + 1)
                        nc.vector.tensor_tensor_scan(state[j], decay[j].rearrange("p i l -> p (i l)"),
                                                     inject[j], 0.0, ALU.mult, ALU.add).then_inc(scanned, 1)
                        dve.wait_ge(scanned, k + 3)
                        dve.wait_ge(c_bcast, k + 1)
                        dve.wait_ge(summed, k + 1)
                        nc.vector.tensor_tensor(read[j].rearrange("p (h t) -> p h t", h=2),
                                                state[j].rearrange("p (h t) -> p h t", h=2),
                                                ps[:, 4 + 2 * j:6 + 2 * j, 0:CH],
                                                ALU.mult).then_inc(read_out, 1)
                dve.wait_ge(summed, q * N + N + 2)
                nc.vector.tensor_tensor(
                    gated[:, ds(q * QT, QT)].rearrange("p (h t) -> p h t", h=2), ps[:, 0:2, 0:CH],
                    sright[:, ds(q * QT, QT)].rearrange("p (h t) -> p h t", h=2),
                    ALU.mult).then_inc(y_gated, 1)
            dve.sem_inc(scan_h, 2)
            with dve.Fori(0, NCH // 2) as i:
                for j in range(2):
                    c = i * 2 + j
                    cs = ds(c * CH, CH)
                    dve.wait_ge(down_ps, c + 1)
                    for m in range(2):
                        mm = nc.vector.scalar_tensor_tensor(
                            out=hF[:, m, cs], in0=ps[:, 2 + 2 * j + m, 0:CH],
                            scalar=S("b_down")[:, m:m + 1], in1=hF[:, m, cs], op0=ALU.add, op1=ALU.add)
                    mm.then_inc(scan_h, 1)

            dve.sem_inc(LNS["moe0"]["normed"], 2)
            dve_norm(dve, LNS["moe0"])
            s = MOE["moe0"]
            dve.wait_ge(s["logits"], 1)
            lgp = ps[:, 0, 0:TT * E8].rearrange("p (t e) -> p t e", t=TT)
            nc.vector.tensor_copy(lg[:], lgp).then_inc(s["lg"], 1)
            dve.wait_ge(s["exp"], 1)
            link(nc.vector.tensor_scalar(sc[:], sc[:], 1.0, None, ALU.add))
            link(nc.vector.reciprocal(sc[:], sc[:]))
            link(nc.vector.tensor_tensor(rt2[:], sc[:], bc(S("gate_b"), 1, TT), ALU.add))
            g4 = rt2[:].rearrange("p t (g e) -> p t g e", g=2)
            link(nc.vector.tensor_tensor(pairs[:, :, :, 0:3], g4[:, :, :, 0:3], g4[:, :, :, 1:4], ALU.add))
            link(nc.vector.tensor_tensor(pairs[:, :, :, 3:5], g4[:, :, :, 0:2], g4[:, :, :, 2:4], ALU.add))
            link(nc.vector.tensor_tensor(pairs[:, :, :, 5:6], g4[:, :, :, 0:1], g4[:, :, :, 3:4], ALU.add))
            link(nc.vector.tensor_reduce(gsum[:], pairs[:], AX, ALU.max))
            link(nc.vector.tensor_tensor(gsel[:, :, 0:1], gsum[:, :, 0:1], gsum[:, :, 1:2], ALU.is_ge))
            link(nc.vector.tensor_scalar(gsel[:, :, 1:2], gsel[:, :, 0:1], -1.0, 1.0, ALU.mult, ALU.add))
            link(nc.vector.tensor_tensor(g4, g4, bc(gsel[:], 3, 4), ALU.mult))
            dve_select(link, rt2[:], 2, rt1[:])
            link(nc.vector.tensor_tensor(rt1[:], rt1[:], sc[:], ALU.mult))
            link(nc.vector.tensor_reduce(red[:], rt1[:], AX, ALU.add))
            link(nc.vector.tensor_scalar(red[:], red[:], 1e-20, None, ALU.add))
            link(nc.vector.reciprocal(red[:], red[:]))
            link(nc.vector.tensor_tensor(rt1[:], rt1[:], bc(red[:], 2, E8), ALU.mult))
            nc.vector.tensor_scalar(rt1[:], rt1[:], 2.5, None, ALU.mult).then_inc(s["route"], 1)
            dve_copy_weights(dve, s)
            dve_moe(dve, s, 12, True, False)

            dve.sem_inc(LNS["attn"]["normed"], 2)
            dve_norm(dve, LNS["attn"])
            dve.sem_inc(masked, 1)
            dve.sem_inc(v_spread, 1)
            head_of = S("v_mask")[0:KG * L]
            for n in range(2):
                nc.vector.tensor_copy(
                    vm[n][0:KG * L].rearrange("p i b d -> p (i b) d")[:, :, KG * DK:VB],
                    bc(head_of[:, KG * DK:VB], 1, 4 * KG)).then_inc(vm_ones, 1)

            def soften(c, cj, p):
                k = c * 4 + p
                pr = prob[p % 2][0:QR]
                dve.wait_ge(scores_ps, k + 3)
                dve.wait_ge(p_turned, k + 1)
                nc.vector.tensor_tensor(pr.rearrange("p (a h) l -> p a h l", a=2),
                                        ps[0:QR, 0:2, 0:8 * L].rearrange("p a (h l) -> p a h l", h=8),
                                        bc(bc(S("causal")[0:QR], 1, 8), 1, 2),
                                        ALU.add).then_inc(masked, 1)
                dve.wait_ge(masked, k + 2)
                nc.vector.tensor_reduce(rowm[0:QR, p % 2, :], pr, AX, ALU.max).then_inc(maxed, 1)
                dve.wait_ge(maxed, k + 1)
                nc.vector.tensor_tensor(pr, pr, bc(rowm[0:QR, p % 2, :], 2, L),
                                        ALU.subtract).then_inc(shifted, 1)

            def spread_values(c, cj, p):
                k = c * 4 + p
                dve.wait_ge(v_ps, k + 1)
                dve.wait_ge(o_ps, k + 1)
                v = ps[0:KG * L, 4, 0:2 * D].rearrange("p (x d) -> p x d", x=4)
                o = vm[p % 2][0:KG * L].rearrange("p i (a b) d -> p (i a) b d", a=2)
                w3 = KG * DK
                nc.vector.tensor_tensor(o[:, :, 0:2, 0:w3],
                                        v[:, :, 0:2 * w3].rearrange("p x (b d) -> p x b d", b=2),
                                        bc(bc(head_of[:, 0:w3], 1, 2), 1, 4), ALU.mult)
                nc.vector.tensor_tensor(o[:, :, 2, 0:w3], v[:, :, P - w3:P],
                                        bc(head_of[:, 0:w3], 1, 4), ALU.mult).then_inc(v_spread, 1)

            def scale_outputs(c, cj, p):
                k = c * 4 + p
                dve.wait_ge(o_ps, k + 3)
                o = ps[0:QR, 5, 0:2 * KG * VB].rearrange("p (x d) -> p x d", x=2 * KG)
                nc.vector.reciprocal(rows[0:QR], o[:, :, KG * DK:VB]).then_inc(inverted, 1)
                dve.wait_ge(inverted, k + 1)
                dve.wait_ge(o_turned, k + 1)
                o = o[:, :, 0:KG * DK].rearrange("p (a b) (h d) -> p a b h d", a=2, h=KG)
                inv = rows[0:QR].rearrange("p (a b) h -> p a b h", a=2)
                for b in range(KG):
                    h0 = min(KG * b, 8 - KG)
                    skip = KG * b - h0
                    ins = nc.vector.tensor_tensor(osb[p % 2][0:QR, :, KG * b:h0 + KG, :],
                                                  o[:, :, b, skip:KG, :],
                                                  bc(inv[:, :, b, skip:KG], 3, DK), ALU.mult)
                ins.then_inc(o_scaled, 1)

            def add_projected(c):
                dve.wait_ge(wo_ps, c + 3)
                nc.vector.tensor_tensor(hF[:, :, ds(c * CH, CH)], hF[:, :, ds(c * CH, CH)],
                                        ps[:, 6:8, 0:CH], ALU.add).then_inc(attn_h, 1)

            def dve_first():
                soften(0, 0, 0)
                spread_values(0, 0, 0)

            def dve_step(c, cj, p, more2, more1):
                if more1 or p < 3:
                    soften(*ahead(c, cj, p, 1))
                scale_outputs(c, cj, p)
                if more1 or p < 3:
                    spread_values(*ahead(c, cj, p, 1))
                if p == 1 and not (isinstance(c, int) and c == 0):
                    add_projected(c - 1)

            attention(dve, dve_first, dve_step, lambda: add_projected(NCH - 1))

            dve.sem_inc(LNS["moe1"]["normed"], 2)
            dve_norm(dve, LNS["moe1"])
            s = MOE["moe1"]
            dve.wait_ge(s["logits"], 1)
            link(nc.vector.tensor_tensor(lg[:], lgp, bc(S("b_r"), 1, TT), ALU.add))
            link(nc.vector.tensor_reduce(red[:], lg[:], AX, ALU.max))
            nc.vector.tensor_tensor(lg[:], lg[:], bc(red[:], 2, E8), ALU.subtract).then_inc(s["lg"], 1)
            dve.wait_ge(s["exp"], 1)
            link(nc.vector.tensor_reduce(red[:], sc[:], AX, ALU.add))
            link(nc.vector.reciprocal(red[:], red[:]))
            link(nc.vector.tensor_tensor(sc[:], sc[:], bc(red[:], 2, E8), ALU.mult))
            dve_select(link, sc[:], 1, rt1[:])
            nc.vector.tensor_tensor(rt1[:], rt1[:], sc[:], ALU.mult).then_inc(s["route"], 1)
            dve_copy_weights(dve, s)
            dve_moe(dve, s, 32, False, True)


def kernel(**inputs):
    import numpy as np
    import concourse.bacc as bacc
    from concourse.bass_utils import run_bass_kernel_spmd

    g = {k: np.asarray(v) for k, v in inputs.items()}

    def rows(a, k):
        return np.ascontiguousarray(a.reshape(k, P, -1).transpose(1, 0, 2))

    def cols(v):
        return v.reshape(-1, P).T

    x = g["x"].reshape(NCH, IC, 3, 6, 16, 6, 16).transpose(0, 2, 4, 6, 1, 3, 5)
    x = x.reshape(NCH, FK, P, IC * NP).transpose(0, 2, 1, 3)

    row = np.arange(P)
    eye = np.eye(P, dtype=np.float32)
    head_of_row = (row[:, None] // DK == np.arange(E8)[None]).astype(np.float32)
    of = np.concatenate([np.arange(KG * DK) // DK, np.arange(KG)])
    v_mask = (np.minimum(row // L, KG)[:, None] == of[None]).astype(np.float32)
    causal = np.where(np.arange(L)[None] <= (row % 64)[:, None], 0.0, -1e30).astype(np.float32)
    earlier = np.tile((np.arange(E8)[None] < np.arange(E8)[:, None]).astype(np.float32).reshape(1, -1), (P, 1))
    row32 = (row[:, None] % 32 == np.arange(32)[None]).astype(np.float32)
    pieces = {
        "pos": rows(g["L0_tok_position_embeddings"][0].T, 2).reshape(P, -1),
        "b_lin": cols(g["L0_tok_b_lin"]), "cls": cols(g["L0_tok_class_token"].reshape(-1)),
        "b_up": cols(g["L0_attn_b_up"]), "conv_w": g["L0_attn_conv_w"],
        "conv_b": cols(g["L0_attn_conv_b"]), "b_delta": cols(g["L0_attn_b_delta"]),
        "b_bc": cols(np.concatenate([g["L0_attn_b_B"], g["L0_attn_b_C"]])),
        "a_log": g["L0_attn_A_log"], "d_skip": cols(g["L0_attn_D_skip"]),
        "b_down": cols(g["L0_attn_b_down"]),
        "gate_b": np.broadcast_to(g["L0_ffn_gate_bias"][None], (P, E8)),
        "b_r": np.broadcast_to(g["L1_ffn_br"][None], (P, E8)),
        "b1": cols(g["L1_ffn_b1"].reshape(-1)), "ident": eye, "head_of_row": head_of_row,
        "v_mask": v_mask, "causal": causal, "earlier": earlier, "row32": row32,
        "eps": np.full((P, 1), EPS, np.float32),
    }
    for n, w in SMALL:
        assert pieces[n].shape == (P, w), (n, pieces[n].shape)
    zero = np.zeros((64, D), np.float32)
    dense = {
        "w_up": rows(g["L0_attn_W_up"], 2), "w_delta": g["L0_attn_W_delta"],
        "w_bc": np.concatenate([g["L0_attn_W_B"], g["L0_attn_W_C"]], axis=1),
        "w_down": g["L0_attn_W_down"], "gate_w": rows(g["L0_ffn_gate_weight"].T, 2),
        "w_dqkv": rows(np.concatenate([g["L1_attn_W_dq"], g["L1_attn_W_dkv"]], axis=1), 2),
        "w_u": np.concatenate([np.concatenate([g["L1_attn_W_uq"], zero], axis=1),
                               np.concatenate([g["L1_attn_W_uk"], g["L1_attn_W_uv"]], axis=1)]),
        "w_o": rows(g["L1_attn_W_o"], 2), "w_r": rows(g["L1_ffn_Wr"], 2),
    }
    arrays = {
        "small": np.concatenate([pieces[n] for n, _ in SMALL], axis=1),
        "dense": np.concatenate([dense[n].reshape(P, -1) for n, _ in DENSE], axis=1),
        "patches": x,
        "w_lin": rows(g["L0_tok_W_lin"].T, FK),
        "up0": rows(np.concatenate([g["L0_ffn_up_weights"].reshape(1024, D), g["L0_ffn_shared_up_weight"]]).T, 2),
        "dn0": np.concatenate([g["L0_ffn_down_weights"].transpose(0, 2, 1),
                               g["L0_ffn_shared_down_weight"].T.reshape(4, P, D)]).transpose(1, 0, 2),
        "w1": rows(g["L1_ffn_W1"].transpose(1, 0, 2).reshape(D, -1), 2),
        "w2": g["L1_ffn_W2"].reshape(32, P, D).transpose(1, 0, 2),
        "b2": g["L1_ffn_b2"],
    }
    arrays = {f"in_{k}": np.ascontiguousarray(v) for k, v in arrays.items()}
    nc = bacc.Bacc("TRN2", target_bir_lowering=False, num_devices=1)
    args = [nc.dram_tensor(k, v.shape, F32, kind="ExternalInput").ap() for k, v in arrays.items()]
    gates = nc.dram_tensor("gates", (2, E8, T), F32, kind="Internal").ap()
    res = nc.dram_tensor("out_h", (P, HALVES, T), F32, kind="ExternalOutput").ap()
    build(nc, *args, gates, res)
    got = run_bass_kernel_spmd(nc, [arrays], core_ids=[0]).results[0]["out_h"]
    return np.ascontiguousarray(got.transpose(1, 0, 2).reshape(D, NI, L).transpose(1, 2, 0))
```

```python
from contextlib import ExitStack

import concourse.bass as bass
from concourse import mybir

P = 128
NI, L = 64, 37
NP = L - 1
T = NI * L
IC = 8
CH = IC * L
NCH = NI // IC
D, HALVES = 256, 2
FK = 6
N = 64
NQ = 4
QI = NI // NQ
POOL_SPLIT = (1, 5)
DVE_SPLIT = tuple(c for c in range(NCH) if c not in POOL_SPLIT)
QT = QI * L
TT = 19
TP = TT * P
E8 = 8
EF = 2
HEADS, DK = 16, 16
KG = 3
QR = 64 + L
O_T = 2 * KG * (KG * DK + KG)
VB = KG * DK + KG
EPS = 1e-5

HID1 = 512
ST = T // P + E8
assert ST % 4 == 2 and ST * P >= (T + E8 * (P - 1)) // P * P
ROW = 2 * D + 2
NR = 5
NOBODY = 1 << 30

F32, BF16, I32 = mybir.dt.float32, mybir.dt.bfloat16, mybir.dt.int32
ALU = mybir.AluOpType
ACT = mybir.ActivationFunctionType
AX = mybir.AxisListType.X
ds = bass.ds

SMALL = [("pos", 2 * L), ("b_lin", 2), ("cls", 2), ("b_up", 2), ("conv_w", 3), ("conv_b", 1),
         ("b_delta", 1), ("b_bc", 1), ("a_log", N), ("d_skip", 1), ("b_down", 2), ("gate_b", E8),
         ("b_r", E8), ("ident", P), ("head_of_row", E8), ("v_mask", VB),
         ("causal", L), ("rank", E8), ("row32", 32), ("eps", 1),
         ("before", P), ("not_first", E8 * TT), ("tile_ends", TT), ("one8", E8), ("slot_tile", ST),
         ("real", TT)]
AT = {}
_n = 0
for _name, _w in SMALL:
    AT[_name] = (_n, _w)
    _n += _w
NSMALL = _n

DENSE = [("w_up", 512), ("w_delta", 128), ("w_bc", 128), ("w_down", 256), ("gate_w", 16),
         ("w_dqkv", 256), ("w_u", 512), ("w_o", 512), ("w_r", 16)]
WAT = {}
_n = 0
for _name, _w in DENSE:
    WAT[_name] = (_n, _w)
    _n += _w
NDENSE = _n


def bc(ap, axis, n):
    ap = ap.unsqueeze(axis)
    shape = list(ap.shape)
    shape[axis] = n
    return ap.broadcast_to(shape)


def build(nc, small, dense, patches, w_lin, up0, dn0, w1, w2, b1, b2, gates_dram, slots, out):
    with ExitStack() as ctx:
        def sb(name, shape, dt=F32):
            return ctx.enter_context(nc.sbuf_tensor(name, shape, dt))

        def sem(name):
            return ctx.enter_context(nc.semaphore(name))

        hT = sb("hT", [P, HALVES, NI, L])
        hF = hT[:].rearrange("p a i l -> p a (i l)")
        xn = sb("xn", [P, HALVES, TP])
        sm = sb("sm", [P, NSMALL])
        wd = sb("wd", [P, NDENSE])
        ones = sb("ones", [P, P])
        sq = sb("sq", [P, 2, HALVES, CH])
        rstd = sb("rstd", [P, 2, CH])
        posb = sb("posb", [P, HALVES, L])
        lg = sb("lg", [P, TT, E8])
        sc = sb("sc", [P, TT, E8])
        rt1 = sb("rt1", [P, TT, E8])
        rt2 = sb("rt2", [P, TT, E8])
        rt2b = sb("rt2b", [P, TT, E8])
        pairs = sb("pairs", [P, TT, 2, 6])
        gsum = sb("gsum", [P, TT, 2])
        gsel = sb("gsel", [P, TT, 2])
        red = sb("red", [P, TT])

        gbc = sb("gbc", [P, 2, E8, CH])
        gflat = gbc[:].rearrange("p a e t -> p (a e t)")
        xin = gflat[:, 0:2 * FK * IC * NP].rearrange("p (j k n) -> p j k n", j=2, k=FK)
        sel = gflat[0:96, 0:32 * P // 2].bitcast(BF16).rearrange("p (n m) -> p n m", n=32)

        AREA = 30720
        area = sb("area", [P, AREA])
        a_off = [0]

        def carve(words, dt=F32):
            v = area[:, a_off[0]:a_off[0] + words]
            a_off[0] += words
            assert a_off[0] <= AREA, a_off[0]
            return v if dt == F32 else v.bitcast(dt)

        wl = carve(FK * D).rearrange("p (k d) -> p k d", k=FK)
        bcv = carve(T)
        parts = [carve(T // 2, BF16) for _ in range(3)]
        leftp = carve(NI * (L + 2)).rearrange("p (i l) -> p i l", i=NI)
        cv = carve(T).rearrange("p (i l) -> p i l", i=NI)
        cvF = cv.rearrange("p i l -> p (i l)")
        xs = carve(T)
        sright = carve(T)
        delta = carve(T)
        dx = carve(T)
        dz = carve(T)
        stacks = [carve(T // 2, BF16) for _ in range(4)]
        aneg = sb("aneg", [P, N])
        diag_d = sb("diag_d", [P, P])
        decay = [carve(QT).rearrange("p (i l) -> p i l", i=QI) for _ in range(2)]
        inject = [cvF[:, 0:QT], cvF[:, QT:2 * QT]]
        state = [cvF[:, 2 * QT:3 * QT], cvF[:, 3 * QT:4 * QT]]
        leftF = leftp.rearrange("p i l -> p (i l)")
        read = [leftF[:, 0:QT], leftF[:, QT:2 * QT]]
        bsb = [leftF[:, 2 * QT:3 * QT], leftF[:, 3 * QT:4 * QT]]
        gated = dz
        empty = carve(ROW)

        a_off[0] = 0
        up0s = carve(2 * 1536).rearrange("p (k n) -> p k n", k=2)
        dn0s = carve(12 * D).rearrange("p (j n) -> p j n", j=12)
        w_off = a_off[0]
        w1s = carve(2 * 4096).rearrange("p (k n) -> p k n", k=2)
        w2s = carve(32 * D).rearrange("p (j n) -> p j n", j=32)
        hid, hid2, hid3 = [carve(3 * CH).rearrange("p (b t) -> p b t", b=3) for _ in range(3)]
        cwT = carve(TP)[0:E8]
        free_off = a_off[0]
        a_off[0] = 0
        cc = carve(CH)
        qT = [carve(2 * CH).rearrange("p (a t) -> p a t", a=2) for _ in range(2)]
        kT = [carve(2 * CH).rearrange("p (a t) -> p a t", a=2) for _ in range(2)]
        prob = [carve(HEADS * L).rearrange("p (h l) -> p h l", h=HEADS) for _ in range(2)]
        oT = [carve(2 * CH).rearrange("p (a t) -> p a t", a=2) for _ in range(2)]
        osb = [carve(D).rearrange("p (a h d) -> p a h d", a=2, h=8) for _ in range(2)]
        assert a_off[0] <= w_off
        a_off[0] = free_off
        probT = carve(2 * KG * QR).rearrange("p (a c q) -> p a c q", a=2, c=KG)
        vm = [carve(4 * KG * VB).rearrange("p (i b d) -> p i b d", i=2, b=2 * KG) for _ in range(2)]
        rowm = carve(2 * HEADS).rearrange("p (j h) -> p j h", j=2)
        rows = carve(2 * KG * KG).rearrange("p (b h) -> p b h", b=2 * KG)
        kbd = [gflat[:, n * 32 * L:(n + 1) * 32 * L].rearrange("p (a i h l) -> p a i h l", a=2, i=2, h=8)
               for n in range(2)]
        ckv3 = [gflat[:, 64 * L + n * CH * KG:64 * L + (n + 1) * CH * KG].rearrange(
            "p (i r l) -> p i r l", i=IC, r=KG) for n in range(2)]

        a_off[0] = 0
        token_row = [area[:, n * ROW:(n + 1) * ROW] for n in range(NR)]
        slot_row = [carve(ROW) for _ in range(4)]
        slot_xT = [carve(D).rearrange("p (k n) -> p k n", k=2) for _ in range(2)]
        hid_rT = [carve(HID1).rearrange("p (k n) -> p k n", k=4) for _ in range(2)]
        out_row = [carve(D) for _ in range(2)]
        assert max(a_off[0], NR * ROW) <= w_off
        a_off[0] = w_off + 2 * 32 * D
        b1r = carve(E8 * HID1)
        b2r = carve(E8 * D)
        hid_b = [carve(HID1) for _ in range(2)]
        hid_r = [carve(HID1) for _ in range(2)]
        token = sb("token", [P, TT], I32)
        slot_i = sb("slot_i", [P, TT], I32)
        slot_token = sb("slot_token", [P, ST], I32)
        expert_i = sb("expert_i", [P, ST], I32)
        gate = sb("gate", [P, TT])
        slot_f = sb("slot_f", [P, TT])
        tot = sb("tot", [P, E8, TT])
        run = sb("run", [P, E8, TT])
        ntile = sb("ntile", [P, 3, E8])
        spare = gflat[:, TT * 128:TT * 128 + ST * E8]
        spare2 = gflat[:, TT * 128 + ST * E8:TT * 128 + ST * E8 + ST]

        ps = ctx.enter_context(nc.psum_tensor("ps", [P, 8, 512], F32))

        def S(name):
            o, w = AT[name]
            return sm[:, o:o + w]

        def W(name):
            o, w = WAT[name]
            return wd[:, o:o + w]

        ident = S("ident")
        w_up = W("w_up").rearrange("p (k n) -> p k n", k=2)
        gate_w = W("gate_w").rearrange("p (k n) -> p k n", k=2)
        w_r = W("w_r").rearrange("p (k n) -> p k n", k=2)
        w_dqkv = W("w_dqkv").rearrange("p (k n) -> p k n", k=2)
        w_u = W("w_u")
        w_o = W("w_o").rearrange("p (k n) -> p k n", k=2)

        small_in, dense_in, patches_first = sem("small_in"), sem("dense_in"), sem("patches_first")
        lin_in = [sem("lin_in0"), sem("lin_in1")]
        patches_in = [sem("patches_in0"), sem("patches_in1")]
        ffn0_in, ffn1_in = sem("ffn0_in"), sem("ffn1_in")
        consts_set = sem("consts_set")
        pos_ready = sem("pos_ready")
        embedded_ps, embedded = sem("embedded_ps"), sem("embedded")
        LNS = {}
        for ph in ("scan", "moe0", "attn", "moe1"):
            LNS[ph] = {n: sem(f"{ph}_{n}") for n in
                       ("mean", "centered", "squared", "var", "logvar", "rstd", "normed")}
        up_ps, up_left, up_right = sem("up_ps"), sem("up_left"), sem("up_right")
        conv_step, x_ready = sem("conv_step"), sem("x_ready")
        zbc_ps, z_copied, bc_copied = sem("zbc_ps"), sem("z_copied"), sem("bc_copied")
        soft_step, delta_ready, dx_ready = sem("soft_step"), sem("delta_ready"), sem("dx_ready")
        right_ready, soft_abs = sem("right_ready"), sem("soft_abs")
        a_exp, a_ready = sem("a_exp"), sem("a_ready")
        split_step, split_pool = sem("split_step"), sem("split_pool")
        stacks_in = [sem("stacks_in0"), sem("stacks_in1")]
        b_bcast, b_copied, c_bcast = sem("b_bcast"), sem("b_copied"), sem("c_bcast")
        decayed, injected, scanned = sem("decayed"), sem("injected"), sem("scanned")
        read_out, summed = sem("read_out"), sem("summed")
        y_gated = sem("y_gated")
        down_ps, scan_h = sem("down_ps"), sem("scan_h")
        MOE = {}
        for ph in ("moe0",):
            MOE[ph] = {n: sem(f"{ph}_{n}") for n in
                       ("logits", "logits_copied", "logits_turned", "shared_up", "shared_relu",
                        "shared_hid", "route", "routeT", "cwT_first", "cwT", "gates_first", "gates_out", "gates_in0", "gates_in1",
                        "up", "relu", "hid", "down", "h", "gate1", "lg", "exp")}
        MOE["moe1"] = {n: sem(f"moe1_{n}") for n in ("logits", "logits_copied", "logits_turned")}
        lg1, exp1 = sem("moe1_lg"), sem("moe1_exp")
        chosen, counted, slot_ready = sem("chosen"), sem("counted"), sem("slot_ready")
        tiles_ready = sem("tiles_ready")
        empty_set, empty_out, bias_in = sem("empty_set"), sem("empty_out"), sem("bias_in")
        token_set = sem("token_set")
        rows_ps, rows_copied, rows_tagged = sem("rows_ps"), sem("rows_copied"), sem("rows_tagged")
        rows_out = [sem(f"rows_out{n}") for n in range(NR)]
        slots_in = [sem(f"slots_in{n}") for n in range(4)]
        x_turned, x_copied = sem("x_turned"), sem("x_copied")
        hid_ps, hid_biased, hid_relu = sem("hid_ps"), sem("hid_biased"), sem("hid_relu")
        hid_turned, hid_copied = sem("hid_turned"), sem("hid_copied")
        y_ps, y_biased, y_ready = sem("y_ps"), sem("y_biased"), sem("y_ready")
        y_out = [sem("y_out0"), sem("y_out1")]
        cc_ps, cc_copied, ckv_rep = sem("cc_ps"), sem("cc_copied"), sem("ckv_rep")
        q_ps, k_ps, q_copied, k_copied = sem("q_ps"), sem("k_ps"), sem("q_copied"), sem("k_copied")
        k_spread = sem("k_spread")
        scores_ps, masked, maxed, shifted = sem("scores_ps"), sem("masked"), sem("maxed"), sem("shifted")
        exped, inverted = sem("exped"), sem("inverted")
        p_turned, p_copied = sem("p_turned"), sem("p_copied")
        v_ps, v_spread = sem("v_ps"), sem("v_spread")
        vm_ones = sem("vm_ones")
        o_ps, o_scaled, o_turned, o_copied = sem("o_ps"), sem("o_scaled"), sem("o_turned"), sem("o_copied")
        wo_ps, attn_h = sem("wo_ps"), sem("attn_h")

        def attention(eng, first, step, last):
            first()
            for cj in range(2):
                for p in range(4):
                    step(cj, cj, p, True, True)
            with eng.Fori(1, NCH // 2 - 1) as i:
                for cj in range(2):
                    for p in range(4):
                        step(i * 2 + cj, cj, p, True, True)
            for cj in range(2):
                for p in range(4):
                    step(NCH - 2 + cj, cj, p, False, cj == 0)
            last()

        def ahead(c, cj, p, d):
            return (c, cj, p + d) if p + d < 4 else (c + 1, 1 - cj, p + d - 4)

        def tile(i, u):
            return i * 4 + (u + 2), u % 2, (u + 2) % 4

        def half(i, u):
            return i * 2 + (u + 2) // 2

        def quarter(i, u):
            return i + (u + 2) // 4

        def slot_tiles(eng, step):
            for u in range(-2, 4):
                step(0, u)
            with eng.Fori(1, ST // 4 - 1) as i:
                for u in range(4):
                    step(i, u)
            for u in range(4):
                step(ST // 4 - 1, u, last=(u == 3))

        block = ctx.enter_context(nc.Block())

        def pe_mean(pe, s, c, bank, deep=1):
            pe.wait_ge(s["centered"], c + 3 - deep)
            for k in range(HALVES):
                mm = nc.tensor.matmul(ps[:, bank, 0:CH], ones[:], hF[:, k, ds(c * CH, CH)],
                                      start=(k == 0), stop=(k == HALVES - 1))
            mm.then_inc(s["mean"], 1)

        def pe_var(pe, s, c, j, bank, deep=1):
            pe.wait_ge(s["squared"], c + 1)
            pe.wait_ge(s["logvar"], c + 3 - deep)
            for k in range(HALVES):
                mm = nc.tensor.matmul(ps[:, bank, 0:CH], ones[:], sq[:, j, k, :],
                                      start=(k == 0), stop=(k == HALVES - 1))
            mm.then_inc(s["var"], 1)

        def act_square(act, s, c, j):
            act.wait_ge(s["centered"], c + 3)
            act.wait_ge(s["logvar"], c + 1)
            nc.scalar.activation(sq[:, j, :, :], xn[:, :, ds(c * CH, CH)],
                                 ACT.Square).then_inc(s["squared"], 1)

        def act_rstd(act, s, c, j, bank):
            act.wait_ge(s["var"], c + 1)
            act.wait_ge(s["normed"], c + 1)
            nc.scalar.activation(rstd[:, j, :], ps[:, bank, 0:CH], ACT.Ln,
                                 bias=S("eps")).then_inc(s["logvar"], 1)
            act.wait_ge(s["logvar"], c + 3)
            nc.scalar.activation(rstd[:, j, :], rstd[:, j, :], ACT.Exp,
                                 scale=-0.5).then_inc(s["rstd"], 1)

        def dve_center(dve, s, c, bank):
            dve.wait_ge(s["mean"], c + 1)
            nc.vector.tensor_tensor(xn[:, :, ds(c * CH, CH)], hF[:, :, ds(c * CH, CH)],
                                    bc(ps[:, bank, 0:CH], 1, HALVES),
                                    ALU.subtract).then_inc(s["centered"], 1)

        def dve_scale(dve, s, c, j):
            dve.wait_ge(s["rstd"], c + 1)
            dve.wait_ge(s["centered"], c + 3)
            nc.vector.tensor_tensor(xn[:, :, ds(c * CH, CH)], xn[:, :, ds(c * CH, CH)],
                                    bc(rstd[:, j, :], 1, HALVES),
                                    ALU.mult).then_inc(s["normed"], 1)

        def act_norm_start(act, s):
            act.sem_inc(s["logvar"], 2)

        def dve_norm_start(dve, s):
            dve.sem_inc(s["centered"], 2)
            dve.sem_inc(s["normed"], 2)

        def staged(eng, step, lag):
            first = lag + lag % 2
            for k in range(first):
                step(k, k % 2, lambda d: k >= d)
            with eng.Fori(first // 2, NCH // 2) as i:
                for j in range(2):
                    step(i * 2 + j, j, lambda d: True)
            for k in range(NCH, NCH + lag):
                step(k, k % 2, lambda d: k - d < NCH)

        def logit_cols(c):
            return ds(c * CH, CH + (TP - T if isinstance(c, int) and c == NCH - 1 else 0))

        def pe_logits(pe, s, ln, c, bank, w):
            cols = logit_cols(c)
            n = CH + (TP - T if isinstance(c, int) and c == NCH - 1 else 0)
            pe.wait_ge(ln["normed"], c + 3)
            if not (isinstance(c, int) and c == 0):
                pe.wait_ge(s["logits_copied"], c)
            for k in range(HALVES):
                mm = nc.tensor.matmul(ps[0:E8, bank, 0:n], w[:, k, :], xn[:, k, cols],
                                      start=(k == 0), stop=(k == HALVES - 1))
            mm.then_inc(s["logits"], 1)

        def act_logits(act, s, c, bank):
            cols = logit_cols(c)
            n = CH + (TP - T if isinstance(c, int) and c == NCH - 1 else 0)
            act.wait_ge(s["logits"], c + 1)
            nc.scalar.activation(cwT[:, cols], ps[0:E8, bank, 0:n],
                                 ACT.Copy).then_inc(s["logits_copied"], 1)

        def pe_turn_logits(pe, s):
            pe.wait_ge(s["logits_copied"], NCH)
            for t in range(TT):
                mm = nc.tensor.transpose(ps[:, 0, t * E8:(t + 1) * E8], cwT[:, t * P:(t + 1) * P],
                                         ident[0:E8, 0:E8])
            mm.then_inc(s["logits_turned"], 1)

        WB = [0, 5, 6, 7, 0]

        def pe_turn_weights(pe, s, n_route, weights):
            pe.wait_ge(s["route"], n_route)
            for t in range(TT):
                if t == 16:
                    pe.wait_ge(s["cwT_first"], 1)
                mm = nc.tensor.transpose(ps[0:E8, WB[t // 4], (t % 4) * P:(t % 4 + 1) * P],
                                         weights[:, t, :], ident)
                if t % 4 == 3 or t == TT - 1:
                    mm.then_inc(s["routeT"], 1)

        def copy_weights(eng, copy, s, b, done):
            n = min(512, TP - b * 512)
            eng.wait_ge(s["routeT"], b + 1)
            copy(cwT[:, b * 512:b * 512 + n], ps[0:E8, WB[b], 0:n]).then_inc(done, 1)

        def dve_first_max(link, values, tmp, out_):
            link(nc.vector.tensor_reduce(red[:], values, AX, ALU.max))
            link(nc.vector.tensor_tensor(tmp, values, bc(red[:], 2, E8), ALU.is_equal))
            link(nc.vector.tensor_tensor(tmp, tmp, bc(S("rank"), 1, TT), ALU.mult))
            link(nc.vector.tensor_reduce(red[:], tmp, AX, ALU.max))
            link(nc.vector.tensor_tensor(out_, tmp, bc(red[:], 2, E8), ALU.is_equal))

        def piece(c, j, nt):
            if isinstance(c, int) and c < 2:
                return c * E8 + j, (c * E8 + j) % 3
            skipped = 2 * (nt - E8)
            return c * nt + (j - skipped), (j - skipped) % 3

        def pieces(c, nt):
            return E8 if isinstance(c, int) and c < 2 else nt

        def pe_up(w, row0, cols, bank):
            for k in range(HALVES):
                mm = nc.tensor.matmul(ps[:, bank, 0:CH], w[:, k, row0:row0 + P], xn[:, k, cols],
                                      start=(k == 0), stop=(k == HALVES - 1))
            return mm

        def pe_shared(pe, s, up_w, dn_w):
            for g in range(2 * 4 + 2):
                if g < 8:
                    if g >= 3:
                        pe.wait_ge(s["shared_relu"], g - 2)
                    pe_up(up_w, (E8 + g % 4) * P, ds(g // 4 * CH, CH),
                          5 + g % 3).then_inc(s["shared_up"], 1)
                if g >= 2:
                    g -= 2
                    pe.wait_ge(s["shared_hid"], g + 1)
                    for m in range(HALVES):
                        nc.tensor.matmul(ps[:, 1 + 2 * (g // 4) + m, 0:CH],
                                         dn_w[:, E8 + g % 4, m * P:(m + 1) * P], hid2[:, g % 3, :],
                                         start=(g % 4 == 0), stop=False, skip_group_check=True)

        def act_shared(act, s):
            for g in range(8):
                act.wait_ge(s["shared_up"], g + 1)
                nc.scalar.activation(hid[:, g % 3, :], ps[:, 5 + g % 3, 0:CH],
                                     ACT.Relu).then_inc(s["shared_relu"], 1)
                act.wait_ge(s["shared_relu"], g + 1)
                nc.scalar.activation(hid2[:, g % 3, :], hid[:, g % 3, :],
                                     ACT.Square).then_inc(s["shared_hid"], 1)

        def pe_moe(pe, s, ln, nt, up_w, dn_w):
            pe.wait_ge(s["cwT"], 4)
            pe.wait_ge(s["cwT_first"], 1)

            def norm_mean(c):
                pe.wait_ge(s["h"], c + 3)
                pe.wait_ge(ln["logvar"], c + 2)
                pe_mean(pe, ln, c, 0)

            def step(c, cj, on):
                if not on(0):
                    return
                n = pieces(c, nt)
                for j in range(n + 2):
                    if on(1) and j == 5:
                        norm_mean(c - 1)
                    if on(1) and j == 8:
                        pe_var(pe, ln, c - 1, 1 - cj, 0)
                    if j < n:
                        g, b = piece(c, j, nt)
                        pe.wait_ge(s["relu"], g + 1)
                        pe_up(up_w, j * P, ds(c * CH, CH), 5 + b).then_inc(s["up"], 1)
                    if j == 0:
                        pe.wait_ge(s["h"], c + 1)
                    if j >= 2:
                        g, b = piece(c, j - 2, nt)
                        pe.wait_ge(s["hid"], g + 4)
                        for m in range(HALVES):
                            mm = nc.tensor.matmul(ps[:, 1 + 2 * cj + m, 0:CH],
                                                  dn_w[:, j - 2, m * P:(m + 1) * P], hid2[:, b, :],
                                                  start=(j == 2 and n == nt), stop=(j == n + 1),
                                                  skip_group_check=True)
                mm.then_inc(s["down"], 1)

            staged(pe, step, 1)
            return norm_mean

        def act_exp(act, ready, done, sign):
            act.wait_ge(ready, 1)
            nc.scalar.activation(sc[:], lg[:], ACT.Exp, scale=sign).then_inc(done, 1)

        def act_moe(act, s, ln, nt):
            act.sem_inc(s["relu"], 3)

            def step(c, cj, on):
                if not on(0):
                    return
                n = pieces(c, nt)
                for j in range(n):
                    g, b = piece(c, j, nt)
                    act.wait_ge(s["up"], g + 1)
                    act.wait_ge(s["hid"], g + 1)
                    nc.scalar.activation(hid[:, b, :], ps[:, 5 + b, 0:CH],
                                         ACT.Relu).then_inc(s["relu"], 1)
                    if on(1) and j == 6:
                        act_square(act, ln, c - 1, 1 - cj)
                if on(1):
                    act_rstd(act, ln, c - 1, 1 - cj, 0)

            staged(act, step, 1)

        def dve_moe(dve, s, ln, nt):
            dve.sem_inc(s["hid"], 3)
            dve.sem_inc(s["h"], 2)

            def step(c, cj, on):
                if not on(0):
                    dve_center(dve, ln, c - 1, 0)
                    dve_scale(dve, ln, c - 1, 1 - cj)
                    return
                gates_in = s["gates_in0" if cj == 0 else "gates_in1"]
                start = isinstance(c, int) and c == 0
                if start:
                    dve.wait_ge(s["gates_first"], 16)
                else:
                    dve.wait_ge(gates_in, (c - cj) * 8 + 16)
                for j in range(pieces(c, nt)):
                    if start and j == EF:
                        dve.wait_ge(gates_in, 16)
                    g, b = piece(c, j, nt)
                    dve.wait_ge(s["relu"], g + 4)
                    a = hid[:, b, :]
                    if j < E8:
                        nc.vector.tensor_tensor(hid3[:, b, :], a, gbc[:, cj, j, :],
                                                ALU.mult).then_inc(s["gate1"], 1)
                        dve.wait_ge(s["gate1"], c * E8 + j + 1)
                        factor = hid3[:, b, :]
                    else:
                        factor = a
                    nc.vector.tensor_tensor(hid2[:, b, :], a, factor, ALU.mult).then_inc(s["hid"], 1)
                    if on(1) and j == 5:
                        dve_center(dve, ln, c - 1, 0)
                if on(1):
                    dve_scale(dve, ln, c - 1, 1 - cj)
                dve.wait_ge(s["down"], c + 1)
                cs = ds(c * CH, CH)
                nc.vector.tensor_tensor(hF[:, :, cs], hF[:, :, cs], ps[:, 1 + 2 * cj:3 + 2 * cj, 0:CH],
                                        ALU.add).then_inc(s["h"], 1)

            staged(dve, step, 1)

        def sp_gates(sp, s):
            def load_gates(c, cj, experts=slice(0, E8), done=None):
                sp.dma_start(gbc[:, cj, experts, :],
                             gates_dram[experts, ds(c * CH, CH)].partition_broadcast(P)
                             ).then_inc(done or s["gates_in0" if cj == 0 else "gates_in1"], 16)

            sp.wait_ge(s["cwT_first"], 1)
            sp.dma_start(gates_dram[:, 0:512], cwT[:, 0:512]).then_inc(s["gates_out"], 16)
            sp.wait_ge(s["gates_out"], 16)
            load_gates(0, 0, slice(0, EF), s["gates_first"])
            load_gates(0, 0, slice(EF, E8))
            sp.wait_ge(s["cwT"], 4)
            sp.dma_start(gates_dram[:, 512:T], cwT[:, 512:T]).then_inc(s["gates_out"], 16)
            sp.wait_ge(s["gates_out"], 32)
            load_gates(1, 1)
            with sp.Fori(1, NCH // 2) as i:
                for cj in range(2):
                    c = i * 2 + cj
                    sp.wait_ge(s["h"], c + 1)
                    load_gates(c, cj)

        def split_chunks(eng, ops, step, chunks, before=0):
            for i, c in enumerate(chunks, before):
                cs = ds(c * CH, CH)
                eng.wait_ge(bc_copied, c + 3)
                ops.tensor_copy(parts[0][:, cs], bcv[:, cs]).then_inc(step, 1)
                for k in (1, 2):
                    eng.wait_ge(step, i * 5 + 2 * k - 1)
                    ops.tensor_tensor(bcv[:, cs], bcv[:, cs], parts[k - 1][:, cs],
                                      ALU.subtract).then_inc(step, 1)
                    eng.wait_ge(step, i * 5 + 2 * k)
                    ops.tensor_copy(parts[k][:, cs], bcv[:, cs]).then_inc(step, 1)

        @block.sync
        def _(sp):
            for h in range(2):
                ks = slice(h * FK // 2, (h + 1) * FK // 2)
                sp.dma_start(wl[:, ks, :], w_lin[:, ks, :]).then_inc(lin_in[h], 16)
                sp.dma_start(xin[:, 0, ks, :], patches[0, :, ks, :]).then_inc(
                    patches_first if h == 0 else patches_in[0], 16)
            def load_patches(c, j):
                if not isinstance(c, int):
                    sp.wait_ge(embedded, c * 2 + 2)
                sp.dma_start(xin[:, j, :, :], patches[ds(c, 1), :, :, :].rearrange(
                    "o p k n -> (o p) k n")).then_inc(patches_in[j], 16)

            sp.dma_start(sm[:], small).then_inc(small_in, 16)
            load_patches(1, 1)
            sp.dma_start(wd[:], dense).then_inc(dense_in, 16)
            with sp.Fori(1, NCH // 2) as i:
                for j in range(2):
                    load_patches(i * 2 + j, j)
            for h in range(2):
                sp.wait_ge(split_step, 5 * sum(c < NCH // 2 * (h + 1) for c in DVE_SPLIT))
                sp.wait_ge(split_pool, 5 * sum(c < NCH // 2 * (h + 1) for c in POOL_SPLIT))
                hs = slice(h * T // 2, (h + 1) * T // 2)
                for g in range(4):
                    for k in range(3):
                        sp.dma_start(stacks[g][32 * k:32 * k + 32, hs],
                                     parts[k][32 * g:32 * g + 32, hs]).then_inc(stacks_in[h], 16)
            for h in range(2):
                sp.wait_ge(stacks_in[h], 16 * 12)
            sp.dma_start(up0s, up0).then_inc(ffn0_in, 16)
            sp.dma_start(dn0s, dn0).then_inc(ffn0_in, 16)
            sp.wait_ge(empty_set, 2)
            sp.dma_start(slots.rearrange("(t p) w -> p t w", p=P), bc(empty, 1, ST)).then_inc(empty_out, 16)
            sp.wait_ge(empty_out, 16)
            sp.wait_ge(scan_h, NCH + 2)
            sp.dma_start(w1s, w1).then_inc(ffn1_in, 16)
            sp.dma_start(w2s, w2).then_inc(ffn1_in, 16)
            sp_gates(sp, MOE["moe0"])
            sp.wait_ge(attn_h, NCH)
            sp.wait_ge(MOE["moe1"]["logits_turned"], 1)
            sp.dma_start(b1r, b1.partition_broadcast(P)).then_inc(bias_in, 16)
            sp.dma_start(b2r, b2.partition_broadcast(P)).then_inc(bias_in, 16)
            for n in range(NR):
                sp.wait_ge(rows_out[n], 16 * len(range(n, TT, NR)))

            def load_rows(i, u, first=False):
                s, j, r = tile(i, u)
                if not first:
                    sp.wait_ge(y_ready, s + 1)
                sp.dma_start(slot_row[r], slots[ds(s * P, P), :]).then_inc(slots_in[r], 16)

            for u in range(-2, 2):
                load_rows(0, u, first=True)
            with sp.Fori(1, ST // 4) as i:
                for u in range(-2, 2):
                    load_rows(i, u)
            for u in range(-2, 0):
                load_rows(ST // 4, u)

        @block.gpsimd
        def _(pool):
            nc.gpsimd.memset(ones[:], 1.0 / D).then_inc(consts_set, 1)
            nc.gpsimd.memset(xn[:, :, T:TP], 0.0).then_inc(consts_set, 1)
            nc.gpsimd.memset(leftp, 0.0).then_inc(consts_set, 1)
            nc.gpsimd.memset(empty[:, 0:ROW - 1], 0.0).then_inc(empty_set, 1)
            nc.gpsimd.memset(empty[:, ROW - 1:ROW].bitcast(I32), NOBODY).then_inc(empty_set, 1)
            nc.gpsimd.iota(token[:], pattern=[[P, TT]], base=0, channel_multiplier=1).then_inc(token_set, 1)
            for j in range(2):
                nc.gpsimd.memset(decay[j], 0.0).then_inc(consts_set, 1)
            pool.wait_ge(small_in, 16)
            pool.wait_ge(embedded, 4 + 2 * NCH)
            nc.gpsimd.tensor_copy(sel, bc(S("row32")[0:96, :], 2, P)).then_inc(consts_set, 1)

            split_chunks(pool, nc.gpsimd, split_pool, POOL_SPLIT)

            pool.sem_inc(injected, 2)
            for q in range(NQ):
                pool.wait_ge(dx_ready, q + 1)
                with pool.Fori(0, N // 2) as i:
                    for j in range(2):
                        k = q * N + i * 2 + j
                        pool.wait_ge(b_copied, k + 2)
                        pool.wait_ge(scanned, k + 1)
                        nc.gpsimd.tensor_tensor(inject[j], dx[:, q * QT:(q + 1) * QT], bsb[j],
                                                ALU.mult).then_inc(injected, 1)

            mask = S("head_of_row")
            pool.wait_ge(MOE["moe0"]["h"], NCH + 2)
            with pool.Fori(0, NCH // 2) as i:
                for cj in range(2):
                    c = i * 2 + cj
                    pool.wait_ge(k_copied, c + 1)
                    for p in range(4):
                        pool.wait_ge(scores_ps, c * 4 + p + 1)
                        for a in range(2):
                            for im in range(2):
                                t0 = (2 * p + im) * L
                                last = nc.gpsimd.tensor_tensor(
                                    kbd[p % 2][:, a, im, :, :], bc(kT[cj][:, a, t0:t0 + L], 1, 8),
                                    bc(mask, 2, L), ALU.mult)
                        last.then_inc(k_spread, 1)

            pool.wait_ge(empty_out, 16)
            pool.wait_ge(slot_ready, 1)
            for t in range(TT):
                n = min(P, T - t * P)
                pool.wait_ge(rows_tagged, t + 1)
                pool.wait_ge(rows_copied, t + 1)
                nc.gpsimd.indirect_dma_start(
                    out=slots, out_offset=bass.IndirectOffsetOnAxis(ap=slot_i[0:n, t:t + 1], axis=0),
                    in_=token_row[t % NR][0:n, :], in_offset=None).then_inc(rows_out[t % NR], 16)
            for s in range(ST):
                j = s % 2
                pool.wait_ge(y_ready, s + 5)
                nc.gpsimd.indirect_dma_start(
                    out=out, out_offset=bass.IndirectOffsetOnAxis(
                        ap=slot_token[:, s:s + 1], axis=0),
                    in_=out_row[j], in_offset=None, bounds_check=T - 1,
                    oob_is_err=False).then_inc(y_out[j], 16)
            for j in range(2):
                pool.wait_ge(y_out[j], 16 * (ST // 2))

        @block.tensor
        def _(pe):
            ln = LNS["scan"]

            def pe_embed(k, j, on):
                def products(m, start=False):
                    for f in range(FK):
                        if start and f == 0:
                            pe.wait_ge(lin_in[0], 16)
                            pe.wait_ge(patches_first, 16)
                        if start and f == FK // 2:
                            pe.wait_ge(lin_in[1], 16)
                            pe.wait_ge(patches_in[0], 16)
                        mm = nc.tensor.matmul(ps[:, 2 * j + m, 0:IC * NP],
                                              wl[:, f, m * P:(m + 1) * P], xin[:, j, f, :],
                                              start=(f == 0), stop=(f == FK - 1))
                    return mm

                if on(0):
                    start = isinstance(k, int) and k == 0
                    if not start:
                        pe.wait_ge(patches_in[j], (k - j) * 8 + 16)
                    if not isinstance(k, int):
                        pe.wait_ge(embedded, k * 2 + 2)
                    products(0, start)
                if isinstance(k, int) and k == 1:
                    pe.wait_ge(consts_set, 5)
                    pe.wait_ge(pos_ready, 6)
                if on(1):
                    pe.wait_ge(embedded, k * 2 + 4)
                    pe_mean(pe, ln, k - 1, 4)
                if on(0):
                    products(1).then_inc(embedded_ps, 1)
                if on(2):
                    c = k - 2
                    pe.wait_ge(dense_in, 16)
                    pe.wait_ge(ln["normed"], c + 3)
                    pe.wait_ge(up_right, c + 1)
                    for m in range(2):
                        for f in range(HALVES):
                            mm = nc.tensor.matmul(ps[:, 6 + m, 0:CH], w_up[:, f, m * P:(m + 1) * P],
                                                  xn[:, f, ds(c * CH, CH)],
                                                  start=(f == 0), stop=(f == 1))
                    mm.then_inc(up_ps, 1)
                if on(1):
                    pe_var(pe, ln, k - 1, 1 - j, 5)

            staged(pe, pe_embed, 2)

            pe.wait_ge(embedded, 4 + 2 * NCH)
            with pe.Fori(0, NCH // 2) as i:
                for j in range(2):
                    c = i * 2 + j
                    pe.wait_ge(x_ready, c + 1)
                    pe.wait_ge(z_copied, c + 1)
                    pe.wait_ge(bc_copied, c + 1)
                    nc.tensor.matmul(ps[:, j, 0:CH], W("w_delta"), xs[:, ds(c * CH, CH)],
                                     start=True, stop=True)
                    nc.tensor.matmul(ps[:, 2 + j, 0:CH], W("w_bc"), xs[:, ds(c * CH, CH)],
                                     start=True, stop=True).then_inc(zbc_ps, 1)

            def row(stack, q, i, h, bank):
                return nc.tensor.matmul(ps[:, bank, 0:CH],
                                        sel[:, ds(i, 1), :].rearrange("p o m -> p (o m)"),
                                        stacks[stack][0:96, ds(q * QT + h * CH, CH)],
                                        start=True, stop=True)

            def spread_b(q, i, j):
                pe.wait_ge(b_copied, q * N + i * 2 + j + 1)
                for h in range(2):
                    mm = row(j, q, i, h, 2 + h)
                mm.then_inc(b_bcast, 1)

            def spread_c(q, i, j):
                pe.wait_ge(read_out, q * N + i * 2 + j + 1)
                for h in range(2):
                    mm = row(2 + j, q, i, h, 4 + 2 * j + h)
                mm.then_inc(c_bcast, 1)

            def sum_state(q, i, j, last=False):
                k = q * N + i * 2 + j
                pe.wait_ge(read_out, k + 3)
                for h in range(2):
                    mm = nc.tensor.matmul(ps[:, h, 0:CH], ident, read[j][:, h * CH:(h + 1) * CH],
                                          start=False, stop=last, skip_group_check=True)
                mm.then_inc(summed, 1)

            def skip_product(q):
                pe.wait_ge(y_gated, q + 1)
                for h in range(2):
                    nc.tensor.matmul(ps[:, h, 0:CH], diag_d[:],
                                     xs[:, q * QT + h * CH:q * QT + (h + 1) * CH],
                                     start=True, stop=False, skip_group_check=True)

            pe.wait_ge(a_ready, 2)
            pe.wait_ge(bc_copied, NCH + 2)
            pe.wait_ge(z_copied, NCH + 2)
            skip_product(0)
            pe.wait_ge(stacks_in[0], 16 * 12)
            pe.wait_ge(consts_set, 6)
            pe.sem_inc(summed, 2)
            spread_b(0, 0, 0)
            spread_b(0, 0, 1)
            spread_c(0, 0, 0)
            spread_b(0, 1, 0)
            spread_c(0, 0, 1)
            for q in range(NQ):
                if q == NQ // 2 - 1:
                    pe.wait_ge(stacks_in[1], 16 * 12)
                spread_b(q, 1, 1)
                spread_c(q, 1, 0)
                if q > 0:
                    skip_product(q)
                sum_state(q, 0, 0)
                spread_b(q, 2, 0)
                spread_c(q, 1, 1)
                sum_state(q, 0, 1)
                with pe.Fori(2, N // 2 - 1) as i:
                    spread_b(q, i, 1)
                    spread_c(q, i, 0)
                    sum_state(q, i - 1, 0)
                    spread_b(q, i + 1, 0)
                    spread_c(q, i, 1)
                    sum_state(q, i - 1, 1)
                more = q + 1 < NQ
                spread_b(q, N // 2 - 1, 1)
                spread_c(q, N // 2 - 1, 0)
                sum_state(q, N // 2 - 2, 0)
                if more:
                    spread_b(q + 1, 0, 0)
                spread_c(q, N // 2 - 1, 1)
                sum_state(q, N // 2 - 2, 1)
                if more:
                    spread_b(q + 1, 0, 1)
                    spread_c(q + 1, 0, 0)
                sum_state(q, N // 2 - 1, 0)
                if more:
                    spread_b(q + 1, 1, 0)
                    spread_c(q + 1, 0, 1)
                sum_state(q, N // 2 - 1, 1, last=True)
            pe.wait_ge(y_gated, NQ + 1)
            ln = LNS["moe0"]

            def pe_down(k, j, on):
                if on(0):
                    pe.wait_ge(scan_h, k + 1)
                    for m in range(2):
                        mm = nc.tensor.matmul(ps[:, 2 + 2 * j + m, 0:CH],
                                              W("w_down")[:, m * P:(m + 1) * P],
                                              gated[:, ds(k * CH, CH)], start=True, stop=True)
                    mm.then_inc(down_ps, 1)
                if on(1):
                    pe.wait_ge(scan_h, k + 2)
                    pe_mean(pe, ln, k - 1, 0)
                if on(2):
                    pe_var(pe, ln, k - 2, j, 6 + j, deep=2)
                if on(3):
                    pe_logits(pe, MOE["moe0"], ln, k - 3, 1, gate_w)

            staged(pe, pe_down, 3)

            pe_turn_logits(pe, MOE["moe0"])
            pe.wait_ge(ffn0_in, 32)
            pe_shared(pe, MOE["moe0"], up0s, dn0s)
            pe_turn_weights(pe, MOE["moe0"], 1, rt1)
            last_mean = pe_moe(pe, MOE["moe0"], LNS["attn"], 12, up0s, dn0s)

            before_ln = LNS["attn"]
            pe.sem_inc(scores_ps, 2)
            pe.sem_inc(p_turned, 2)
            pe.sem_inc(o_ps, 2)
            pe.sem_inc(o_turned, 2)
            pe.sem_inc(wo_ps, 2)

            def compress(c):
                if isinstance(c, int) and c in (1, 2):
                    pe.wait_ge(k_copied, c)
                elif not isinstance(c, int) or c > 2:
                    pe.wait_ge(attn_h, c - 2)
                if not isinstance(c, int) or c > 3:
                    pe.wait_ge(MOE["moe1"]["logits_copied"], c - 3)
                pe.wait_ge(before_ln["normed"], c + 3)
                for k in range(HALVES):
                    mm = nc.tensor.matmul(ps[:, 6, 0:CH], w_dqkv[:, k, :], xn[:, k, ds(c * CH, CH)],
                                          start=(k == 0), stop=(k == 1))
                mm.then_inc(cc_ps, 1)

            def queries(c):
                pe.wait_ge(cc_copied, c + 1)
                if not (isinstance(c, int) and c < 3):
                    pe.wait_ge(ln["logvar"], c)
                for m in range(2):
                    mm = nc.tensor.matmul(ps[:, 6 + m, 0:CH], w_u[0:64, m * P:(m + 1) * P],
                                          cc[0:64, :], start=True, stop=True)
                mm.then_inc(q_ps, 1)

            def keys(c):
                pe.wait_ge(q_copied, c + 1)
                for m in range(2):
                    mm = nc.tensor.matmul(ps[:, 6 + m, 0:CH], w_u[64:128, m * P:(m + 1) * P],
                                          cc[64:128, :], start=True, stop=True)
                mm.then_inc(k_ps, 1)

            def scores(c, cj, p):
                k = c * 4 + p
                if isinstance(k, int) and k == 0:
                    pe.wait_ge(before_ln["logvar"], NCH + 2)
                pe.wait_ge(k_spread, k + 1)
                pe.wait_ge(masked, k + 1)
                for im in range(2):
                    t0 = (2 * p + im) * L
                    nq = 64 if im == 0 else L
                    for a in range(2):
                        mm = nc.tensor.matmul(ps[64 * im:64 * im + nq, a, 0:8 * L],
                                              qT[cj][:, a, t0:t0 + nq],
                                              kbd[p % 2][:, a, im, :, :].rearrange("p h l -> p (h l)"),
                                              start=True, stop=True)
                mm.then_inc(scores_ps, 1)

            def values(c, cj, p):
                k = c * 4 + p
                pe.wait_ge(ckv_rep, c + 1)
                pe.wait_ge(v_spread, k + 1)
                for im in range(2):
                    mm = nc.tensor.matmul(ps[0:KG * L, 4, im * D:(im + 1) * D],
                                          ckv3[cj][64:128, 2 * p + im, :, :].rearrange("p r l -> p (r l)"),
                                          w_u[64:128, D:2 * D], start=True, stop=True)
                mm.then_inc(v_ps, 1)

            def project(c, cj):
                pe.wait_ge(o_copied, c * 4 + 5)
                for m in range(2):
                    for k in range(2):
                        mm = nc.tensor.matmul(ps[:, 6 + m, 0:CH], w_o[:, k, m * P:(m + 1) * P],
                                              oT[cj][:, k, :], start=(k == 0), stop=(k == 1))
                mm.then_inc(wo_ps, 1)

            def pe_first():
                pe.wait_ge(MOE["moe0"]["relu"], piece(NCH - 1, 11, 12)[0] + 4)
                compress(0)
                last_mean(NCH - 1)
                queries(0)
                pe_var(pe, before_ln, NCH - 1, 1, 0)
                keys(0)
                compress(1)
                scores(0, 0, 0)
                scores(0, 0, 1)
                values(0, 0, 0)
                pe.wait_ge(vm_ones, 2)

            def pe_step(c, cj, p, more2, more1):
                k = c * 4 + p
                pe.wait_ge(exped, k + 1)
                pe.wait_ge(p_copied, k + 1)
                for a in range(2):
                    for b in range(KG):
                        h0 = 8 * a + min(KG * b, 8 - KG)
                        mm = nc.tensor.transpose(ps[0:KG * L, 2 + a, b * QR:(b + 1) * QR],
                                                 prob[p % 2][0:QR, h0:h0 + KG, :].rearrange(
                                                     "p h l -> p (h l)"), ident[0:QR, 0:QR])
                mm.then_inc(p_turned, 1)
                if more1 and p == 1:
                    keys(c + 1)
                if more1 and p == 0:
                    queries(c + 1)
                if more1 or p < 3:
                    values(*ahead(c, cj, p, 1))
                pe.wait_ge(p_copied, k + 2)
                pe.wait_ge(v_spread, k + 2)
                pe.wait_ge(o_copied, k + 1)
                for im in range(2):
                    nq = 64 if im == 0 else L
                    for ab in range(2 * KG):
                        mm = nc.tensor.matmul(ps[64 * im:64 * im + nq, 5, ab * VB:(ab + 1) * VB],
                                              probT[0:KG * L, ab // KG, ab % KG, 64 * im:64 * im + nq],
                                              vm[p % 2][0:KG * L, im, ab, :], start=True, stop=True)
                mm.then_inc(o_ps, 1)
                if more1 or p < 2:
                    scores(*ahead(c, cj, p, 2))
                if p == 1 and not (isinstance(c, int) and c == 0):
                    if more1:
                        pe.wait_ge(k_copied, c + 2)
                    else:
                        pe.wait_ge(attn_h, c - 1)
                    project(c - 1, 1 - cj)
                if p == 2 and not (isinstance(c, int) and c == 0):
                    pe.wait_ge(attn_h, c)
                    pe_mean(pe, ln, c - 1, 7)
                if p == 2 and not (isinstance(c, int) and c < 2):
                    pe_logits(pe, MOE["moe1"], ln, c - 2, 6, w_r)
                if p == 3 and not (isinstance(c, int) and c == 0):
                    pe_var(pe, ln, c - 1, 1 - cj, 7)
                pe.wait_ge(o_scaled, k + 1)
                for a in range(2):
                    mm = nc.tensor.transpose(ps[:, 5, O_T + a * QR:O_T + (a + 1) * QR],
                                             osb[p % 2][0:QR, a, :, :].rearrange("p h d -> p (h d)"),
                                             ident[0:QR, 0:QR])
                mm.then_inc(o_turned, 1)
                if more2 and p == 3:
                    compress(c + 2)

            def pe_last():
                pe.wait_ge(attn_h, NCH - 1)
                pe.wait_ge(ln["logvar"], NCH + 1)
                project(NCH - 1, 1)
                pe.wait_ge(attn_h, NCH)
                pe_mean(pe, ln, NCH - 1, 7)
                pe_logits(pe, MOE["moe1"], ln, NCH - 2, 6, w_r)
                pe_var(pe, ln, NCH - 1, 1, 7)
                pe_logits(pe, MOE["moe1"], ln, NCH - 1, 6, w_r)

            ln = LNS["moe1"]
            attention(pe, pe_first, pe_step, pe_last)

            pe_turn_logits(pe, MOE["moe1"])

            def turn_rows(t):
                n = min(P, T - t * P)
                if t >= 2:
                    pe.wait_ge(rows_copied, t - 1)
                for k in range(HALVES):
                    nc.tensor.transpose(ps[0:n, 3 + t % 2, k * P:(k + 1) * P],
                                        hF[:, k, t * P:t * P + n], ident)
                for k in range(HALVES):
                    mm = nc.tensor.transpose(ps[0:n, 3 + t % 2, D + k * P:D + (k + 1) * P],
                                             xn[:, k, t * P:t * P + n], ident)
                mm.then_inc(rows_ps, 1)

            for t in range(4):
                turn_rows(t)
            pe.wait_ge(chosen, 1)
            onehot = rt1[:].rearrange("p t e -> p (t e)")
            nc.tensor.matmul(ps[:, 1, 0:TT * E8], S("before"), onehot, start=True, stop=True)
            nc.tensor.matmul(ps[:, 2, 0:TT * E8], ones[:], onehot, start=True,
                             stop=True).then_inc(counted, 1)
            for t in range(4, TT):
                turn_rows(t)

            def turn_x(i, u):
                s, j, r = tile(i, u)
                pe.wait_ge(slots_in[r], quarter(i, u) * 16 + 16)
                pe.wait_ge(x_copied, s + 1)
                for k in range(2):
                    mm = nc.tensor.transpose(ps[:, j, k * P:(k + 1) * P],
                                             slot_row[r][:, D + k * P:D + (k + 1) * P], ident)
                mm.then_inc(x_turned, 1)

            def expert_of(s):
                return pe.value_load(expert_i[0:1, ds(s, 1)], min_val=0, max_val=E8 - 1)

            def hidden(s, j, e):
                pe.wait_ge(x_copied, s + 3)
                pe.wait_ge(hid_biased, s + 1)
                for k in range(2):
                    mm = nc.tensor.matmul(ps[:, 2 + j, 0:HID1], slot_xT[j][:, k, :],
                                          w1s[:, k, ds(e * HID1, HID1)], start=(k == 0), stop=(k == 1))
                mm.then_inc(hid_ps, 1)

            def turn_hidden(s, j):
                pe.wait_ge(hid_relu, s + 3)
                pe.wait_ge(hid_copied, s + 1)
                for k in range(4):
                    mm = nc.tensor.transpose(ps[:, 4 + j, k * P:(k + 1) * P],
                                             hid_r[j][:, k * P:(k + 1) * P], ident)
                mm.then_inc(hid_turned, 1)

            def outputs(s, j, e):
                pe.wait_ge(hid_copied, s + 3)
                pe.wait_ge(y_biased, s + 1)
                for k in range(4):
                    mm = nc.tensor.matmul(ps[:, 6 + j, 0:D], hid_rT[j][:, k, :],
                                          w2s[:, ds(e * 4 + k, 1), :].rearrange("p o d -> p (o d)"),
                                          start=(k == 0), stop=(k == 3))
                mm.then_inc(y_ps, 1)

            loaded = {}

            def pe_tile(i, u, last=False):
                s, j, r = tile(i, u)
                first = isinstance(i, int) and i == 0 and u == -2
                alone = first or u == 0
                e = expert_of(s) if alone else loaded["this"]
                if not first:
                    before = expert_of(s - 1) if alone else loaded["before"]
                hidden(s, j, e)
                if not last:
                    turn_x(i, u + 1)
                if not first:
                    outputs(s - 1, 1 - j, before)
                if u not in (-1, 3):
                    loaded["this"], loaded["before"] = expert_of(s + 1), e
                turn_hidden(s, j)

            pe.sem_inc(hid_ps, 2)
            pe.sem_inc(hid_turned, 2)
            pe.sem_inc(y_ps, 2)
            pe.wait_ge(rows_copied, TT)
            pe.wait_ge(tiles_ready, 1)
            pe.wait_ge(ffn1_in, 32)
            turn_x(0, -2)
            slot_tiles(pe, pe_tile)
            outputs(ST - 1, 1, expert_of(ST - 1))

        @block.scalar
        def _(act):
            act.wait_ge(small_in, 16)
            ln = LNS["scan"]
            nc.scalar.preload_act_table_set("natural_log_exp_and_others")
            act_norm_start(act, ln)
            act.sem_inc(up_right, 1)
            act.wait_ge(consts_set, 3)

            def act_embed(k, j, on):
                if on(1):
                    act_square(act, ln, k - 1, 1 - j)
                if on(2):
                    c = k - 2
                    act.wait_ge(up_ps, c + 1)
                    nc.scalar.activation(leftp[:, ds(c * IC, IC), 2:L + 2],
                                         ps[:, 6, 0:CH].rearrange("p (i l) -> p i l", i=IC),
                                         ACT.Identity, bias=S("b_up")[:, 0:1]).then_inc(up_left, 1)
                    nc.scalar.activation(sright[:, ds(c * CH, CH)], ps[:, 7, 0:CH], ACT.Identity,
                                         bias=S("b_up")[:, 1:2]).then_inc(up_right, 1)
                if on(1):
                    act_rstd(act, ln, k - 1, 1 - j, 5)

            staged(act, act_embed, 2)
            nc.scalar.preload_act_table(ACT.Silu)

            def act_silu(k, j, on):
                if on(0):
                    act.wait_ge(conv_step, k * 3 + 3)
                    nc.scalar.activation(xs[:, ds(k * CH, CH)], cvF[:, ds(k * CH, CH)],
                                         ACT.Silu).then_inc(x_ready, 1)
                if on(1):
                    c = k - 1
                    act.wait_ge(zbc_ps, c + 1)
                    nc.scalar.activation(dz[:, ds(c * CH, CH)], ps[:, 1 - j, 0:CH], ACT.Identity,
                                         bias=S("b_delta")).then_inc(z_copied, 1)
                    nc.scalar.activation(bcv[:, ds(c * CH, CH)], ps[:, 3 - j, 0:CH], ACT.Identity,
                                         bias=S("b_bc")).then_inc(bc_copied, 1)
                if on(0):
                    nc.scalar.activation(sright[:, ds(k * CH, CH)], sright[:, ds(k * CH, CH)],
                                         ACT.Silu).then_inc(right_ready, 1)

            act.wait_ge(up_right, NCH + 1)
            act.sem_inc(z_copied, 2)
            act.sem_inc(bc_copied, 2)
            staged(act, act_silu, 1)
            nc.scalar.preload_act_table_set("natural_log_exp_and_others")
            nc.scalar.activation(aneg[:], S("a_log"), ACT.Exp).then_inc(a_exp, 1)
            act.wait_ge(z_copied, NCH + 2)
            for q in range(NQ):
                qs = slice(q * QT, (q + 1) * QT)
                act.wait_ge(soft_abs, q + 1)
                nc.scalar.activation(delta[:, qs], delta[:, qs], ACT.Exp).then_inc(soft_step, 1)
                act.wait_ge(soft_step, 2 * q + 1)
                nc.scalar.activation(delta[:, qs], delta[:, qs], ACT.Ln, bias=1.0).then_inc(soft_step, 1)

            act.sem_inc(b_copied, 1)
            act.wait_ge(delta_ready, NQ)
            act.wait_ge(a_ready, 2)
            with act.Fori(0, NQ) as q:
                with act.Fori(0, N // 2) as i:
                    for j in range(2):
                        k = q * N + i * 2 + j
                        act.wait_ge(b_bcast, k + 1)
                        act.wait_ge(injected, k + 1)
                        nc.scalar.activation(bsb[j].rearrange("p (h t) -> p h t", h=2),
                                             ps[:, 2:4, 0:CH], ACT.Copy).then_inc(b_copied, 1)
                        act.wait_ge(scanned, k + 1)
                        nc.scalar.activation(decay[j][:, :, 1:L],
                                             delta.rearrange("p (i l) -> p i l", i=NI)[:, ds(q * QI, QI), 1:L],
                                             ACT.Exp, scale=aneg[:, ds(i + j * 32, 1)]).then_inc(decayed, 1)

            ln = LNS["moe0"]
            act_norm_start(act, ln)

            def act_down(k, j, on):
                if on(1):
                    act_square(act, ln, k - 1, 1 - j)
                if on(2):
                    act_rstd(act, ln, k - 2, j, 6 + j)
                if on(3):
                    act_logits(act, MOE["moe0"], k - 3, 1)

            staged(act, act_down, 3)
            act_exp(act, MOE["moe0"]["lg"], MOE["moe0"]["exp"], -1.0)
            act_norm_start(act, LNS["attn"])
            act_shared(act, MOE["moe0"])
            for b in (1, 2, 3):
                copy_weights(act, nc.scalar.copy, MOE["moe0"], b, MOE["moe0"]["cwT"])
            act_moe(act, MOE["moe0"], LNS["attn"], 12)

            act.sem_inc(p_copied, 1)
            act.sem_inc(o_copied, 1)

            def act_compress(c, cj):
                act.wait_ge(cc_ps, c + 1)
                nc.scalar.activation(cc, ps[:, 6, 0:CH], ACT.Copy).then_inc(cc_copied, 1)
                act.wait_ge(cc_copied, c + 1)
                nc.scalar.activation(ckv3[cj][64:128],
                                     bc(cc[64:128, :].rearrange("p (i l) -> p i l", i=IC), 2, KG),
                                     ACT.Copy).then_inc(ckv_rep, 1)

            def act_queries(c, cj):
                act.wait_ge(q_ps, c + 1)
                nc.scalar.activation(qT[cj], ps[:, 6:8, 0:CH], ACT.Copy,
                                     scale=DK ** -0.5).then_inc(q_copied, 1)

            def act_keys(c, cj):
                act.wait_ge(k_ps, c + 1)
                nc.scalar.activation(kT[cj], ps[:, 6:8, 0:CH], ACT.Copy).then_inc(k_copied, 1)

            def act_exp_scores(c, cj, p):
                k = c * 4 + p
                act.wait_ge(shifted, k + 1)
                pr = prob[p % 2][0:QR]
                nc.scalar.activation(pr, pr, ACT.Exp).then_inc(exped, 1)

            def act_first():
                act.wait_ge(MOE["moe0"]["h"], NCH + 2)
                act_compress(0, 0)
                act_square(act, LNS["attn"], NCH - 1, 1)
                act_queries(0, 0)
                act_rstd(act, LNS["attn"], NCH - 1, 1, 0)
                act_keys(0, 0)
                act_compress(1, 1)
                act_exp_scores(0, 0, 0)

            def act_step(c, cj, p, more2, more1):
                k = c * 4 + p
                act.wait_ge(p_turned, k + 3)
                act.wait_ge(o_ps, k + 2)
                nc.scalar.activation(probT[0:KG * L].rearrange("p a c q -> p a (c q)"),
                                     ps[0:KG * L, 2:4, 0:KG * QR], ACT.Copy).then_inc(p_copied, 1)
                if more1 and p == 1:
                    act_keys(c + 1, 1 - cj)
                if more1 or p < 3:
                    act_exp_scores(*ahead(c, cj, p, 1))
                if more1 and p == 0:
                    act_queries(c + 1, 1 - cj)
                act.wait_ge(o_turned, k + 3)
                if p == 0:
                    act.wait_ge(wo_ps, c + 1)
                o = ps[:, 5, O_T:O_T + 2 * QR].rearrange("p (a q) -> p a q", a=2)
                dst = oT[cj].rearrange("p a (i q) -> p a i q", i=IC)
                nc.scalar.activation(dst[:, :, 2 * p, :], o[:, :, 0:L], ACT.Copy)
                nc.scalar.activation(dst[:, :, 2 * p + 1, :], o[:, :, 64:QR],
                                     ACT.Copy).then_inc(o_copied, 1)
                if p == 3 and not (isinstance(c, int) and c == 0):
                    act_rstd(act, ln, c - 1, 1 - cj, 7)
                if p == 2 and not (isinstance(c, int) and c == 0):
                    act_square(act, ln, c - 1, 1 - cj)
                if p == 2 and not (isinstance(c, int) and c < 2):
                    act_logits(act, MOE["moe1"], c - 2, 6)
                if more2 and p == 3:
                    act_compress(c + 2, cj)

            def act_last():
                act_logits(act, MOE["moe1"], NCH - 2, 6)
                act_square(act, ln, NCH - 1, 1)
                act_rstd(act, ln, NCH - 1, 1, 7)
                act_logits(act, MOE["moe1"], NCH - 1, 6)

            ln = LNS["moe1"]
            act_norm_start(act, ln)
            attention(act, act_first, act_step, act_last)

            act_exp(act, lg1, exp1, 1.0)
            for t in range(TT):
                n = min(P, T - t * P)
                act.wait_ge(rows_ps, t + 1)
                if t >= NR:
                    act.wait_ge(rows_out[t % NR], 16 * (t // NR))
                nc.scalar.activation(token_row[t % NR][0:n, 0:2 * D], ps[0:n, 3 + t % 2, :],
                                     ACT.Copy).then_inc(rows_copied, 1)
            act.sem_inc(x_copied, 2)
            act.sem_inc(hid_relu, 2)
            act.sem_inc(hid_copied, 2)
            def act_x(s, j):
                act.wait_ge(x_turned, s + 1)
                act.wait_ge(hid_ps, s + 1)
                nc.scalar.activation(slot_xT[j].rearrange("p k n -> p (k n)"), ps[:, j, 0:D],
                                     ACT.Copy).then_inc(x_copied, 1)

            def act_relu(s, j):
                act.wait_ge(hid_biased, s + 3)
                act.wait_ge(hid_turned, s + 1)
                nc.scalar.activation(hid_r[j], hid_b[j], ACT.Relu).then_inc(hid_relu, 1)

            def act_hidden(s, j):
                act.wait_ge(hid_turned, s + 3)
                act.wait_ge(y_ps, s + 1)
                nc.scalar.activation(hid_rT[j].rearrange("p k n -> p (k n)"), ps[:, 4 + j, :],
                                     ACT.Copy).then_inc(hid_copied, 1)

            act_x(0, 0)
            with act.Fori(0, ST // 2 - 1) as i:
                for j in range(2):
                    s = i * 2 + j
                    act_x(s + 1, 1 - j)
                    act_relu(s, j)
                    act_hidden(s, j)
            act_x(ST - 1, 1)
            for j in range(2):
                act_relu(ST - 2 + j, j)
                act_hidden(ST - 2 + j, j)

        @block.vector
        def _(dve):
            linked = [0]
            chain = sem("dve_chain")

            def link(ins):
                linked[0] += 1
                ins.then_inc(chain, 1)
                dve.wait_ge(chain, linked[0])

            dve.wait_ge(small_in, 16)
            for m in range(HALVES):
                pos = S("pos").rearrange("p (a l) -> p a l", a=2)[:, m, :]
                nc.vector.tensor_scalar(posb[:, m, 1:L], pos[:, 1:L], S("b_lin")[:, m:m + 1], None,
                                        ALU.add).then_inc(pos_ready, 1)
                nc.vector.tensor_tensor(posb[:, m, 0:1], pos[:, 0:1], S("cls")[:, m:m + 1],
                                        ALU.add).then_inc(pos_ready, 1)
            dve.wait_ge(pos_ready, 4)
            for m in range(HALVES):
                nc.vector.tensor_copy(hT[:, m, :, 0], posb[:, m, 0:1].broadcast_to([P, NI])
                                      ).then_inc(pos_ready, 1)
            dve.sem_inc(embedded, 4)
            ln = LNS["scan"]
            dve_norm_start(dve, ln)
            w = S("conv_w")

            def dve_embed(k, j, on):
                if on(1):
                    dve_center(dve, ln, k - 1, 4)
                if on(0):
                    dve.wait_ge(embedded_ps, k + 1)
                    for m in range(HALVES):
                        nc.vector.tensor_tensor(hT[:, m, ds(k * IC, IC), 1:L],
                                                ps[:, 2 * j + m, 0:IC * NP].rearrange("p (i l) -> p i l", i=IC),
                                                bc(posb[:, m, 1:L], 1, IC), ALU.add).then_inc(embedded, 1)
                if on(1):
                    dve_scale(dve, ln, k - 1, 1 - j)
                if on(2):
                    c = k - 2
                    images = ds(c * IC, IC)
                    dve.wait_ge(up_left, c + 1)
                    nc.vector.tensor_scalar(cv[:, images, :], leftp[:, images, 0:L], w[:, 0:1],
                                            S("conv_b"), ALU.mult, ALU.add).then_inc(conv_step, 1)
                    for s_ in (1, 2):
                        dve.wait_ge(conv_step, c * 3 + s_)
                        nc.vector.scalar_tensor_tensor(out=cv[:, images, :], in0=leftp[:, images, s_:L + s_],
                                                       scalar=w[:, s_:s_ + 1], in1=cv[:, images, :],
                                                       op0=ALU.mult, op1=ALU.add).then_inc(conv_step, 1)

            staged(dve, dve_embed, 2)
            done = 0
            for q in range(NQ):
                mine = [c for c in DVE_SPLIT if c * NQ // NCH == q]
                split_chunks(dve, nc.vector, split_step, mine, done)
                done += len(mine)
                qs = slice(q * QT, (q + 1) * QT)
                dve.wait_ge(z_copied, (q + 1) * NCH // NQ + 2)
                nc.vector.scalar_tensor_tensor(out=delta[:, qs], in0=dz[:, qs], scalar=-1.0,
                                               in1=dz[:, qs], op0=ALU.mult,
                                               op1=ALU.min).then_inc(soft_abs, 1)
            dve.wait_ge(a_exp, 1)
            nc.vector.tensor_scalar(aneg[:], aneg[:], -1.0, None, ALU.mult).then_inc(a_ready, 1)
            nc.vector.tensor_scalar(diag_d[:], ident, S("d_skip"), None, ALU.mult).then_inc(a_ready, 1)
            for q in range(NQ):
                qs = slice(q * QT, (q + 1) * QT)
                dve.wait_ge(soft_step, 2 * q + 2)
                nc.vector.scalar_tensor_tensor(out=delta[:, qs], in0=dz[:, qs], scalar=0.0,
                                               in1=delta[:, qs], op0=ALU.max,
                                               op1=ALU.add).then_inc(delta_ready, 1)
                dve.wait_ge(delta_ready, q + 1)
                dve.wait_ge(x_ready, NCH)
                nc.vector.tensor_tensor(dx[:, qs], delta[:, qs], xs[:, qs], ALU.mult).then_inc(dx_ready, 1)

            dve.sem_inc(scanned, 2)
            dve.sem_inc(read_out, 2)
            dve.sem_inc(y_gated, 1)

            def scan_state(q, i, j):
                k = q * N + i * 2 + j
                dve.wait_ge(decayed, k + 1)
                dve.wait_ge(injected, k + 3)
                dve.wait_ge(read_out, k + 1)
                nc.vector.tensor_tensor_scan(state[j], decay[j].rearrange("p i l -> p (i l)"),
                                             inject[j], 0.0, ALU.mult, ALU.add).then_inc(scanned, 1)

            def read_state(q, i, j):
                k = q * N + i * 2 + j
                dve.wait_ge(scanned, k + 3)
                dve.wait_ge(c_bcast, k + 1)
                dve.wait_ge(summed, k + 1)
                nc.vector.tensor_tensor(read[j].rearrange("p (h t) -> p h t", h=2),
                                        state[j].rearrange("p (h t) -> p h t", h=2),
                                        ps[:, 4 + 2 * j:6 + 2 * j, 0:CH],
                                        ALU.mult).then_inc(read_out, 1)

            def gate_part(q):
                dve.wait_ge(summed, q * N + N + 2)
                dve.wait_ge(right_ready, NCH)
                qs = slice(q * QT, (q + 1) * QT)
                nc.vector.tensor_tensor(gated[:, qs].rearrange("p (h t) -> p h t", h=2),
                                        ps[:, 0:2, 0:CH],
                                        sright[:, qs].rearrange("p (h t) -> p h t", h=2),
                                        ALU.mult).then_inc(y_gated, 1)

            for q in range(NQ):
                scan_state(q, 0, 0)
                read_state(q, 0, 0)
                scan_state(q, 0, 1)
                if q > 0:
                    gate_part(q - 1)
                read_state(q, 0, 1)
                with dve.Fori(1, N // 2) as i:
                    for j in range(2):
                        scan_state(q, i, j)
                        read_state(q, i, j)
            gate_part(NQ - 1)
            dve.sem_inc(scan_h, 2)
            ln = LNS["moe0"]
            dve_norm_start(dve, ln)

            def dve_down(k, j, on):
                if on(0):
                    cs = ds(k * CH, CH)
                    dve.wait_ge(down_ps, k + 1)
                    for m in range(2):
                        mm = nc.vector.scalar_tensor_tensor(
                            out=hF[:, m, cs], in0=ps[:, 2 + 2 * j + m, 0:CH],
                            scalar=S("b_down")[:, m:m + 1], in1=hF[:, m, cs], op0=ALU.add, op1=ALU.add)
                    mm.then_inc(scan_h, 1)
                if on(1):
                    dve_center(dve, ln, k - 1, 0)
                if on(2):
                    dve_scale(dve, ln, k - 2, j)

            staged(dve, dve_down, 3)

            s = MOE["moe0"]
            dve.wait_ge(s["logits_turned"], 1)
            lgp = ps[:, 0, 0:TT * E8].rearrange("p (t e) -> p t e", t=TT)
            nc.vector.tensor_copy(lg[:], lgp).then_inc(s["lg"], 1)
            dve.wait_ge(s["exp"], 1)
            link(nc.vector.tensor_scalar(sc[:], sc[:], 1.0, None, ALU.add))
            link(nc.vector.reciprocal(sc[:], sc[:]))
            link(nc.vector.tensor_tensor(rt2[:], sc[:], bc(S("gate_b"), 1, TT), ALU.add))
            g4 = rt2[:].rearrange("p t (g e) -> p t g e", g=2)
            link(nc.vector.tensor_tensor(pairs[:, :, :, 0:3], g4[:, :, :, 0:3], g4[:, :, :, 1:4], ALU.add))
            link(nc.vector.tensor_tensor(pairs[:, :, :, 3:5], g4[:, :, :, 0:2], g4[:, :, :, 2:4], ALU.add))
            link(nc.vector.tensor_tensor(pairs[:, :, :, 5:6], g4[:, :, :, 0:1], g4[:, :, :, 3:4], ALU.add))
            link(nc.vector.tensor_reduce(gsum[:], pairs[:], AX, ALU.max))
            link(nc.vector.tensor_tensor(gsel[:, :, 0:1], gsum[:, :, 0:1], gsum[:, :, 1:2], ALU.is_ge))
            link(nc.vector.tensor_scalar(gsel[:, :, 1:2], gsel[:, :, 0:1], -1.0, 1.0, ALU.mult, ALU.add))
            link(nc.vector.tensor_tensor(g4, g4, bc(gsel[:], 3, 4), ALU.mult))
            dve_first_max(link, rt2[:], lg[:], rt1[:])
            link(nc.vector.scalar_tensor_tensor(out=rt2[:], in0=rt1[:], scalar=-1e30, in1=rt2[:],
                                                op0=ALU.mult, op1=ALU.add))
            dve_first_max(link, rt2[:], lg[:], rt2b[:])
            link(nc.vector.tensor_tensor(rt1[:], rt1[:], rt2b[:], ALU.add))
            link(nc.vector.tensor_tensor(rt1[:], rt1[:], sc[:], ALU.mult))
            link(nc.vector.tensor_reduce(red[:], rt1[:], AX, ALU.add))
            link(nc.vector.tensor_scalar(red[:], red[:], 1e-20, None, ALU.add))
            link(nc.vector.reciprocal(red[:], red[:]))
            link(nc.vector.tensor_tensor(rt1[:], rt1[:], bc(red[:], 2, E8), ALU.mult))
            nc.vector.tensor_scalar(rt1[:], rt1[:], 2.5, None, ALU.mult).then_inc(s["route"], 1)
            copy_weights(dve, nc.vector.tensor_copy, s, 0, s["cwT_first"])
            copy_weights(dve, nc.vector.tensor_copy, s, 4, s["cwT"])
            dve_norm_start(dve, LNS["attn"])
            dve_moe(dve, s, LNS["attn"], 12)

            dve.sem_inc(masked, 1)
            dve.sem_inc(v_spread, 1)
            head_of = S("v_mask")[0:KG * L]
            for n in range(2):
                nc.vector.tensor_copy(
                    vm[n][0:KG * L].rearrange("p i b d -> p (i b) d")[:, :, KG * DK:VB],
                    bc(head_of[:, KG * DK:VB], 1, 4 * KG)).then_inc(vm_ones, 1)

            def soften(c, cj, p):
                k = c * 4 + p
                pr = prob[p % 2][0:QR]
                dve.wait_ge(scores_ps, k + 3)
                dve.wait_ge(p_turned, k + 1)
                nc.vector.tensor_tensor(pr.rearrange("p (a h) l -> p a h l", a=2),
                                        ps[0:QR, 0:2, 0:8 * L].rearrange("p a (h l) -> p a h l", h=8),
                                        bc(bc(S("causal")[0:QR], 1, 8), 1, 2),
                                        ALU.add).then_inc(masked, 1)
                dve.wait_ge(masked, k + 2)
                nc.vector.tensor_reduce(rowm[0:QR, p % 2, :], pr, AX, ALU.max).then_inc(maxed, 1)
                dve.wait_ge(maxed, k + 1)
                nc.vector.tensor_tensor(pr, pr, bc(rowm[0:QR, p % 2, :], 2, L),
                                        ALU.subtract).then_inc(shifted, 1)

            def spread_values(c, cj, p):
                k = c * 4 + p
                dve.wait_ge(v_ps, k + 1)
                dve.wait_ge(o_ps, k + 1)
                v = ps[0:KG * L, 4, 0:2 * D].rearrange("p (x d) -> p x d", x=4)
                o = vm[p % 2][0:KG * L].rearrange("p i (a b) d -> p (i a) b d", a=2)
                w3 = KG * DK
                nc.vector.tensor_tensor(o[:, :, 0:2, 0:w3],
                                        v[:, :, 0:2 * w3].rearrange("p x (b d) -> p x b d", b=2),
                                        bc(bc(head_of[:, 0:w3], 1, 2), 1, 4), ALU.mult)
                nc.vector.tensor_tensor(o[:, :, 2, 0:w3], v[:, :, P - w3:P],
                                        bc(head_of[:, 0:w3], 1, 4), ALU.mult).then_inc(v_spread, 1)

            def scale_outputs(c, cj, p):
                k = c * 4 + p
                dve.wait_ge(o_ps, k + 3)
                o = ps[0:QR, 5, 0:2 * KG * VB].rearrange("p (x d) -> p x d", x=2 * KG)
                nc.vector.reciprocal(rows[0:QR], o[:, :, KG * DK:VB]).then_inc(inverted, 1)
                dve.wait_ge(inverted, k + 1)
                dve.wait_ge(o_turned, k + 1)
                o = o[:, :, 0:KG * DK].rearrange("p (a b) (h d) -> p a b h d", a=2, h=KG)
                inv = rows[0:QR].rearrange("p (a b) h -> p a b h", a=2)
                for b in range(KG):
                    h0 = min(KG * b, 8 - KG)
                    skip = KG * b - h0
                    ins = nc.vector.tensor_tensor(osb[p % 2][0:QR, :, KG * b:h0 + KG, :],
                                                  o[:, :, b, skip:KG, :],
                                                  bc(inv[:, :, b, skip:KG], 3, DK), ALU.mult)
                ins.then_inc(o_scaled, 1)

            def add_projected(c):
                dve.wait_ge(wo_ps, c + 3)
                nc.vector.tensor_tensor(hF[:, :, ds(c * CH, CH)], hF[:, :, ds(c * CH, CH)],
                                        ps[:, 6:8, 0:CH], ALU.add).then_inc(attn_h, 1)

            def dve_first():
                soften(0, 0, 0)
                spread_values(0, 0, 0)

            def dve_step(c, cj, p, more2, more1):
                if more1 or p < 3:
                    soften(*ahead(c, cj, p, 1))
                scale_outputs(c, cj, p)
                if more1 or p < 3:
                    spread_values(*ahead(c, cj, p, 1))
                if p == 1 and not (isinstance(c, int) and c == 0):
                    add_projected(c - 1)
                if p == 2 and not (isinstance(c, int) and c == 0):
                    dve_center(dve, ln, c - 1, 7)
                if p == 0 and not (isinstance(c, int) and c < 2):
                    dve_scale(dve, ln, c - 2, cj)

            def dve_last():
                dve_scale(dve, ln, NCH - 2, 0)
                add_projected(NCH - 1)
                dve_center(dve, ln, NCH - 1, 7)
                dve_scale(dve, ln, NCH - 1, 1)

            ln = LNS["moe1"]
            dve_norm_start(dve, ln)
            attention(dve, dve_first, dve_step, dve_last)

            dve.wait_ge(MOE["moe1"]["logits_turned"], 1)
            link(nc.vector.tensor_tensor(lg[:], lgp, bc(S("b_r"), 1, TT), ALU.add))
            dve_first_max(link, lg[:], rt2[:], rt1[:])
            nc.vector.tensor_tensor(rt1[:], rt1[:], bc(S("real"), 2, E8), ALU.mult).then_inc(chosen, 1)
            link(nc.vector.tensor_reduce(red[:], lg[:], AX, ALU.max))
            nc.vector.tensor_tensor(lg[:], lg[:], bc(red[:], 2, E8), ALU.subtract).then_inc(lg1, 1)
            dve.wait_ge(exp1, 1)
            link(nc.vector.tensor_reduce(red[:], sc[:], AX, ALU.add))
            link(nc.vector.reciprocal(red[:], red[:]))
            link(nc.vector.tensor_tensor(sc[:], sc[:], bc(red[:], 2, E8), ALU.mult))
            dve.wait_ge(chosen, 1)
            link(nc.vector.tensor_tensor(rt2[:], rt1[:], sc[:], ALU.mult))
            link(nc.vector.tensor_reduce(gate[:], rt2[:], AX, ALU.add))
            dve.wait_ge(counted, 1)
            totF, runF = tot[:].rearrange("p e t -> p (e t)"), run[:].rearrange("p e t -> p (e t)")
            link(nc.vector.tensor_scalar(tot[:], ps[:, 2, 0:TT * E8].rearrange("p (t e) -> p e t", t=TT),
                                         float(D), None, ALU.mult))
            link(nc.vector.tensor_tensor_scan(runF, S("not_first"), totF, 0.0, ALU.mult, ALU.add))
            full = spare[:, 0:E8 * TT].rearrange("p (e t) -> p e t", e=E8)
            link(nc.vector.tensor_tensor(full, bc(run[:, :, TT - 1], 2, TT), bc(S("tile_ends"), 1, E8),
                                         ALU.is_gt))
            link(nc.vector.tensor_reduce(ntile[:, 0, :], full, AX, ALU.add))
            link(nc.vector.tensor_tensor_scan(ntile[:, 1, :], S("one8"), ntile[:, 0, :], 0.0, ALU.mult,
                                              ALU.add))
            link(nc.vector.tensor_tensor(ntile[:, 2, :], ntile[:, 1, :], ntile[:, 0, :], ALU.subtract))
            link(nc.vector.tensor_tensor(run[:], run[:], tot[:], ALU.subtract))
            link(nc.vector.tensor_scalar(ntile[:, 2, :], ntile[:, 2, :], float(P), None, ALU.mult))
            link(nc.vector.tensor_tensor(run[:], run[:], bc(ntile[:, 2, :], 2, TT), ALU.add))
            link(nc.vector.tensor_tensor(rt2[:], run[:].rearrange("p e t -> p t e"),
                                         ps[:, 1, 0:TT * E8].rearrange("p (t e) -> p t e", t=TT), ALU.add))
            link(nc.vector.tensor_tensor(rt2[:], rt2[:], rt1[:], ALU.mult))
            link(nc.vector.tensor_reduce(slot_f[:], rt2[:], AX, ALU.add))
            nc.vector.tensor_copy(slot_i[:], slot_f[:]).then_inc(slot_ready, 1)
            dve.wait_ge(token_set, 1)
            for t in range(NR):
                nc.vector.tensor_copy(token_row[t % NR][:, 2 * D:2 * D + 1], gate[:, t:t + 1])
                nc.vector.tensor_copy(token_row[t % NR][:, ROW - 1:ROW].bitcast(I32),
                                      token[:, t:t + 1]).then_inc(rows_tagged, 1)
            owner = spare.rearrange("p (s e) -> p s e", s=ST)
            link(nc.vector.tensor_tensor(owner, bc(S("slot_tile"), 2, E8), bc(ntile[:, 1, :], 1, ST),
                                         ALU.is_ge))
            link(nc.vector.tensor_reduce(spare2, owner, AX, ALU.add))
            link(nc.vector.tensor_scalar(spare2, spare2, float(E8 - 1), None, ALU.min))
            nc.vector.tensor_copy(expert_i[:], spare2).then_inc(tiles_ready, 1)
            for t in range(NR, TT):
                dve.wait_ge(rows_out[t % NR], 16 * (t // NR))
                nc.vector.tensor_copy(token_row[t % NR][:, 2 * D:2 * D + 1], gate[:, t:t + 1])
                nc.vector.tensor_copy(token_row[t % NR][:, ROW - 1:ROW].bitcast(I32),
                                      token[:, t:t + 1]).then_inc(rows_tagged, 1)
            dve.sem_inc(hid_biased, 2)
            dve.sem_inc(y_biased, 2)
            dve.sem_inc(y_ready, 4)
            dve.wait_ge(tiles_ready, 1)
            dve.wait_ge(bias_in, 32)

            def bias_hidden(s, j):
                e = dve.value_load(expert_i[0:1, ds(s, 1)], min_val=0, max_val=E8 - 1)
                dve.wait_ge(hid_ps, s + 3)
                dve.wait_ge(hid_relu, s + 1)
                nc.vector.tensor_tensor(hid_b[j], ps[:, 2 + j, :], b1r[:, ds(e * HID1, HID1)],
                                        ALU.add).then_inc(hid_biased, 1)

            def finish_rows(i, u):
                s, j, r = tile(i, u)
                e = dve.value_load(expert_i[0:1, ds(s, 1)], min_val=0, max_val=E8 - 1)
                dve.wait_ge(y_ps, s + 3)
                if not (isinstance(i, int) and half(i, u) == 0):
                    dve.wait_ge(y_out[j], half(i, u) * 16)
                nc.vector.tensor_tensor(out_row[j], ps[:, 6 + j, 0:D], b2r[:, ds(e * D, D)],
                                        ALU.add).then_inc(y_biased, 1)
                nc.vector.tensor_copy(slot_token[:, ds(s, 1)],
                                      slot_row[r][:, ROW - 1:ROW].bitcast(I32))
                dve.wait_ge(y_biased, s + 3)
                nc.vector.scalar_tensor_tensor(out=out_row[j], in0=out_row[j],
                                               scalar=slot_row[r][:, 2 * D:2 * D + 1],
                                               in1=slot_row[r][:, 0:D], op0=ALU.mult,
                                               op1=ALU.add).then_inc(y_ready, 1)

            def dve_tile(i, u, last=False):
                s, j, r = tile(i, u)
                bias_hidden(s, j)
                if not (isinstance(i, int) and i == 0 and u == -2):
                    finish_rows(i, u - 1)

            slot_tiles(dve, dve_tile)
            finish_rows(ST // 4 - 1, 3)


def kernel(**inputs):
    import numpy as np
    import concourse.bacc as bacc
    from concourse.bass_utils import run_bass_kernel_spmd

    g = {k: np.asarray(v) for k, v in inputs.items()}

    def rows(a, k):
        return np.ascontiguousarray(a.reshape(k, P, -1).transpose(1, 0, 2))

    def cols(v):
        return v.reshape(-1, P).T

    x = g["x"].reshape(NCH, IC, 3, 6, 16, 6, 16).transpose(0, 2, 4, 6, 1, 3, 5)
    x = x.reshape(NCH, FK, P, IC * NP).transpose(0, 2, 1, 3)

    row = np.arange(P)
    eye = np.eye(P, dtype=np.float32)

    def every(v):
        return np.tile(v.astype(np.float32)[None], (P, 1))

    head_of_row = (row[:, None] // DK == np.arange(E8)[None]).astype(np.float32)
    of = np.concatenate([np.arange(KG * DK) // DK, np.arange(KG)])
    v_mask = (np.minimum(row // L, KG)[:, None] == of[None]).astype(np.float32)
    causal = np.where(np.arange(L)[None] <= (row % 64)[:, None], 0.0, -1e30).astype(np.float32)
    row32 = (row[:, None] % 32 == np.arange(32)[None]).astype(np.float32)
    pieces = {
        "pos": rows(g["L0_tok_position_embeddings"][0].T, 2).reshape(P, -1),
        "b_lin": cols(g["L0_tok_b_lin"]), "cls": cols(g["L0_tok_class_token"].reshape(-1)),
        "b_up": cols(g["L0_attn_b_up"]), "conv_w": g["L0_attn_conv_w"],
        "conv_b": cols(g["L0_attn_conv_b"]), "b_delta": cols(g["L0_attn_b_delta"]),
        "b_bc": cols(np.concatenate([g["L0_attn_b_B"], g["L0_attn_b_C"]])),
        "a_log": g["L0_attn_A_log"], "d_skip": cols(g["L0_attn_D_skip"]),
        "b_down": cols(g["L0_attn_b_down"]),
        "gate_b": np.broadcast_to(g["L0_ffn_gate_bias"][None], (P, E8)),
        "b_r": np.broadcast_to(g["L1_ffn_br"][None], (P, E8)),
        "ident": eye, "head_of_row": head_of_row,
        "v_mask": v_mask, "causal": causal, "rank": every(E8 - np.arange(E8)), "row32": row32,
        "eps": np.full((P, 1), EPS, np.float32),
        "before": (row[:, None] < row[None]).astype(np.float32),
        "not_first": every(np.arange(E8 * TT) % TT > 0), "tile_ends": every(np.arange(TT) * P),
        "one8": every(np.ones(E8)), "slot_tile": every(np.arange(ST)),
        "real": (np.arange(TT)[None] * P + row[:, None] < T).astype(np.float32),
    }
    for n, w in SMALL:
        assert pieces[n].shape == (P, w), (n, pieces[n].shape)
    zero = np.zeros((64, D), np.float32)
    dense = {
        "w_up": rows(g["L0_attn_W_up"], 2), "w_delta": g["L0_attn_W_delta"],
        "w_bc": np.concatenate([g["L0_attn_W_B"], g["L0_attn_W_C"]], axis=1),
        "w_down": g["L0_attn_W_down"], "gate_w": rows(g["L0_ffn_gate_weight"].T, 2),
        "w_dqkv": rows(np.concatenate([g["L1_attn_W_dq"], g["L1_attn_W_dkv"]], axis=1), 2),
        "w_u": np.concatenate([np.concatenate([g["L1_attn_W_uq"], zero], axis=1),
                               np.concatenate([g["L1_attn_W_uk"], g["L1_attn_W_uv"]], axis=1)]),
        "w_o": rows(g["L1_attn_W_o"], 2), "w_r": rows(g["L1_ffn_Wr"], 2),
    }
    arrays = {
        "small": np.concatenate([pieces[n] for n, _ in SMALL], axis=1),
        "dense": np.concatenate([dense[n].reshape(P, -1) for n, _ in DENSE], axis=1),
        "patches": x,
        "w_lin": rows(g["L0_tok_W_lin"].T, FK),
        "up0": rows(np.concatenate([g["L0_ffn_up_weights"].reshape(1024, D), g["L0_ffn_shared_up_weight"]]).T, 2),
        "dn0": np.concatenate([g["L0_ffn_down_weights"].transpose(0, 2, 1),
                               g["L0_ffn_shared_down_weight"].T.reshape(4, P, D)]).transpose(1, 0, 2),
        "w1": rows(g["L1_ffn_W1"].transpose(1, 0, 2).reshape(D, -1), 2),
        "w2": g["L1_ffn_W2"].reshape(32, P, D).transpose(1, 0, 2),
        "b1": g["L1_ffn_b1"].reshape(1, -1), "b2": g["L1_ffn_b2"].reshape(1, -1),
    }
    arrays = {f"in_{k}": np.ascontiguousarray(v) for k, v in arrays.items()}
    nc = bacc.Bacc("TRN2", target_bir_lowering=False, num_devices=1)
    args = [nc.dram_tensor(k, v.shape, F32, kind="ExternalInput").ap() for k, v in arrays.items()]
    gates = nc.dram_tensor("gates", (E8, T), F32, kind="Internal").ap()
    slots = nc.dram_tensor("slots", (ST * P, ROW), F32, kind="Internal").ap()
    res = nc.dram_tensor("out_h", (T, D), F32, kind="ExternalOutput").ap()
    build(nc, *args, gates, slots, res)
    got = run_bass_kernel_spmd(nc, [arrays], core_ids=[0]).results[0]["out_h"]
    return got.reshape(NI, L, D)
```
